# Optimizing a Trainium2 kernel written in Bass

```python
import numpy as np
import jax
import jax.numpy as jnp

def _softmax(x, axis=-1):
    return jax.nn.softmax(x, axis=axis)

def _gelu(x):
    return jax.nn.gelu(x, approximate=True)

def _silu(x):
    return jax.nn.silu(x)

def _sigmoid(x):
    return jax.nn.sigmoid(x)

def _layernorm(x, axis=-1, eps=1e-05):
    m = jnp.mean(x, axis=axis, keepdims=True)
    v = jnp.var(x, axis=axis, keepdims=True)
    return (x - m) / jnp.sqrt(v + eps)

def _scatter_add(tgt, idx, src, axis=0):
    return tgt.at[idx].add(src)

def _segment_sum(src, seg, n):
    return jax.ops.segment_sum(src, seg, n)
kernel_name = 'mk_gnn_preln_d2_gnn_r8_dcfa92'

def setup_inputs(seed: int=0):
    np.random.seed(seed)
    _w = jnp.asarray

    def _rec_inputs():
        import jax
        import jax.numpy as jnp
        _gk = jax.random.key(seed)
        x = -0.0003713 + 1 * jax.random.normal(jax.random.fold_in(_gk, 1), (12500, 128), jnp.float32)
        src = jax.random.randint(jax.random.fold_in(_gk, 2), (200000,), 0, 12500, jnp.int32)
        dst = jax.random.randint(jax.random.fold_in(_gk, 3), (200000,), 0, 12500, jnp.int32)
        _o = jnp.argsort(dst, stable=True)
        src = src[_o]
        dst = dst[_o]
        edge_attr_32 = 0.000189758 + 1.00013 * jax.random.normal(jax.random.fold_in(_gk, 11), (200000, 32), jnp.float32)
        return (x, src, dst, edge_attr_32)
    x, src, dst, edge_attr_32 = _rec_inputs()

    def _L0_gnn_setup():
        import jax, jax.numpy as jnp
        import numpy as np
        N_NODES = 12500
        N_EDGES = 200000
        IN_DIM = 128
        OUT_DIM = 128
        EDGE_DIM = 32
        EPS = 1e-05

        def _layernorm(h, gamma, beta):
            mu = jnp.mean(h, axis=-1, keepdims=True)
            var = jnp.var(h, axis=-1, keepdims=True)
            return (h - mu) * jax.lax.rsqrt(var + EPS) * gamma + beta
        key = jax.random.key(seed)
        ks = jax.random.split(key, 10)
        hid = OUT_DIM * 2
        x = jax.random.normal(ks[0], (N_NODES, IN_DIM), dtype=jnp.float32)
        edge_index = jax.random.randint(ks[1], (2, N_EDGES), 0, N_NODES, dtype=jnp.int64)
        edge_attr = jax.random.normal(ks[2], (N_EDGES, EDGE_DIM), dtype=jnp.float32)
        W1 = jax.random.normal(ks[3], (IN_DIM + EDGE_DIM, hid), dtype=jnp.float32) / np.sqrt(IN_DIM + EDGE_DIM)
        b1 = jnp.zeros((hid,), jnp.float32)
        g1 = jnp.ones((hid,), jnp.float32)
        be1 = jnp.zeros((hid,), jnp.float32)
        W2 = jax.random.normal(ks[4], (hid, OUT_DIM), dtype=jnp.float32) / np.sqrt(hid)
        b2 = jnp.zeros((OUT_DIM,), jnp.float32)
        Wu = jax.random.normal(ks[5], (IN_DIM + OUT_DIM, OUT_DIM), dtype=jnp.float32) / np.sqrt(IN_DIM + OUT_DIM)
        bu = jnp.zeros((OUT_DIM,), jnp.float32)
        gu = jnp.ones((OUT_DIM,), jnp.float32)
        beu = jnp.zeros((OUT_DIM,), jnp.float32)
        return {'x': x, 'edge_index': edge_index, 'edge_attr': edge_attr, 'W1': W1, 'b1': b1, 'g1': g1, 'be1': be1, 'W2': W2, 'b2': b2, 'Wu': Wu, 'bu': bu, 'gu': gu, 'beu': beu}
    _L0_gnn_all = _L0_gnn_setup()
    _L0_gnn_in = {k: v for k, v in _L0_gnn_all.items() if k in ('W1', 'b1', 'g1', 'be1', 'W2', 'b2', 'Wu', 'bu', 'gu', 'beu')}
    del _L0_gnn_all

    def _L1_gnn_setup():
        import jax, jax.numpy as jnp
        import numpy as np
        from jax.ops import segment_sum
        N = 12500
        M = 2500
        E = 200000
        D_IN = 128
        D_OUT = 128
        key = jax.random.key(seed)
        k1, k2, k3, k4, k5, k6 = jax.random.split(key, 6)
        x = jax.random.normal(k1, (N, D_IN), dtype=jnp.float32)
        node_idx = jax.random.randint(k2, (E,), 0, N)
        he_idx = jax.random.randint(k3, (E,), 0, M)
        hyperedge_index = jnp.stack([node_idx, he_idx], axis=0)
        hyperedge_weight = jax.random.uniform(k4, (M,), dtype=jnp.float32)
        W = jax.random.normal(k5, (D_OUT, D_IN), dtype=jnp.float32) / np.sqrt(D_IN)
        b = jax.random.normal(k6, (D_OUT,), dtype=jnp.float32) * 0.01
        return {'x': x, 'hyperedge_index': hyperedge_index, 'hyperedge_weight': hyperedge_weight, 'W': W, 'b': b}
    _L1_gnn_all = _L1_gnn_setup()
    _L1_gnn_in = {k: v for k, v in _L1_gnn_all.items() if k in ('hyperedge_weight', 'W', 'b')}
    del _L1_gnn_all
    return {'x': x, 'src': src, 'dst': dst, 'edge_attr_32': edge_attr_32, 'L0_gnn_W1': _L0_gnn_in['W1'], 'L0_gnn_b1': _L0_gnn_in['b1'], 'L0_gnn_g1': _L0_gnn_in['g1'], 'L0_gnn_be1': _L0_gnn_in['be1'], 'L0_gnn_W2': _L0_gnn_in['W2'], 'L0_gnn_b2': _L0_gnn_in['b2'], 'L0_gnn_Wu': _L0_gnn_in['Wu'], 'L0_gnn_bu': _L0_gnn_in['bu'], 'L0_gnn_gu': _L0_gnn_in['gu'], 'L0_gnn_beu': _L0_gnn_in['beu'], 'L1_gnn_hyperedge_weight': _L1_gnn_in['hyperedge_weight'], 'L1_gnn_W': _L1_gnn_in['W'], 'L1_gnn_b': _L1_gnn_in['b']}

def reference(x, src, dst, edge_attr_32, L0_gnn_W1, L0_gnn_b1, L0_gnn_g1, L0_gnn_be1, L0_gnn_W2, L0_gnn_b2, L0_gnn_Wu, L0_gnn_bu, L0_gnn_gu, L0_gnn_beu, L1_gnn_hyperedge_weight, L1_gnn_W, L1_gnn_b):
    import jax
    import jax.numpy as jnp

    def _L0_gnn_ref(x, edge_index, edge_attr, W1, b1, g1, be1, W2, b2, Wu, bu, gu, beu):
        import jax, jax.numpy as jnp
        import numpy as np
        N_NODES = 12500
        N_EDGES = 200000
        IN_DIM = 128
        OUT_DIM = 128
        EDGE_DIM = 32
        EPS = 1e-05

        def _layernorm(h, gamma, beta):
            mu = jnp.mean(h, axis=-1, keepdims=True)
            var = jnp.var(h, axis=-1, keepdims=True)
            return (h - mu) * jax.lax.rsqrt(var + EPS) * gamma + beta
        row, col = (edge_index[0], edge_index[1])
        msg_in = jnp.concatenate([x[row], edge_attr], axis=-1)
        h = msg_in @ W1 + b1
        h = jax.nn.gelu(_layernorm(h, g1, be1), approximate=False)
        msg = h @ W2 + b2
        agg = jax.ops.segment_sum(msg, col, num_segments=x.shape[0])
        u = jnp.concatenate([x, agg], axis=-1) @ Wu + bu
        u = jax.nn.gelu(_layernorm(u, gu, beu), approximate=False)
        return u + x

    def _L1_gnn_ref(x, hyperedge_index, hyperedge_weight, W, b):
        import jax, jax.numpy as jnp
        import numpy as np
        from jax.ops import segment_sum
        N = 12500
        M = 2500
        E = 200000
        D_IN = 128
        D_OUT = 128
        node_idx = hyperedge_index[0]
        he_idx = hyperedge_index[1]
        num_nodes = x.shape[0]
        num_he = hyperedge_weight.shape[0]
        d_e = segment_sum(jnp.ones_like(he_idx, dtype=x.dtype), he_idx, num_segments=num_he)
        d_e = jnp.clip(d_e, 1.0, None)
        d_v = segment_sum(hyperedge_weight[he_idx], node_idx, num_segments=num_nodes)
        d_v = jnp.clip(d_v, 1.0, None)
        d_v_inv_sqrt = d_v ** (-0.5)
        x_prime = x * d_v_inv_sqrt[:, None]
        he_feat = segment_sum(x_prime[node_idx], he_idx, num_segments=num_he)
        he_feat = he_feat * (hyperedge_weight / d_e)[:, None]
        out = segment_sum(he_feat[he_idx], node_idx, num_segments=num_nodes)
        out = out * d_v_inv_sqrt[:, None]
        return out @ W.T + b
    edge_index = jnp.stack([src, dst])
    h = jnp.maximum(_layernorm(x, axis=-1), 0.0)
    x = x + _L0_gnn_ref(h, edge_index, edge_attr_32, L0_gnn_W1, L0_gnn_b1, L0_gnn_g1, L0_gnn_be1, L0_gnn_W2, L0_gnn_b2, L0_gnn_Wu, L0_gnn_bu, L0_gnn_gu, L0_gnn_beu)
    h = jnp.maximum(_layernorm(x, axis=-1), 0.0)
    x = x + _L1_gnn_ref(h, edge_index, L1_gnn_hyperedge_weight, L1_gnn_W, L1_gnn_b)
    return x

_drawn_inputs = setup_inputs


def setup_inputs(seed=0):
    import zlib

    import numpy as np

    out = dict(_drawn_inputs(seed))
    spreads = {'L0_gnn_b1': (0.0, 0.1),
     'L0_gnn_g1': (1.0, 0.2),
     'L0_gnn_be1': (0.0, 0.1),
     'L0_gnn_b2': (0.0, 0.1),
     'L0_gnn_bu': (0.0, 0.8),
     'L0_gnn_gu': (1.0, 0.2),
     'L0_gnn_beu': (0.0, 0.1)}
    factors = {'L1_gnn_b': 8.0}
    for name, (base, spread) in spreads.items():
        noise = np.random.default_rng([zlib.crc32(name.encode()), seed]).standard_normal(out[name].shape)
        drawn = base * np.exp(spread * noise) if base else spread * noise
        out[name] = jnp.asarray(drawn.astype(out[name].dtype))
    for name, factor in factors.items():
        out[name] = (out[name] * factor).astype(out[name].dtype)
    return out
```

```python
import concourse.bass as bass
from concourse import mybir
from contextlib import ExitStack

F32 = mybir.dt.float32
BF16 = mybir.dt.bfloat16
I32 = mybir.dt.int32
ALU = mybir.AluOpType
ACT = mybir.ActivationFunctionType
AXX = mybir.AxisListType.X
ds = bass.ds

P = 128
N_NODES, N_EDGES, N_HYPER = 12500, 200000, 2500
D, HID, DE = 128, 256, 32
EPS = 1e-5
GROUP = 4
HALF = 2 * GROUP
BODY = 2 * HALF
TILES = -(-N_EDGES // (P * BODY)) * BODY
BODIES = TILES // BODY
PAIRS = TILES // 2
WIN = 32
NT = -(-N_NODES // P)
NP = NT * P
UCOLS = max(N_NODES + WIN, NP)
NG = 7
NGROUPS = NT // NG
HT = -(-N_HYPER // P)
HP = HT * P
FAR_COLS = NP // 32
FAR_CHUNKS = NP // FAR_COLS
FAR_HCHUNKS = -(-HP // FAR_COLS)
FAR = 1 << 20
assert FAR_COLS <= 512 and FAR_CHUNKS * FAR_COLS == NP
assert NT % (2 * NG) == 0 and TILES % BODY == 0


class Places:

    def __init__(self, dram):
        self.x, self.meta_d, self.src_d = dram["x"], dram["meta_d"], dram["src_d"]
        self.src_tiles, self.dst_tiles, self.dst_pt = dram["src_tiles"], dram["dst_tiles"], dram["dst_pt"]
        self.pair_first, self.ea_d, self.W1 = dram["pair_first"], dram["ea_d"], dram["W1"]
        self.b1, self.g1_d, self.be1_d = dram["b1"], dram["g1_d"], dram["be1_d"]
        self.W2T, self.b2, self.Wu = dram["W2T"], dram["b2"], dram["Wu"]
        self.bu, self.gu_d, self.beu_d = dram["bu"], dram["gu_d"], dram["beu_d"]
        self.w_d, self.w_pt_d, self.LWT = dram["w_d"], dram["w_pt_d"], dram["LWT"]
        self.lb_d, self.p_tab, self.hwu_tab = dram["lb_d"], dram["p_tab"], dram["hwu_tab"]
        self.xh_tab, self.x1_tab, self.xp_tab = dram["xh_tab"], dram["x1_tab"], dram["xp_tab"]
        self.g_tab, self.acc, self.out = dram["g_tab"], dram["acc"], dram["out"]


def wait_apart(k, eng, sem, value):
    eng.wait_ge(sem, value)
    eng.sem_inc(k.s_apart, 1)


class Order:

    def __init__(self, eng, sem, base=0):
        self.eng, self.sem, self.base, self.n = eng, sem, base, 0

    def __call__(self, ins):
        ins.then_inc(self.sem, 1)
        self.n += 1
        return self.base + self.n

    def wait(self, value=None):
        self.eng.wait_ge(self.sem, self.base + self.n if value is None else value)



def setup_phase(nc, k):
    s_w = k.sem("weights_loaded")
    s_d = k.sem("dst_loaded")
    s_iota = k.sem("pool_constants")
    s_v = k.sem("setup_vector_order")
    s_fold = k.sem("folded_products")
    s_row = k.sem("row_maxima")
    s_z = k.sem("zero_rows_written")
    NW = 14
    dst_all = k.U[:, 0:TILES].bitcast(I32)
    active = k.U[:, TILES:2 * TILES]
    reach = k.U[:, 2 * TILES:3 * TILES]
    tile_no = k.U[:, 3 * TILES:4 * TILES]
    local = k.U[:, 4 * TILES:5 * TILES]
    low = k.U[:, 5 * TILES:6 * TILES]
    w2t = k.U[:, 6 * TILES:6 * TILES + HID]
    wu_bot = k.U[:, 6 * TILES + HID:6 * TILES + HID + D]
    b2col = k.U[:, 6 * TILES + HID + D:6 * TILES + HID + D + 1]
    most = k.U[:, 6 * TILES + HID + D + 2:6 * TILES + HID + D + 4]
    mean = k.U[:, 6 * TILES + HID + D + 4:6 * TILES + HID + D + 7]
    rowmax = k.U[0:1, 6 * TILES + HID + D + 8:6 * TILES + HID + D + 16]
    zero = k.U[:, 7 * TILES:7 * TILES + NT * D // 2]
    with nc.Block() as block:

        @block.sync
        def _(sp):
            sp.dma_start(dst_all, k.dst_pt).then_inc(s_d, 16)
            sp.dma_start(k.firsts[:, :], k.pair_first.partition_broadcast(P)).then_inc(s_d, 16)
            sp.dma_start(k.w0[:, 0:HID], k.W1[0:D, :]).then_inc(s_w, 16)
            sp.dma_start(k.w0[:, HID:HID + D], k.Wu[0:D, :]).then_inc(s_w, 16)
            sp.dma_start(k.w1b[:, :], k.W1[D:D + DE, :]).then_inc(s_w, 16)
            sp.dma_start(k.bias0[:, 0:HID], k.b1.partition_broadcast(P)).then_inc(s_w, 16)
            sp.dma_start(k.bias0[:, HID:HID + D], k.bu.partition_broadcast(P)).then_inc(s_w, 16)
            sp.dma_start(k.g1[:, :], k.g1_d.partition_broadcast(P)).then_inc(s_w, 16)
            sp.dma_start(k.be1[:, :], k.be1_d.partition_broadcast(P)).then_inc(s_w, 16)
            sp.dma_start(k.gu[:, :], k.gu_d.partition_broadcast(P)).then_inc(s_w, 16)
            sp.dma_start(k.beu[:, :], k.beu_d.partition_broadcast(P)).then_inc(s_w, 16)
            sp.dma_start(w2t, k.W2T).then_inc(s_w, 16)
            sp.dma_start(wu_bot, k.Wu[D:2 * D, :]).then_inc(s_w, 16)
            sp.dma_start(b2col, k.b2.rearrange("(p o) -> p o", o=1)).then_inc(s_w, 16)
            sp.dma_start(k.lw[:, :], k.LWT).then_inc(s_w, 16)
            sp.dma_start(k.lb[:, :], k.lb_d.partition_broadcast(P)).then_inc(s_w, 16)
            sp.wait_ge(s_iota, 2)
            n = 0
            for r in range(k.R):
                t = k.acc[r][0:NP, :].rearrange("(c p t) d -> c p (t d)", c=2, p=P)
                for c in range(2):
                    sp.dma_start(t[c], zero).then_inc(s_z, 16)
                    n += 16
            sp.wait_ge(s_z, n)

        @block.gpsimd
        def _(gp):
            gp.memset(k.neghalf[:, :], -0.5).then_inc(s_iota, 1)
            gp.memset(zero, 0.0).then_inc(s_iota, 1)
            gp.memset(k.ident[:, :], 0.0).then_inc(s_iota, 1)
            gp.memset(k.before[:, :], 1.0).then_inc(s_iota, 1)
            gp.memset(k.ones[:, :], 1.0).then_inc(s_iota, 1)
            gp.memset(k.zerob[:, :], 0.0).then_inc(s_iota, 1)
            gp.iota(k.iota[:, :], [[1, P]], base=0, channel_multiplier=0,
                    allow_small_or_imprecise_dtypes=True).then_inc(s_iota, 1)
            gp.iota(k.iotab[:, :], [[1, P]], base=0, channel_multiplier=0,
                    allow_small_or_imprecise_dtypes=True).then_inc(s_iota, 1)
            gp.iota(k.junk[:, :], [[0, 1]], base=NP, channel_multiplier=1,
                    allow_small_or_imprecise_dtypes=True).then_inc(s_iota, 1)
            gp.iota(tile_no, [[1, TILES]], base=1, channel_multiplier=0,
                    allow_small_or_imprecise_dtypes=True).then_inc(s_iota, 1)
            gp.wait_ge(s_iota, 10)
            gp.affine_select(out=k.ident[:, :], in_=k.ident[:, :], compare_op=ALU.not_equal, fill=1.0,
                             base=0, pattern=[[-1, P]], channel_multiplier=1).then_inc(s_iota, 1)
            gp.affine_select(out=k.before[:, :], in_=k.before[:, :], compare_op=ALU.is_ge, fill=0.0,
                             base=-1, pattern=[[-1, P]], channel_multiplier=1).then_inc(s_iota, 1)

        @block.vector
        def _(v):
            o = Order(v, s_v)
            v.wait_ge(s_iota, 12)
            v.wait_ge(s_d, 32)
            o(v.tensor_scalar(active, dst_all, float(N_HYPER), None, ALU.is_lt))
            firsts = k.firsts[:, :].unsqueeze(2).to_broadcast([P, PAIRS, 2])
            o(v.tensor_tensor(local.rearrange("p (a b) -> p a b", b=2),
                              dst_all.rearrange("p (a b) -> p a b", b=2), firsts, ALU.subtract))
            o.wait()
            o(v.tensor_tensor(reach, active, tile_no, ALU.mult))
            o(v.tensor_scalar(low, local, 0.0, None, ALU.is_lt))
            o.wait()
            o(v.tensor_reduce(most[:, 0:1], reach, AXX, ALU.max))
            o(v.tensor_scalar(local, local, float(WIN), None, ALU.is_ge))
            o.wait()
            o(v.tensor_tensor(low, low, local, ALU.max))
            o(v.tensor_scalar(active, dst_all, float(N_NODES), None, ALU.is_lt))
            o.wait()
            o(v.tensor_tensor(low, low, active, ALU.mult))
            o.wait()
            o(v.tensor_reduce(most[:, 1:2], low, AXX, ALU.max))
            o.wait()
            v.sem_inc(s_row, 1)
            v.wait_ge(s_w, 16 * NW)
            o(v.tensor_reduce(mean[:, 0:1], k.w0[:, 0:HID], AXX, ALU.add))
            o(v.tensor_reduce(mean[0:DE, 1:2], k.w1b[:, :], AXX, ALU.add))
            o(v.tensor_reduce(mean[:, 2:3], k.bias0[:, 0:HID], AXX, ALU.add))
            o.wait()
            o(v.tensor_scalar(mean[:, 0:3:2], mean[:, 0:3:2], 1.0 / HID, None, ALU.mult))
            o(v.tensor_scalar(mean[0:DE, 1:2], mean[0:DE, 1:2], 1.0 / HID, None, ALU.mult))
            o.wait()
            o(v.tensor_scalar(k.w0[:, 0:HID], k.w0[:, 0:HID], mean[:, 0:1], None, ALU.subtract))
            o(v.tensor_scalar(k.w1b[:, :], k.w1b[:, :], mean[0:DE, 1:2], None, ALU.subtract))
            o(v.tensor_scalar(k.bias0[:, 0:HID], k.bias0[:, 0:HID], mean[:, 2:3], None, ALU.subtract))
            v.wait_ge(s_row, 2)
            o(v.tensor_reduce(rowmax[:, 0:1], k.psA[0:1, 0:P], AXX, ALU.max))
            o(v.tensor_reduce(rowmax[:, 1:2], k.psA[0:1, P:2 * P], AXX, ALU.max))
            o.wait()
            o(v.tensor_scalar(k.bounds[:, 0:1], rowmax[:, 0:1], float(BODY - 1), float(BODY), ALU.add, ALU.max))
            for i, most_trips in ((1, PAIRS), (2, FAR_CHUNKS), (3, FAR_HCHUNKS)):
                o(v.tensor_scalar(k.bounds[:, i:i + 1], rowmax[:, 1:2], float(most_trips - 1), 1.0, ALU.mult, ALU.add))
            o.wait()
            o(v.tensor_scalar(k.bounds[:, 0:1], k.bounds[:, 0:1], BODY.bit_length() - 1, None,
                              ALU.logical_shift_right))
            v.wait_ge(s_fold, 1)
            o(v.tensor_copy(k.w2u[:, 0:D], k.psB[:, 0:D]))
            o(v.tensor_copy(k.w2u[:, D:2 * D], k.psB[:, D:2 * D]))
            o(v.tensor_copy(k.b2u[0:1, :], k.psB[0:1, 2 * D:3 * D]))
            o.wait()

        @block.tensor
        def _(pe):
            pe.wait_ge(s_iota, 12)
            pe.wait_ge(s_row, 1)
            nc.tensor.matmul(k.psA[0:1, 0:P], most[:, 0:1], k.ident[:, :], start=True, stop=True)
            nc.tensor.matmul(k.psA[0:1, P:2 * P], most[:, 1:2], k.ident[:, :], start=True,
                             stop=True).then_inc(s_row, 1)
            pe.wait_ge(s_w, 16 * NW)
            nc.tensor.matmul(k.psB[:, 0:D], w2t[:, 0:D], wu_bot, start=True, stop=True)
            nc.tensor.matmul(k.psB[:, D:2 * D], w2t[:, D:2 * D], wu_bot, start=True, stop=True)
            nc.tensor.matmul(k.psB[0:1, 2 * D:3 * D], b2col, wu_bot, start=True, stop=True).then_inc(s_fold, 1)


def node_tables(nc, k):
    s_x = [k.sem(f"x_loaded{h}") for h in range(2)]
    s_var = k.sem("x_variance")
    s_rstd = k.sem("x_rstd")
    s_h = k.sem("h_ready")
    s_xh = k.sem("xh_ready")
    s_t = k.sem("hT_in_psum")
    s_hT = k.sem("hT_ready")
    s_p = k.sem("table_product")
    s_pw = k.sem("table_rows_ready")
    s_st = [k.sem(f"tables_stored{h}") for h in range(2)]
    s_xs = [k.sem(f"xh_stored{h}") for h in range(2)]
    s_v = k.sem("tables_vector_order")
    at = [0]

    def take(n):
        at[0] += n
        return k.U[:, at[0] - n:at[0]]

    xg = [take(NG * D).rearrange("p (t d) -> p t d", d=D) for _ in range(2)]
    hg = [take(NG * D).rearrange("p (t d) -> p t d", d=D) for _ in range(2)]
    xh = [take(NG * D).rearrange("p (t d) -> p t d", d=D) for _ in range(2)]
    rows = [take(NG * (HID + D)).rearrange("p (t d) -> p t d", d=HID + D) for _ in range(2)]
    hT = [take(P) for _ in range(2)]
    stats = [take(NG * 6).rearrange("p (t d) -> p t d", d=6) for _ in range(2)]
    mv = [take(NG * 2).rearrange("p (t d) -> p t d", d=2) for _ in range(2)]
    var = [take(NG) for _ in range(2)]
    rstd = [take(NG) for _ in range(2)]
    psT = [k.psA, k.psB]
    psP = [k.psH[0], k.psH[1]]
    x_v = k.x.rearrange("(g t p) d -> g p t d", p=P, t=NG)
    xh_v = k.xh_tab.rearrange("(g t p) d -> g p t d", p=P, t=NG)
    p_v = k.p_tab.rearrange("(g t p) d -> g p t d", p=P, t=NG)
    hwu_v = k.hwu_tab.rearrange("(g t p) d -> g p t d", p=P, t=NG)
    LAST = NGROUPS // 2 - 1

    with nc.Block() as block:

        @block.sync
        def _(sp):
            def load(g, h):
                sp.dma_start(xg[h], x_v[ds(g, 1)].rearrange("o p t d -> (o p) t d")).then_inc(s_x[h], 16)

            def store(g, h):
                sp.wait_ge(s_xh, g + 1)
                sp.dma_start(xh_v[ds(g, 1)].rearrange("o p t d -> (o p) t d"), xh[h]).then_inc(s_xs[h], 16)
                sp.wait_ge(s_pw, NG * (g + 1))
                sp.dma_start(p_v[ds(g, 1)].rearrange("o p t d -> (o p) t d"),
                             rows[h][:, :, 0:HID]).then_inc(s_st[h], 16)
                sp.dma_start(hwu_v[ds(g, 1)].rearrange("o p t d -> (o p) t d"),
                             rows[h][:, :, HID:HID + D]).then_inc(s_st[h], 16)

            for h in range(2):
                sp.sem_inc(s_st[h], 32)
                sp.sem_inc(s_xs[h], 16)
                load(h, h)
            with sp.Fori(0, LAST) as b:
                for h in range(2):
                    sp.wait_ge(s_xh, 2 * b + h + 1)
                    load(2 * b + 2 + h, h)
                    store(2 * b + h, h)
            for h in range(2):
                store(2 * LAST + h, h)
            for h in range(2):
                sp.wait_ge(s_st[h], 32 * (LAST + 2))
                sp.wait_ge(s_xs[h], 16 * (LAST + 2))

        @block.gpsimd
        def _(gp):
            with gp.Fori(0, LAST + 1) as b:
                for h in range(2):
                    g = 2 * b + h
                    gp.wait_ge(s_var, g + 1)
                    gp.tensor_tensor(rstd[h], var[h], k.neghalf[:, 0:NG], ALU.pow).then_inc(s_rstd, 1)
                    gp.wait_ge(s_h, g + 1)
                    gp.wait_ge(s_xs[h], 16 * b + 16)
                    gp.tensor_tensor(xh[h], xg[h], hg[h], ALU.add).then_inc(s_xh, 1)

        @block.vector
        def _(v):
            K = 3 * NG

            def products(g, h):
                v.wait_ge(s_st[h], 16 * (g - h) + 32)
                for t in range(NG):
                    v.wait_ge(s_p, NG * g + t + 1 + 2)
                    v.tensor_tensor(rows[h][:, t, :], psP[(NG * h + t) % 2][:, 0:HID + D], k.bias0[:, :],
                                    ALU.add).then_inc(s_pw, 1)

            def slot(g, h, prev):
                o = Order(v, s_v, K * g)
                v.wait_ge(s_x[h], 8 * (g - h) + 16)
                for t in range(NG):
                    o(v.bn_stats(stats[h][:, t, :], xg[h][:, t, :]))
                for t in range(NG):
                    wait_apart(k, v, s_v, o.base + t + 1)
                    o(v.bn_aggr(mv[h][:, t, :], stats[h][:, t, :]))
                o.wait()
                v.tensor_scalar(var[h], mv[h][:, :, 1], EPS, None, ALU.add).then_inc(s_var, 1)
                if prev:
                    products(g - 1, 1 - h)
                    if not isinstance(g, int) or g >= 2:
                        v.wait_ge(s_xh, g - 1)
                v.wait_ge(s_rstd, g + 1)
                for t in range(NG):
                    o(v.tensor_scalar(hg[h][:, t, :], xg[h][:, t, :], mv[h][:, t, 0:1], rstd[h][:, t:t + 1],
                                      ALU.subtract, ALU.mult))
                o.wait()
                v.tensor_scalar(hg[h], hg[h], 0.0, None, ALU.max).then_inc(s_h, 1)

            slot(0, 0, False)
            slot(1, 1, True)
            with v.Fori(1, LAST + 1) as b:
                for h in range(2):
                    slot(2 * b + h, h, True)
            products(2 * LAST + 1, 1)

        @block.scalar
        def _(a):
            with a.Fori(0, LAST + 1) as b:
                for n in range(2 * NG):
                    a.wait_ge(s_t, 2 * NG * b + n + 1)
                    a.wait_ge(s_p, 2 * NG * b + n + 1)
                    a.copy(hT[n % 2], psT[n % 2][:, 0:P]).then_inc(s_hT, 1)

        @block.tensor
        def _(pe):
            pe.sem_inc(s_p, 2)

            def transpose(b, n):
                h, t = divmod(n, NG)
                if t == 0:
                    pe.wait_ge(s_h, 2 * b + h + 1)
                if isinstance(b, int) and 2 * NG * b + n < 2:
                    pass
                else:
                    pe.wait_ge(s_hT, 2 * NG * b + n - 1)
                nc.tensor.transpose(psT[n % 2][:, 0:P], hg[h][:, t, :], k.ident[:, :]).then_inc(s_t, 1)

            def product(b, n, first=False):
                pe.wait_ge(s_hT, 2 * NG * b + n + 1)
                if not (isinstance(b, int) and 2 * NG * b + n < 2):
                    pe.wait_ge(s_pw, 2 * NG * b + n - 1)
                nc.tensor.matmul(psP[n % 2][:, 0:HID + D], hT[n % 2], k.w0[:, :], start=True,
                                 stop=True).then_inc(s_p, 1)

            def body(b):
                for n in range(2 * NG):
                    transpose(b, n)
                    if n % NG:
                        product(b, n - 1)
                    if n % NG == NG - 1:
                        product(b, n)

            body(0)
            with pe.Fori(1, LAST + 1) as b:
                body(b)



def edge_messages(nc, k):
    s_meta = [k.sem(f"indices_loaded{h}") for h in range(2)]
    s_ea = [k.sem(f"edge_features_loaded{g}") for g in range(4)]
    s_g = [k.sem(f"rows_gathered{j}") for j in range(HALF)]
    s_tile = k.sem("tile_in_psum")
    s_sq = k.sem("squares_summed")
    s_var = k.sem("edge_variance")
    s_rstd = k.sem("edge_rstd")
    s_z = k.sem("normalised")
    s_gelu = k.sem("gelu_done")
    s_loc = k.sem("indices_taken")
    s_oh = k.sem("window_masks")
    s_hm = k.sem("histogram_masks")
    s_hist = k.sem("histogram_added")
    s_seg = k.sem("windows_summed")
    s_u = k.sem("windows_kept")
    s_v = k.sem("edge_vector_order")
    s_a = k.sem("edge_scalar_order")
    s_u0 = k.sem("sums_zeroed")
    NGR = TILES // GROUP
    LAG_Z, LAG_SEG, LAG_U = 1, 2, 3
    assert BODY == 4 * GROUP

    rows = k.stage[:, 0:HALF * HID].rearrange("p (j d) -> p j d", d=HID)
    z = [k.stage[:, (HALF + GROUP * i) * HID:(HALF + GROUP * (i + 1)) * HID].rearrange("p (j d) -> p j d", d=HID)
         for i in range(2)]
    psH = [t[:, :].rearrange("p (j d) -> p j d", d=HID) for t in k.psH]
    psU = [t[:, 0:2 * 3 * WIN].rearrange("p (q c w) -> p q c w", q=2, c=3) for t in (k.psA, k.psB)]
    psC = k.psC[:, 0:NT]
    U3 = k.U[:, :].rearrange("p (c n) -> p c n", c=3)

    with nc.Block() as block:

        @block.sync
        def _(sp):
            def load_meta(b, h):
                sp.dma_start(k.meta[h][:, :], k.meta_d[ds(2 * b + h, 1)].rearrange("o p c -> (o p) c"))\
                  .then_inc(s_meta[h], 16)

            def load_ea(b, g):
                sp.dma_start(k.ea[g][:, :].rearrange("f (t e) -> f t e", e=P),
                             k.ea_d[ds(BODY * b + GROUP * g, GROUP)].rearrange("t f e -> f t e"))\
                  .then_inc(s_ea[g], 16)

            for h in range(2):
                load_meta(0, h)
                load_ea(0, 2 * h)
                load_ea(0, 2 * h + 1)
            with sp.Fori(0, BODIES - 1) as b:
                for g in range(4):
                    sp.wait_ge(s_tile, BODY * b + GROUP * (g + 1))
                    load_ea(b + 1, g)
                    if g % 2:
                        sp.wait_ge(s_loc, 2 * b + g // 2 + 1)
                        load_meta(b + 1, g // 2)

        @block.gpsimd
        def _(gp):
            def gather(h, j):
                gp.indirect_dma_start(out=rows[:, j, :], out_offset=None, in_=k.p_tab[:, :],
                                      in_offset=bass.IndirectOffsetOnAxis(ap=k.meta[h][:, j:j + 1], axis=0))\
                  .then_inc(s_g[j], 16)

            def rstd(gg, g):
                gp.wait_ge(s_var, gg + 1)
                gp.tensor_tensor(k.rstd[g % 2][:, :], k.var[g % 2][:, :], k.neghalf[:, 0:GROUP], ALU.pow)\
                  .then_inc(s_rstd, 1)

            def second_half(b):
                wait_apart(k, gp, s_meta[1], 16 * b + 16)
                for j in range(HALF):
                    wait_apart(k, gp, s_tile, BODY * b + j + 1)
                    gather(1, j)
                    if j % GROUP == 1:
                        rstd(4 * b + j // GROUP, j // GROUP)

            def next_first_half(b):
                wait_apart(k, gp, s_meta[0], 16 * b + 32)
                for j in range(HALF):
                    wait_apart(k, gp, s_tile, BODY * b + HALF + j + 1)
                    gather(0, j)
                    if j % GROUP == 1:
                        rstd(4 * b + 2 + j // GROUP, j // GROUP)

            wait_apart(k, gp, s_meta[0], 16)
            for j in range(HALF):
                gather(0, j)
            with gp.Fori(0, BODIES - 1) as b:
                second_half(b)
                next_first_half(b)
            second_half(BODIES - 1)
            rstd(NGR - 2, 0)
            rstd(NGR - 1, 1)

        @block.tensor
        def _(pe):
            def products(b, g):
                gg = 4 * b + g
                h = g // 2
                pe.wait_ge(s_ea[g], 16 * b + 16)
                if not (isinstance(gg, int) and gg < 2):
                    pe.wait_ge(s_z, gg - 1)
                for t in range(GROUP):
                    j = GROUP * (g % 2) + t
                    nc.tensor.matmul(psH[g % 2][:, t, :], k.ea[g][:, P * t:P * t + P], k.w1b[:, :],
                                     start=True, stop=False)
                    pe.wait_ge(s_g[j], 16 * (2 * b + h) + 16)
                    nc.tensor.matmul(psH[g % 2][:, t, :], k.ident[:, :], rows[:, j, :], start=False,
                                     stop=True).then_inc(s_tile, 1)

            def histogram(b, g):
                gg = 4 * b + g
                for t in range(GROUP):
                    pe.wait_ge(s_hm, GROUP * gg + t + 1)
                    nc.tensor.matmul(psC, k.ohb[t][:, :], k.oha[t][:, 0:NT], start=False, stop=False)\
                      .then_inc(s_hist, 1)

            def window_sums(gg, g):
                pe.wait_ge(s_gelu, gg + 1)
                if not (isinstance(gg, int) and gg < 2):
                    pe.wait_ge(s_u, gg - 1)
                for q in range(2):
                    for c in range(3):
                        for i in range(2):
                            t = 2 * q + i
                            left = z[g % 2][:, t, c * P:(c + 1) * P] if c < 2 else k.ones[:, :]
                            last = nc.tensor.matmul(psU[g % 2][:, q, c, :], left,
                                                    k.oh[g // 2][:, GROUP * (g % 2) + t, :],
                                                    start=i == 0, stop=i == 1)
                last.then_inc(s_seg, 1)

            nc.tensor.matmul(psC, k.zerob[:, :], k.zerob[:, 0:NT], start=True, stop=False)
            for g in range(4):
                products(0, g)
                if g >= LAG_SEG:
                    window_sums(g - LAG_SEG, g - LAG_SEG)
                histogram(0, g)
            with pe.Fori(1, BODIES) as b:
                for g in range(4):
                    products(b, g)
                    window_sums(4 * b + g - LAG_SEG, (g - LAG_SEG) % 4)
                    histogram(b, g)
            for gg in range(NGR - LAG_SEG, NGR):
                window_sums(gg, gg % 4)
            nc.tensor.matmul(psC, k.zerob[:, :], k.zerob[:, 0:NT], start=False, stop=True).then_inc(s_hist, 1)

        @block.scalar
        def _(a):
            def squares(b, g):
                gg = 4 * b + g
                for t in range(GROUP):
                    a.wait_ge(s_tile, GROUP * gg + t // 2 * 2 + 2)
                    if not (isinstance(gg, int) and gg < 1):
                        a.wait_ge(s_sq, GROUP * gg + t - GROUP + 1)
                        if t == 0:
                            a.wait_ge(s_var, gg - 1) if not (isinstance(gg, int) and gg < 2) else None
                    nc.scalar.activation(k.scratch[:, t, :], psH[g % 2][:, t, :], ACT.Square, scale=HID ** -0.5,
                                         accum_out=k.ssq[g % 2][:, t:t + 1]).then_inc(s_sq, 1)

            def gelu(gg, g):
                a.wait_ge(s_z, gg + 1)
                nc.scalar.activation(z[g % 2], z[g % 2], ACT.Gelu).then_inc(s_gelu, 1)

            for g in range(4):
                squares(0, g)
                if g >= LAG_Z:
                    gelu(g - LAG_Z, g - LAG_Z)
            with a.Fori(1, BODIES) as b:
                for g in range(4):
                    squares(b, g)
                    gelu(4 * b + g - LAG_Z, (g - LAG_Z) % 4)
            gelu(NGR - 1, 3)

        @block.vector
        def _(v):
            K = 2 * 5 + 4 * (GROUP + 1)

            def indices(o, b, h):
                v.wait_ge(s_meta[h], 16 * b + 16)
                src, dst = k.meta[h][:, 0:HALF], k.meta[h][:, HALF:2 * HALF]
                first = k.firsts[:, ds(8 * b + 4 * h, 4)].unsqueeze(2).to_broadcast([P, 4, 2])
                o(v.tensor_tensor(k.local[h][:, :].rearrange("p (a c) -> p a c", c=2),
                                  dst.rearrange("p (a c) -> p a c", c=2), first, ALU.subtract))
                o(v.tensor_scalar(k.bits[h][:, 0:HALF], src, P - 1, None, ALU.bitwise_and))
                o(v.tensor_scalar(k.bits[h][:, HALF:2 * HALF], src, P.bit_length() - 1, None, ALU.logical_shift_right))
                o(v.tensor_scalar(k.beyond[h][:, :], dst, float(N_HYPER), None, ALU.is_ge))
                o.wait()
                o(v.tensor_copy(k.digits[h][:, 0:2 * HALF], k.bits[h][:, 0:2 * HALF]))
                o.wait()
                v.sem_inc(s_loc, 1)

            def window_masks(b, h):
                gg = 4 * b + 2 * h
                if not (isinstance(b, int) and b < 1):
                    v.wait_ge(s_seg, gg - 2)
                v.tensor_tensor(k.oh[h][:, :, :], k.iota[:, 0:WIN].unsqueeze(1).to_broadcast([P, HALF, WIN]),
                                k.local[h][:, :].unsqueeze(2).to_broadcast([P, HALF, WIN]),
                                ALU.is_equal).then_inc(s_oh, 1)

            def histogram_masks(b, g):
                gg = 4 * b + g
                if not (isinstance(gg, int) and gg < 1):
                    v.wait_ge(s_hist, GROUP * gg)
                for t in range(GROUP):
                    j = GROUP * (g % 2) + t
                    h = g // 2
                    v.tensor_scalar(k.ohb[t][:, :], k.iotab[:, :], k.src_lo[h][:, j:j + 1], None, ALU.is_equal)
                    v.tensor_scalar(k.oha[t][:, :], k.iotab[:, 0:NT], k.src_hi[h][:, j:j + 1],
                                    k.beyond[h][:, j:j + 1], ALU.is_equal, ALU.mult).then_inc(s_hm, 1)

            def variance(gg, g):
                v.wait_ge(s_sq, GROUP * gg + GROUP)
                if not (isinstance(gg, int) and gg < 2):
                    v.wait_ge(s_rstd, gg - 1)
                v.tensor_scalar(k.var[g % 2][:, :], k.ssq[g % 2][:, :], EPS, None, ALU.add).then_inc(s_var, 1)

            def normalise(o, gg, g):
                v.wait_ge(s_rstd, gg + 1)
                if not (isinstance(gg, int) and gg < 2):
                    v.wait_ge(s_seg, gg - 1)
                for t in range(GROUP):
                    o(v.scalar_tensor_tensor(z[g % 2][:, t, :], psH[g % 2][:, t, :], k.rstd[g % 2][:, t:t + 1],
                                             k.g1[:, :], ALU.mult, ALU.mult))
                o.wait()
                v.tensor_tensor(z[g % 2], z[g % 2], k.be1[:, :].unsqueeze(1).to_broadcast([P, GROUP, HID]),
                                ALU.add).then_inc(s_z, 1)

            def keep(o, gg, g):
                v.wait_ge(s_seg, gg + 1)
                for q in range(2):
                    first = v.value_load(k.firsts[0:1, ds(2 * gg + q, 1)], min_val=0, max_val=N_NODES)
                    if q == 1:
                        o.wait(at[0])
                    at[0] = None
                    ins = v.tensor_tensor(U3[:, :, ds(first, WIN)], U3[:, :, ds(first, WIN)], psU[g % 2][:, q],
                                          ALU.add)
                    if q == 0:
                        at[0] = o(ins)
                    else:
                        ins.then_inc(s_u, 1)

            at = [None]

            def slot(o, b, g, lead):
                gg = 4 * b + g
                if g % 2 == 0:
                    indices(o, b, g // 2)
                    window_masks(b, g // 2)
                histogram_masks(b, g)
                if not lead or g >= LAG_U:
                    if not (lead and g == LAG_U):
                        v.wait_ge(s_u, gg - LAG_U)
                    keep(o, gg - LAG_U, (g - LAG_U) % 4)
                variance(gg, g)
                if not lead or g >= LAG_Z:
                    normalise(o, gg - LAG_Z, (g - LAG_Z) % 4)

            v.memset(k.U[:, :], 0.0).then_inc(s_u0, 1)
            v.wait_ge(s_u0, 1)
            o = Order(v, s_v)
            for g in range(4):
                slot(o, 0, g, True)
            start = o.n
            with v.Fori(1, BODIES) as b:
                o = Order(v, s_v, start + K * (b - 1))
                for g in range(4):
                    slot(o, b, g, False)
                k_body = o.n
            o = Order(v, s_v, start + k_body * (BODIES - 1))
            normalise(o, NGR - 1, 3)
            for gg in range(NGR - LAG_U, NGR):
                v.wait_ge(s_u, gg)
                keep(o, gg, gg % 4)
            v.wait_ge(s_u, NGR)
            v.wait_ge(s_hist, TILES + 1)
            v.tensor_copy(k.beyond_count[:, :], psC)
            assert k_body == K, (k_body, K)



def far_edges(nc, k, messages):
    layer = "far_messages" if messages else "far_hyperedges"
    chunks = FAR_CHUNKS if messages else FAR_HCHUNKS
    s_ld = k.sem(f"{layer}_loaded")
    s_g = k.sem(f"{layer}_rows_gathered")
    s_h = k.sem(f"{layer}_hidden")
    s_sq = k.sem(f"{layer}_squares")
    s_var = k.sem(f"{layer}_variance")
    s_rs = k.sem(f"{layer}_rstd")
    s_n = k.sem(f"{layer}_normalised")
    s_z = k.sem(f"{layer}_rows_ready")
    s_m = [k.sem(f"{layer}_masks{i}") for i in range(2)]
    s_p = [k.sem(f"{layer}_products{i}") for i in range(2)]
    s_k = [k.sem(f"{layer}_kept{i}") for i in range(2)]
    s_t = k.sem(f"{layer}_tiles_done")
    s_i = k.sem(f"{layer}_columns")
    s_f = [k.sem(f"{layer}_destinations{i}") for i in range(2)]
    s_v = k.sem(f"{layer}_vector_order")
    cols = HID if messages else D
    loads = 48 if messages else 32
    parts = 3 if messages else 1
    table = k.p_tab if messages else k.xp_tab
    rows = k.stage[:, 0:cols]
    columns = k.stage[:, HID:HID + FAR_COLS]
    mask = k.stage[:, HID + FAR_COLS:HID + 2 * FAR_COLS]
    at = HID + 2 * FAR_COLS
    z = k.stage[:, at:at + HID]
    square = k.stage[:, at + HID:at + 2 * HID]
    ea = k.stage[0:DE, at + 2 * HID:at + 2 * HID + P]
    at += 2 * HID + P
    local, low, high, far, ssq, rstd = (k.stage[:, at + i:at + i + 1] for i in range(6))
    src = k.stage[:, at + 6:at + 7].bitcast(I32)
    dst = k.stage[:, at + 7:at + 8].bitcast(I32)
    ps = [k.psA, k.psB, k.psC]
    sums = k.U[:, :].rearrange("p (c n) -> p c n", c=3)

    def trips(eng):
        return (eng.value_load(k.bounds[0:1, 1:2], min_val=1, max_val=PAIRS),
                eng.value_load(k.bounds[0:1, 2 if messages else 3:3 if messages else 4], min_val=1, max_val=chunks))

    with nc.Block() as block:

        @block.sync
        def _(sp):
            n_pairs, _ = trips(sp)
            sp.sem_inc(s_t, 1)
            with sp.Fori(0, n_pairs) as b:
                for i in range(2):
                    tile = 2 * b + i
                    sp.wait_ge(s_t, tile + 1)
                    sp.dma_start(src, k.src_tiles[ds(tile, 1)].rearrange("o e c -> (o e) c")).then_inc(s_ld, 16)
                    sp.dma_start(dst, k.dst_tiles[ds(tile, 1)].rearrange("o e c -> (o e) c")).then_inc(s_ld, 16)
                    if messages:
                        sp.dma_start(ea, k.ea_d[ds(tile, 1)].rearrange("o f e -> (o f) e")).then_inc(s_ld, 16)

        @block.gpsimd
        def _(gp):
            n_pairs, _ = trips(gp)
            gp.iota(columns, [[1, FAR_COLS]], base=1, channel_multiplier=0,
                    allow_small_or_imprecise_dtypes=True).then_inc(s_i, 1)
            with gp.Fori(0, n_pairs) as b:
                for i in range(2):
                    tile = 2 * b + i
                    wait_apart(k, gp, s_ld, loads * tile + loads)
                    gp.indirect_dma_start(out=rows, out_offset=None, in_=table[:, :],
                                          in_offset=bass.IndirectOffsetOnAxis(ap=src, axis=0)).then_inc(s_g, 16)
                    if messages:
                        gp.wait_ge(s_var, tile + 1)
                        gp.tensor_tensor(rstd, ssq, k.neghalf[:, 0:1], ALU.pow).then_inc(s_rs, 1)

        @block.scalar
        def _(a):
            n_pairs, _ = trips(a)
            if messages:
                with a.Fori(0, n_pairs) as b:
                    for i in range(2):
                        tile = 2 * b + i
                        a.wait_ge(s_h, tile + 1)
                        nc.scalar.activation(square, k.psH[0][:, 0:HID], ACT.Square, scale=HID ** -0.5,
                                             accum_out=ssq).then_inc(s_sq, 1)
                        a.wait_ge(s_n, tile + 1)
                        nc.scalar.activation(z, z, ACT.Gelu).then_inc(s_z, 1)

        @block.tensor
        def _(pe):
            n_pairs, n_chunks = trips(pe)
            with pe.Fori(0, n_pairs) as b:
                for i in range(2):
                    tile = 2 * b + i
                    wait_apart(k, pe, s_g, 16 * tile + 16)
                    if messages:
                        pe.wait_ge(s_ld, loads * tile + loads)
                        nc.tensor.matmul(k.psH[0][:, 0:HID], ea, k.w1b[:, :], start=True, stop=False)
                        nc.tensor.matmul(k.psH[0][:, 0:HID], k.ident[:, :], rows, start=False, stop=True).then_inc(s_h, 1)
                        wait_apart(k, pe, s_z, tile + 1)
                        left = [z[:, 0:P], z[:, P:HID], k.ones[:, :]]
                    else:
                        left = [rows]
                    with pe.Fori(0, n_chunks) as c:
                        pe.wait_ge(s_m[i], chunks * b + c + 1)
                        for m in range(parts):
                            last = nc.tensor.matmul(ps[m][:, 0:FAR_COLS], left[m], mask, start=True, stop=True)
                        last.then_inc(s_p[i], 1)

        @block.vector
        def _(v):
            n_pairs, n_chunks = trips(v)
            K = 7 if messages else 5
            v.wait_ge(s_i, 1)
            for i in range(2):
                v.sem_inc(s_k[i], 1)
            with v.Fori(0, n_pairs) as b:
                for i in range(2):
                    tile = 2 * b + i
                    o = Order(v, s_v, K * tile)
                    v.wait_ge(s_ld, loads * tile + loads)
                    o(v.tensor_tensor(local, dst, k.firsts[:, ds(b, 1)], ALU.subtract))
                    o(v.tensor_scalar(far, dst, 1.0, None, ALU.add))
                    o.wait()
                    o(v.tensor_scalar(low, local, 0.0, None, ALU.is_lt))
                    o(v.tensor_scalar(high, local, float(WIN), None, ALU.is_ge))
                    o.wait()
                    o(v.tensor_tensor(low, low, high, ALU.max))
                    o.wait()
                    v.tensor_tensor(far, far, low, ALU.mult).then_inc(s_f[i], 1)
                    if messages:
                        v.wait_ge(s_sq, tile + 1)
                        o(v.tensor_scalar(ssq, ssq, EPS, None, ALU.add))
                        o.wait()
                        v.sem_inc(s_var, 1)
                        v.wait_ge(s_rs, tile + 1)
                        o(v.scalar_tensor_tensor(z, k.psH[0][:, 0:HID], rstd, k.g1[:, :], ALU.mult, ALU.mult))
                        o.wait()
                        v.tensor_tensor(z, z, k.be1[:, :], ALU.add).then_inc(s_n, 1)
                    with v.Fori(0, n_chunks) as c:
                        step = chunks * b + c
                        wait_apart(k, v, s_f[i], b + step + 1)
                        v.wait_ge(s_k[i], step + 1)
                        v.tensor_scalar(mask, columns, far, None, ALU.is_equal).then_inc(s_m[i], 1)
                        v.wait_ge(s_p[i], step + 1)
                        v.tensor_scalar(far, far, -float(FAR_COLS), None, ALU.add).then_inc(s_f[i], 1)
                        for m in range(parts):
                            to = sums[:, m, ds(c * FAR_COLS, FAR_COLS)]
                            last = v.tensor_tensor(to, to, ps[m][:, 0:FAR_COLS], ALU.add)
                        last.then_inc(s_k[i], 1)
                    v.wait_ge(s_k[i], chunks * b + n_chunks + 1)
                    v.sem_inc(s_t, 1)


def far_messages(nc, k):
    far_edges(nc, k, True)


def far_hyperedges(nc, k):
    far_edges(nc, k, False)


def hyper_degrees(nc, k):
    s_meta = [k.sem(f"deg_indices_loaded{h}") for h in range(2)]
    s_ix = k.sem("deg_indices_ready")
    s_wg = [k.sem(f"weights_gathered{h}") for h in range(2)]
    s_m = k.sem("deg_masks")
    s_mu = k.sem("deg_added")
    s_v = k.sem("deg_vector_order")
    s_ld = k.sem("deg_constants_loaded")
    s_pow = k.sem("deg_base")
    s_dv = k.sem("deg_sum_order")
    s_end = k.sem("deg_done")
    psV = k.psA[:, 0:NT]
    psD = k.psB[:, 0:HT]
    IX = 7

    with nc.Block() as block:

        @block.sync
        def _(sp):
            n_bodies = sp.value_load(k.bounds[0:1, 0:1], min_val=1, max_val=BODIES)

            def load_meta(b, h):
                sp.dma_start(k.meta[h][:, :], k.meta_d[ds(2 * b + h, 1)].rearrange("o p c -> (o p) c"))\
                  .then_inc(s_meta[h], 16)

            sp.dma_start(k.w_last[:, :], k.w_d[N_HYPER - 1:N_HYPER, :].partition_broadcast(P)
                         .rearrange("p a b -> p (a b)")).then_inc(s_ld, 16)
            sp.dma_start(k.w_pt[:, :], k.w_pt_d).then_inc(s_ld, 16)
            for h in range(2):
                load_meta(0, h)
            with sp.Fori(0, n_bodies) as b:
                for h in range(2):
                    sp.wait_ge(s_wg[h], 16 * HALF * (b + 1))
                    load_meta(b + 1, h)
            for h in range(2):
                wait_apart(k, sp, s_meta[h], 16 * n_bodies + 16)

        @block.gpsimd
        def _(gp):
            n_bodies = gp.value_load(k.bounds[0:1, 0:1], min_val=1, max_val=BODIES)
            with gp.Fori(0, n_bodies) as b:
                for h in range(2):
                    wait_apart(k, gp, s_ix, 2 * b + h + 1)
                    for j in range(HALF):
                        gp.indirect_dma_start(out=k.w_row[h][:, j:j + 1], out_offset=None, in_=k.w_d[:, :],
                                              in_offset=bass.IndirectOffsetOnAxis(ap=k.gidx[h][:, j:j + 1], axis=0))\
                          .then_inc(s_wg[h], 16)
            gp.wait_ge(s_pow, 1)
            gp.tensor_tensor(k.dvr[:, :], k.dvr[:, :], k.neghalf[:, 0:NT], ALU.pow).then_inc(s_end, 1)

        @block.tensor
        def _(pe):
            n_bodies = pe.value_load(k.bounds[0:1, 0:1], min_val=1, max_val=BODIES)
            pe.sem_inc(s_mu, 2)
            nc.tensor.matmul(psV, k.zerob[:, :], k.zerob[:, 0:NT], start=True, stop=False)
            nc.tensor.matmul(psD, k.zerob[:, :], k.zerob[:, 0:HT], start=True, stop=False)
            with pe.Fori(0, n_bodies) as b:
                for n in range(BODY):
                    pe.wait_ge(s_m, BODY * b + n + 1)
                    nc.tensor.matmul(psV, k.mask_lo[n % 2][:, :], k.mask_hi[n % 2][:, 0:NT], start=False, stop=False)
                    nc.tensor.matmul(psD, k.ohb[n % 2][:, :], k.oha[n % 2][:, 0:HT], start=False,
                                     stop=False).then_inc(s_mu, 1)
            nc.tensor.matmul(psV, k.zerob[:, :], k.zerob[:, 0:NT], start=False, stop=True)
            nc.tensor.matmul(psD, k.zerob[:, :], k.zerob[:, 0:HT], start=False, stop=True).then_inc(s_mu, 1)

        @block.vector
        def _(v):
            n_bodies = v.value_load(k.bounds[0:1, 0:1], min_val=1, max_val=BODIES)
            v.wait_ge(s_ld, 32)
            K = 2 * (IX + 1)

            def indices(o, b, h):
                v.wait_ge(s_meta[h], 16 * b + 16)
                src, dst = k.meta[h][:, 0:HALF], k.meta[h][:, HALF:2 * HALF]
                o(v.tensor_scalar(k.gidx[h][:, :], dst, float(N_HYPER - 1), None, ALU.min))
                o(v.tensor_scalar(k.beyond[h][:, :], dst, float(N_HYPER), None, ALU.is_lt))
                o(v.tensor_scalar(k.bits[h][:, 0:HALF], src, P - 1, None, ALU.bitwise_and))
                o(v.tensor_scalar(k.bits[h][:, HALF:2 * HALF], src, P.bit_length() - 1, None, ALU.logical_shift_right))
                o(v.tensor_scalar(k.bits[h][:, 2 * HALF:3 * HALF], dst, P - 1, None, ALU.bitwise_and))
                o(v.tensor_scalar(k.bits[h][:, 3 * HALF:4 * HALF], dst, P.bit_length() - 1, None, ALU.logical_shift_right))
                o.wait()
                o(v.tensor_copy(k.digits[h][:, :], k.bits[h][:, :]))
                o.wait()
                v.sem_inc(s_ix, 1)

            def masks(o, b, h):
                v.wait_ge(s_wg[h], 16 * HALF * (b + 1))
                o(v.tensor_tensor(k.w_act[h][:, :], k.w_row[h][:, :], k.beyond[h][:, :], ALU.mult))
                o.wait()
                for j in range(HALF):
                    n = HALF * h + j
                    v.wait_ge(s_mu, BODY * b + n + 1)
                    i = n % 2
                    v.tensor_scalar(k.mask_lo[i][:, :], k.iota[:, :], k.src_lo[h][:, j:j + 1], None, ALU.is_equal)
                    v.tensor_scalar(k.mask_hi[i][:, 0:NT], k.iota[:, 0:NT], k.src_hi[h][:, j:j + 1],
                                    k.w_act[h][:, j:j + 1], ALU.is_equal, ALU.mult)
                    v.tensor_scalar(k.ohb[i][:, :], k.iotab[:, :], k.dst_lo[h][:, j:j + 1], None, ALU.is_equal)
                    v.tensor_scalar(k.oha[i][:, 0:HT], k.iotab[:, 0:HT], k.dst_hi[h][:, j:j + 1], None,
                                    ALU.is_equal).then_inc(s_m, 1)

            o = Order(v, s_v)
            indices(o, 0, 0)
            with v.Fori(0, n_bodies) as b:
                o = Order(v, s_v, K * b + IX)
                indices(o, b, 1)
                masks(o, b, 0)
                indices(o, b + 1, 0)
                masks(o, b, 1)
                assert o.n == K, (o.n, K)
            last = n_bodies * BODY
            v.wait_ge(s_mu, last + 3)
            o = Order(v, s_dv)
            o(v.scalar_tensor_tensor(k.dvr[:, :], k.beyond_count[:, :], k.w_last[:, 0:1], psV, ALU.mult, ALU.add))
            o(v.tensor_scalar(k.w_de[:, :], psD, 1.0, None, ALU.max))
            o.wait()
            o(v.tensor_scalar(k.dvr[:, :], k.dvr[:, :], 1.0, None, ALU.max))
            o(v.reciprocal(k.w_de[:, :], k.w_de[:, :]))
            o.wait()
            o(v.tensor_tensor(k.w_de[:, :], k.w_de[:, :], k.w_pt[:, :], ALU.mult))
            v.sem_inc(s_pow, 1)


def node_update(nc, k):
    s_ld = [k.sem(f"update_loaded{h}") for h in range(2)]
    s_ut = k.sem("sums_copied")
    s_ps = k.sem("update_product")
    s_u = k.sem("update_taken")
    s_var = k.sem("update_variance")
    s_rs = k.sem("update_rstd")
    s_n = k.sem("update_scaled")
    s_b = k.sem("update_biased")
    s_g = k.sem("update_gelu")
    s_x1 = k.sem("x1_ready")
    s_xp = k.sem("xp_ready")
    s_st = [k.sem(f"update_stored{h}") for h in range(2)]
    s_v = k.sem("update_vector_order")
    W = NG * D
    LAST = NGROUPS // 2

    def grp(i):
        return k.stage[:, i * W:(i + 1) * W].rearrange("p (t d) -> p t d", d=D)

    u, xh, xp = [grp(0), grp(1)], [grp(2), grp(3)], [grp(4), grp(5)]
    U3 = k.U[:, :].rearrange("p (c n) -> p c n", c=3)
    ps = [k.psA, k.psB]
    view = {n: t.rearrange("(g t p) d -> g p t d", p=P, t=NG)
            for n, t in (("hwu", k.hwu_tab), ("xh", k.xh_tab), ("x1", k.x1_tab), ("xp", k.xp_tab))}

    def rows(n, g):
        return view[n][ds(g, 1)].rearrange("o p t d -> (o p) t d")

    with nc.Block() as block:

        @block.sync
        def _(sp):
            def load(g, h):
                sp.dma_start(u[h], rows("hwu", g)).then_inc(s_ld[h], 16)
                sp.dma_start(xh[h], rows("xh", g)).then_inc(s_ld[h], 16)

            def store(g, h):
                sp.wait_ge(s_x1, g + 1)
                sp.dma_start(rows("x1", g), xh[h]).then_inc(s_st[h], 16)
                sp.wait_ge(s_xp, g + 1)
                sp.dma_start(rows("xp", g), xp[h]).then_inc(s_st[h], 16)

            for h in range(2):
                load(h, h)
            with sp.Fori(0, LAST - 1) as b:
                for h in range(2):
                    store(2 * b + h, h)
                    sp.wait_ge(s_st[h], 32 * b + 32)
                    load(2 * b + 2 + h, h)
            for h in range(2):
                store(2 * LAST - 2 + h, h)
            for h in range(2):
                sp.wait_ge(s_st[h], 32 * LAST)

        @block.scalar
        def _(a):
            with a.Fori(0, LAST) as b:
                for h in range(2):
                    for t in range(NG):
                        n = NG * h + t
                        a.wait_ge(s_ps, 2 * NG * b + n + 1)
                        a.copy(k.ut[n % 2][:, :, :], U3[:, :, ds(2 * NG * P * b + n * P, P)]).then_inc(s_ut, 1)
                    a.wait_ge(s_b, 2 * b + h + 1)
                    nc.scalar.activation(u[h], u[h], ACT.Gelu).then_inc(s_g, 1)

        @block.tensor
        def _(pe):
            pe.sem_inc(s_ps, 2)
            with pe.Fori(0, LAST) as b:
                for n in range(2 * NG):
                    pe.wait_ge(s_ut, 2 * NG * b + n + 1)
                    pe.wait_ge(s_u, 2 * NG * b + n + 1)
                    i = n % 2
                    nc.tensor.matmul(ps[i][:, 0:D], k.ut[i][:, 0, :], k.w2u[:, 0:D], start=True, stop=False)
                    nc.tensor.matmul(ps[i][:, 0:D], k.ut[i][:, 1, :], k.w2u[:, D:2 * D], start=False, stop=False)
                    nc.tensor.matmul(ps[i][:, 0:D], k.ut[i][0:1, 2, :], k.b2u[0:1, :], start=False,
                                     stop=True).then_inc(s_ps, 1)

        @block.gpsimd
        def _(gp):
            with gp.Fori(0, LAST) as b:
                for h in range(2):
                    g = 2 * b + h
                    gp.wait_ge(s_var, 2 * g + 1)
                    gp.tensor_tensor(k.nrs[h][:, 0:NG], k.nvar[h][:, 0:NG], k.neghalf[:, 0:NG], ALU.pow).then_inc(s_rs, 1)
                    gp.wait_ge(s_n, g + 1)
                    gp.tensor_tensor(u[h], u[h], k.beu[:, :].unsqueeze(1).to_broadcast([P, NG, D]), ALU.add).then_inc(s_b, 1)
                    gp.wait_ge(s_g, g + 1)
                    gp.tensor_tensor(xh[h], xh[h], u[h], ALU.add).then_inc(s_x1, 1)
                    gp.wait_ge(s_var, 2 * g + 2)
                    gp.tensor_tensor(k.nrs[h][:, NG:2 * NG], k.nvar[h][:, NG:2 * NG], k.neghalf[:, 0:NG],
                                     ALU.pow).then_inc(s_rs, 1)

        @block.vector
        def _(v):
            K = 6 * NG + 1
            v.sem_inc(s_u, 2)

            def stats(o, x, h, part):
                first = o.n
                for t in range(NG):
                    o(v.bn_stats(k.nst[h][:, t, :], x[:, t, :]))
                for t in range(NG):
                    wait_apart(k, v, s_v, o.base + first + t + 1)
                    o(v.bn_aggr(k.nmv[h][:, NG * part + t, :], k.nst[h][:, t, :]))
                o.wait()
                v.tensor_scalar(k.nvar[h][:, NG * part:NG * part + NG], k.nmv[h][:, NG * part:NG * part + NG, 1],
                                EPS, None, ALU.add).then_inc(s_var, 1)

            with v.Fori(0, LAST) as b:
                o = Order(v, s_v, 2 * K * b)
                for h in range(2):
                    g = 2 * b + h
                    v.wait_ge(s_ld[h], 32 * b + 32)
                    for t in range(NG):
                        n = 2 * NG * b + NG * h + t
                        v.wait_ge(s_ps, n + 3)
                        v.tensor_tensor(u[h][:, t, :], ps[(NG * h + t) % 2][:, 0:D], u[h][:, t, :], ALU.add).then_inc(s_u, 1)
                    v.wait_ge(s_u, 2 * NG * b + NG * (h + 1) + 2)
                    stats(o, u[h], h, 0)
                    v.wait_ge(s_rs, 2 * g + 1)
                    for t in range(NG):
                        o(v.tensor_scalar(u[h][:, t, :], u[h][:, t, :], k.nmv[h][:, t, 0:1], k.nrs[h][:, t:t + 1],
                                          ALU.subtract, ALU.mult))
                    o.wait()
                    v.tensor_tensor(u[h], u[h], k.gu[:, :].unsqueeze(1).to_broadcast([P, NG, D]), ALU.mult).then_inc(s_n, 1)
                    v.wait_ge(s_x1, g + 1)
                    stats(o, xh[h], h, 1)
                    v.wait_ge(s_rs, 2 * g + 2)
                    o(v.tensor_tensor(k.nrs[h][:, NG:2 * NG], k.nrs[h][:, NG:2 * NG], k.dvr[:, ds(NG * g, NG)], ALU.mult))
                    o.wait()
                    v.wait_ge(s_ld[h], 32 * b + 32)
                    for t in range(NG):
                        o(v.tensor_scalar(xp[h][:, t, :], xh[h][:, t, :], k.nmv[h][:, NG + t, 0:1],
                                          k.nrs[h][:, NG + t:NG + t + 1], ALU.subtract, ALU.mult))
                    o.wait()
                    v.tensor_scalar(xp[h], xp[h], 0.0, None, ALU.max).then_inc(s_xp, 1)
                assert o.n == 2 * K, (o.n, 2 * K)



def hyperedge_sums(nc, k):
    s_meta = [k.sem(f"he_indices_loaded{h}") for h in range(2)]
    s_g = [k.sem(f"he_rows_gathered{j}") for j in range(HALF)]
    s_loc = k.sem("he_indices_taken")
    s_oh = k.sem("he_window_masks")
    s_seg = k.sem("he_windows_summed")
    s_u = k.sem("he_windows_kept")
    s_v = k.sem("he_vector_order")
    s_z = k.sem("he_sums_zeroed")
    heT = k.U[:, 0:UCOLS]
    rows = k.stage[:, 0:HALF * D].rearrange("p (j d) -> p j d", d=D)
    psU = [k.psA[:, 0:WIN], k.psC[:, 0:WIN]]

    with nc.Block() as block:

        @block.sync
        def _(sp):
            n_bodies = sp.value_load(k.bounds[0:1, 0:1], min_val=1, max_val=BODIES)

            def load_meta(b, h):
                sp.dma_start(k.meta[h][:, :], k.meta_d[ds(2 * b + h, 1)].rearrange("o p c -> (o p) c"))\
                  .then_inc(s_meta[h], 16)

            for h in range(2):
                load_meta(0, h)
            with sp.Fori(0, n_bodies) as b:
                for h in range(2):
                    sp.wait_ge(s_seg, 8 * b + 4 * h + 8)
                    load_meta(b + 1, h)
            for h in range(2):
                wait_apart(k, sp, s_meta[h], 16 * n_bodies + 16)

        @block.gpsimd
        def _(gp):
            n_bodies = gp.value_load(k.bounds[0:1, 0:1], min_val=1, max_val=BODIES)
            gp.memset(heT, 0.0).then_inc(s_z, 1)
            gp.sem_inc(s_seg, 4)
            with gp.Fori(0, n_bodies) as b:
                for h in range(2):
                    wait_apart(k, gp, s_meta[h], 16 * b + 16)
                    for j in range(HALF):
                        if j % 2 == 0:
                            wait_apart(k, gp, s_seg, 8 * b + 4 * h + j // 2 + 1)
                        gp.indirect_dma_start(out=rows[:, j, :], out_offset=None, in_=k.xp_tab[:, :],
                                              in_offset=bass.IndirectOffsetOnAxis(ap=k.meta[h][:, j:j + 1], axis=0))\
                          .then_inc(s_g[j], 16)

        @block.tensor
        def _(pe):
            n_bodies = pe.value_load(k.bounds[0:1, 0:1], min_val=1, max_val=BODIES)
            pe.sem_inc(s_u, 2)
            with pe.Fori(0, n_bodies) as b:
                for h in range(2):
                    pe.wait_ge(s_oh, 2 * b + h + 1)
                    for q in range(HALF // 2):
                        pe.wait_ge(s_u, 8 * b + 4 * h + q + 1)
                        for i in range(2):
                            j = 2 * q + i
                            pe.wait_ge(s_g[j], 16 * (2 * b + h) + 16)
                            last = nc.tensor.matmul(psU[q % 2], rows[:, j, :], k.oh[h][:, j, :],
                                                    start=i == 0, stop=i == 1)
                        last.then_inc(s_seg, 1)

        @block.vector
        def _(v):
            n_bodies = v.value_load(k.bounds[0:1, 0:1], min_val=1, max_val=BODIES)
            v.wait_ge(s_z, 1)
            with v.Fori(0, n_bodies) as b:
                for h in range(2):
                    v.wait_ge(s_meta[h], 16 * b + 16)
                    dst = k.meta[h][:, HALF:2 * HALF]
                    first = k.firsts[:, ds(8 * b + 4 * h, 4)].unsqueeze(2).to_broadcast([P, 4, 2])
                    v.tensor_tensor(k.local[h][:, :].rearrange("p (a c) -> p a c", c=2),
                                    dst.rearrange("p (a c) -> p a c", c=2), first, ALU.subtract).then_inc(s_loc, 1)
                    v.wait_ge(s_loc, 2 * b + h + 1)
                    v.tensor_tensor(k.oh[h][:, :, :], k.iota[:, 0:WIN].unsqueeze(1).to_broadcast([P, HALF, WIN]),
                                    k.local[h][:, :].unsqueeze(2).to_broadcast([P, HALF, WIN]),
                                    ALU.is_equal).then_inc(s_oh, 1)
                    for q in range(HALF // 2):
                        w = 8 * b + 4 * h + q
                        first = v.value_load(k.firsts[0:1, ds(w, 1)], min_val=0, max_val=N_NODES)
                        v.wait_ge(s_seg, w + 1 + 4)
                        v.wait_ge(s_u, w + 2)
                        v.tensor_tensor(heT[:, ds(first, WIN)], heT[:, ds(first, WIN)], psU[q % 2],
                                        ALU.add).then_inc(s_u, 1)
            wait_apart(k, v, s_u, 8 * n_bodies + 2)


def hyperedge_rows(nc, k):
    s_gp = k.sem("he_product")
    s_gr = k.sem("he_rows_ready")
    s_st = k.sem("he_rows_stored")
    heT = k.U[:, 0:UCOLS]
    g_rows = k.stage[:, 0:HT * D].rearrange("p (t d) -> p t d", d=D)
    psG = [k.psA, k.psB]

    with nc.Block() as block:

        @block.sync
        def _(sp):
            sp.wait_ge(s_gr, HT)
            sp.dma_start(k.g_tab.rearrange("(t p) d -> p t d", p=P), g_rows).then_inc(s_st, 16)
            sp.wait_ge(s_st, 16)

        @block.tensor
        def _(pe):
            for t in range(HT):
                if t >= 2:
                    pe.wait_ge(s_gr, t - 1)
                nc.tensor.matmul(psG[t % 2][:, 0:D], heT[:, t * P:(t + 1) * P], k.lw[:, :], start=True,
                                 stop=True).then_inc(s_gp, 1)

        @block.vector
        def _(v):
            for t in range(HT):
                v.wait_ge(s_gp, t + 1)
                v.tensor_scalar(g_rows[:, t, :], psG[t % 2][:, 0:D], k.w_de[:, t:t + 1], None, ALU.mult).then_inc(s_gr, 1)


def scatter_rows(nc, k):
    s_meta = [k.sem(f"sc_indices_loaded{h}") for h in range(2)]
    s_row = [k.sem(f"sc_sources_loaded{h}") for h in range(2)]
    s_ix = k.sem("sc_indices_ready")
    s_g = [k.sem(f"sc_rows_gathered{j}") for j in range(HALF)]
    s_same = k.sem("sc_same_source")
    s_ps = k.sem("sc_tile_summed")
    s_c = k.sem("sc_rows_copied")
    s_to = k.sem("sc_targets_ready")
    s_sc = [k.sem(f"sc_scattered{r}") for r in range(k.R)]
    s_v = k.sem("sc_vector_order")
    s_sz = k.sem("sc_zeros")
    rows = k.stage[:, 0:HALF * D].rearrange("p (j d) -> p j d", d=D)
    at = HALF * D
    summed = k.stage[:, at:at + k.R * D].rearrange("p (j d) -> p j d", d=D)
    src_row = [k.U[:, i * HALF * P:(i + 1) * HALF * P].bitcast(I32).rearrange("p (j e) -> p j e", e=P)
               for i in range(2)]
    same = k.U[:, 2 * HALF * P:3 * HALF * P].rearrange("p (j e) -> p j e", e=P)
    waste = k.U[:, 3 * HALF * P:4 * HALF * P].rearrange("p (j e) -> p j e", e=P)
    at = 4 * HALF * P
    earlier = k.U[:, at:at + 2 * HALF].rearrange("p (i j) -> p i j", i=2)
    away = k.U[:, at + 2 * HALF:at + 4 * HALF].rearrange("p (i j) -> p i j", i=2)
    ps = [k.psA, k.psB]
    R = k.R

    with nc.Block() as block:

        @block.sync
        def _(sp):
            n_bodies = sp.value_load(k.bounds[0:1, 0:1], min_val=1, max_val=BODIES)

            def load(b, h):
                sp.dma_start(k.meta[h][:, :], k.meta_d[ds(2 * b + h, 1)].rearrange("o p c -> (o p) c"))\
                  .then_inc(s_meta[h], 16)
                sp.dma_start(src_row[h], k.src_d[ds(2 * b + h, 1)].rearrange("o j e -> (o j) e").partition_broadcast(P))\
                  .then_inc(s_row[h], 16)

            for h in range(2):
                load(0, h)
            with sp.Fori(0, n_bodies) as b:
                for h in range(2):
                    sp.wait_ge(s_to, 2 * b + h + 1)
                    load(b + 1, h)
            for h in range(2):
                wait_apart(k, sp, s_meta[h], 16 * n_bodies + 16)
                wait_apart(k, sp, s_row[h], 16 * n_bodies + 16)

        @block.gpsimd
        def _(gp):
            n_bodies = gp.value_load(k.bounds[0:1, 0:1], min_val=1, max_val=BODIES)
            gp.sem_inc(s_ps, HALF)
            gp.memset(summed, 0.0).then_inc(s_sz, 1)
            gp.wait_ge(s_sz, 1)
            for r in range(R):
                gp.dma_start(k.acc[r][NP:NP + P, :], summed[:, r, :]).then_inc(s_sc[r], 16)

            with gp.Fori(0, n_bodies) as b:
                for h in range(2):
                    wait_apart(k, gp, s_ix, 2 * b + h + 1)
                    for j in range(HALF):
                        n = HALF * h + j
                        wait_apart(k, gp, s_ps, BODY * b + n + 1)
                        gp.indirect_dma_start(out=rows[:, j, :], out_offset=None, in_=k.g_tab[:, :],
                                              in_offset=bass.IndirectOffsetOnAxis(ap=k.gidx[h][:, j:j + 1], axis=0))\
                          .then_inc(s_g[j], 16)
                    wait_apart(k, gp, s_to, 2 * b + h + 1)
                    for j in range(HALF):
                        n = HALF * h + j
                        r = j % R
                        wait_apart(k, gp, s_c, BODY * b + n + 3)
                        wait_apart(k, gp, s_sc[r], 16 * (BODY // R * b + n // R) + 16)
                        gp.indirect_dma_start(out=k.acc[r], out_offset=bass.IndirectOffsetOnAxis(
                            ap=k.target[h][:, j:j + 1], axis=0), in_=summed[:, r, :], in_offset=None,
                            compute_op=ALU.add).then_inc(s_sc[r], 16)
            for r in range(R):
                wait_apart(k, gp, s_sc[r], 16 * (BODY // R) * n_bodies + 16)

        @block.tensor
        def _(pe):
            n_bodies = pe.value_load(k.bounds[0:1, 0:1], min_val=1, max_val=BODIES)
            pe.sem_inc(s_c, 2)
            with pe.Fori(0, n_bodies) as b:
                for n in range(BODY):
                    j = n % HALF
                    h = n // HALF
                    if j == 0:
                        pe.wait_ge(s_same, 2 * b + h + 1)
                    pe.wait_ge(s_g[j], 16 * (2 * b + h) + 16)
                    pe.wait_ge(s_c, BODY * b + n + 1)
                    nc.tensor.matmul(ps[n % 2][:, 0:D], same[:, j, :], rows[:, j, :], start=True,
                                     stop=True).then_inc(s_ps, 1)

        @block.scalar
        def _(a):
            n_bodies = a.value_load(k.bounds[0:1, 0:1], min_val=1, max_val=BODIES)
            with a.Fori(0, n_bodies) as b:
                for n in range(BODY):
                    r = n % R
                    a.wait_ge(s_ps, BODY * b + n + 1 + HALF)
                    a.wait_ge(s_sc[r], 16 * (BODY // R * b + n // R) + 16)
                    a.copy(summed[:, r, :], ps[n % 2][:, 0:D]).then_inc(s_c, 1)

        @block.vector
        def _(v):
            n_bodies = v.value_load(k.bounds[0:1, 0:1], min_val=1, max_val=BODIES)
            K = 2 * (2 + 2 * HALF + 3)
            with v.Fori(0, n_bodies) as b:
                o = Order(v, s_v, K * b)
                for h in range(2):
                    v.wait_ge(s_meta[h], 16 * b + 16)
                    src, dst = k.meta[h][:, 0:HALF], k.meta[h][:, HALF:2 * HALF]
                    o(v.tensor_scalar(k.beyond[h][:, :], dst, float(N_HYPER), None, ALU.is_lt))
                    o(v.tensor_scalar(k.gidx[h][:, :], dst, float(N_HYPER - 1), None, ALU.min))
                    o.wait()
                    v.sem_inc(s_ix, 1)
                    v.wait_ge(s_row[h], 16 * b + 16)
                    v.wait_ge(s_ps, BODY * b + HALF * h + HALF)
                    for j in range(HALF):
                        o(v.tensor_scalar(same[:, j, :], src_row[h][:, j, :], src[:, j:j + 1], None, ALU.is_equal))
                    for j in range(HALF):
                        o.wait(o.base + o.n - HALF + 1)
                        o(v.tensor_tensor_reduce(waste[:, j, :], same[:, j, :], k.before[:, :], 1.0, 0.0, ALU.mult,
                                                 ALU.add, earlier[:, h, j:j + 1]))
                    o.wait()
                    v.tensor_tensor(same[:, :, :], same[:, :, :],
                                    k.beyond[h][:, :].unsqueeze(2).to_broadcast([P, HALF, P]),
                                    ALU.mult).then_inc(s_same, 1)
                    o(v.tensor_scalar(earlier[:, h, :], earlier[:, h, :], 1.0, None, ALU.min))
                    o(v.tensor_scalar(away[:, h, :], src, -1.0, k.junk[:, 0:1], ALU.mult, ALU.add))
                    o.wait()
                    o(v.tensor_tensor(away[:, h, :], away[:, h, :], earlier[:, h, :], ALU.mult))
                    o.wait()
                    v.tensor_tensor(k.target[h][:, :], away[:, h, :], src, ALU.add).then_inc(s_to, 1)
                assert o.n == K, (o.n, K)


def output_rows(nc, k):
    s_ld = [k.sem(f"out_loaded{h}") for h in range(2)]
    s_c = k.sem("out_constants")
    s_v = k.sem("out_vector_order")
    s_s = k.sem("out_summed")
    s_o = k.sem("out_ready")
    s_st = [k.sem(f"out_stored{h}") for h in range(2)]
    R = k.R
    W = NG * D

    def grp(i):
        return k.U[:, i * W:(i + 1) * W].rearrange("p (t d) -> p t d", d=D)

    x1 = [grp(0), grp(1)]
    acc = [[grp(2 + R * h + r) for r in range(R)] for h in range(2)]
    g_last = k.U[:, (2 + 2 * R) * W:(2 + 2 * R) * W + D]
    x1_v = k.x1_tab.rearrange("(g t p) d -> g p t d", p=P, t=NG)
    acc_v = [k.acc[r][0:NP, :].rearrange("(g t p) d -> g p t d", p=P, t=NG) for r in range(R)]
    FULL = N_NODES // (NG * P)

    with nc.Block() as block:

        @block.sync
        def _(sp):
            sp.dma_start(g_last, k.g_tab[N_HYPER - 1:N_HYPER, :].partition_broadcast(P)
                         .rearrange("p a d -> p (a d)")).then_inc(s_c, 16)

            def load(g, h):
                sp.dma_start(x1[h], x1_v[ds(g, 1)].rearrange("o p t d -> (o p) t d")).then_inc(s_ld[h], 16)
                for r in range(R):
                    sp.dma_start(acc[h][r], acc_v[r][ds(g, 1)].rearrange("o p t d -> (o p) t d")).then_inc(s_ld[h], 16)

            def store(g, h):
                sp.wait_ge(s_o, g + 1)
                sp.dma_start(k.out[ds(g * NG * P, NG * P), :].rearrange("(t p) d -> p t d", p=P),
                             x1[h]).then_inc(s_st[h], 16)

            for h in range(2):
                load(h, h)
            with sp.Fori(0, NGROUPS // 2 - 1) as b:
                for h in range(2):
                    store(2 * b + h, h)
                    sp.wait_ge(s_st[h], 16 * b + 16)
                    load(2 * b + 2 + h, h)
            store(NGROUPS - 2, 0)
            g = NGROUPS - 1
            whole = (N_NODES - g * NG * P) // P
            rest = N_NODES - g * NG * P - whole * P
            sp.wait_ge(s_o, g + 1)
            sp.dma_start(k.out[g * NG * P:g * NG * P + whole * P, :].rearrange("(t p) d -> p t d", p=P),
                         x1[1][:, 0:whole, :]).then_inc(s_st[1], 16)
            sp.dma_start(k.out[N_NODES - rest:N_NODES, :], x1[1][0:rest, whole, :]).then_inc(s_st[1], 16)
            sp.wait_ge(s_st[0], 16 * (NGROUPS // 2))
            sp.wait_ge(s_st[1], 16 * (NGROUPS // 2) + 16)

        @block.gpsimd
        def _(gp):
            with gp.Fori(0, NGROUPS // 2) as b:
                for h in range(2):
                    gp.wait_ge(s_ld[h], 16 * (1 + R) * (b + 1))
                    gp.tensor_tensor(x1[h], x1[h], k.lb[:, :].unsqueeze(1).to_broadcast([P, NG, D]), ALU.add).then_inc(s_s, 1)

        @block.vector
        def _(v):
            K = 2 * (R - 1 + NG)
            v.wait_ge(s_c, 16)
            with v.Fori(0, NGROUPS // 2) as b:
                o = Order(v, s_v, K * b)
                for h in range(2):
                    g = 2 * b + h
                    v.wait_ge(s_ld[h], 16 * (1 + R) * (b + 1))
                    for r in range(1, R):
                        o(v.tensor_tensor(acc[h][0], acc[h][0], acc[h][r], ALU.add))
                        o.wait()
                    for t in range(NG):
                        o(v.scalar_tensor_tensor(acc[h][0][:, t, :], g_last, k.beyond_count[:, ds(NG * g + t, 1)],
                                                 acc[h][0][:, t, :], ALU.mult, ALU.add))
                    v.wait_ge(s_s, g + 1)
                    o.wait()
                    for t in range(NG):
                        last = v.scalar_tensor_tensor(x1[h][:, t, :], acc[h][0][:, t, :], k.dvr[:, ds(NG * g + t, 1)],
                                                      x1[h][:, t, :], ALU.mult, ALU.add)
                    last.then_inc(s_o, 1)
                assert o.n == K, (o.n, K)




PHASES = (setup_phase, node_tables, edge_messages, far_messages, hyper_degrees, node_update,
          hyperedge_sums, far_hyperedges, hyperedge_rows, scatter_rows, output_rows)


def message_passing(nc, k):
    for phase in PHASES:
        taken = []

        def sem(name):
            taken.append(nc.alloc_semaphore(name=name))
            return taken[-1]

        k.sem = sem
        phase(nc, k)
        nc.clear_and_free_semaphores(taken)
        nc.all_engine_barrier()


def program(nc, dram):
    with ExitStack() as ctx:
        k = Places(dram)

        def sb(name, shape, dt=F32):
            return ctx.enter_context(nc.sbuf_tensor(name, shape, dt))

        def pair(name, shape, dt=F32, n=2):
            return [sb(f"{name}{i}", shape, dt) for i in range(n)]

        k.R = 4
        k.s_apart = ctx.enter_context(nc.semaphore('waits_taken_apart'))
        k.U = sb("sums", [P, 3 * UCOLS])
        k.stage = sb("stage", [P, 6 * NG * D + 6 * P])
        k.firsts = sb("window_starts", [P, PAIRS], I32)
        k.bounds = sb("loop_bounds", [1, 4], I32)
        k.w0 = sb("table_weights", [P, HID + D])
        k.bias0 = sb("table_bias", [P, HID + D])
        k.w1b = sb("edge_weights", [DE, HID])
        k.g1, k.be1 = sb("g1", [P, HID]), sb("be1", [P, HID])
        k.gu, k.beu = sb("gu", [P, D]), sb("beu", [P, D])
        k.w2u, k.b2u = sb("w2u", [P, 2 * D]), sb("b2u", [1, D])
        k.lw, k.lb = sb("lw", [P, D]), sb("lb", [P, D])
        k.ident, k.before, k.ones = sb("identity", [P, P]), sb("before", [P, P]), sb("ones", [P, P])
        k.iota, k.iotab = sb("iota", [P, P]), sb("iota_bf16", [P, P], BF16)
        k.zerob = sb("zeros_bf16", [P, P], BF16)
        k.junk = sb("spare_rows", [P, 1])
        k.neghalf = sb("minus_half", [P, NT])
        k.meta = pair("indices", [P, 2 * HALF], I32)
        k.ea = pair("edge_features", [DE, GROUP * P], n=4)
        k.local, k.beyond = pair("local", [P, HALF]), pair("beyond", [P, HALF])
        k.bits, k.digits = pair("bits", [P, 4 * HALF], I32), pair("digits", [P, 4 * HALF])
        k.src_lo, k.src_hi, k.dst_lo, k.dst_hi = ([d[:, i * HALF:(i + 1) * HALF] for d in k.digits] for i in range(4))
        k.gidx, k.target = pair("hyper_index", [P, HALF], I32), pair("target", [P, HALF], I32)
        k.w_row, k.w_act = pair("w_row", [P, HALF]), pair("w_act", [P, HALF])
        k.oh = pair("window_mask", [P, HALF, WIN])
        k.ohb, k.oha = pair("mask_lo_bf16", [P, P], BF16, 4), pair("mask_hi_bf16", [P, NT], BF16, 4)
        k.scratch = sb("scratch", [P, GROUP, HID], BF16)
        k.ssq, k.var, k.rstd = pair("ssq", [P, GROUP]), pair("var", [P, GROUP]), pair("rstd", [P, GROUP])
        k.beyond_count, k.dvr = sb("beyond_count", [P, NT]), sb("dvr", [P, NT])
        k.w_last, k.w_pt, k.w_de = sb("w_last", [P, 1]), sb("w_pt", [P, HT]), sb("w_de", [P, HT])
        k.nst, k.nmv = pair("nst", [P, NG, 6]), pair("nmv", [P, 2 * NG, 2])
        k.nvar, k.nrs = pair("nvar", [P, 2 * NG]), pair("nrs", [P, 2 * NG])
        k.mask_lo = [k.stage[:, i * P:(i + 1) * P] for i in range(2)]
        k.mask_hi = [k.stage[:, (2 + i) * P:(3 + i) * P] for i in range(2)]
        k.ut = [k.stage[:, 6 * NG * D + 3 * P * i:6 * NG * D + 3 * P * (i + 1)].rearrange("p (c n) -> p c n", c=3)
                for i in range(2)]

        def pb(name, cols):
            return ctx.enter_context(nc.psum_tensor(name, [P, cols], F32))

        k.psH = [pb("ps_tiles0", GROUP * HID), pb("ps_tiles1", GROUP * HID)]
        k.psA, k.psB, k.psC = pb("ps_a", 512), pb("ps_b", 512), pb("ps_c", 512)
        message_passing(nc, k)


def kernel(**inputs):
    import numpy as np
    import concourse.bacc as bacc
    from concourse.bass_utils import run_bass_kernel_spmd

    def padded(a, n, fill):
        a = np.asarray(a)
        return np.concatenate([a, np.full((n - a.shape[0],) + a.shape[1:], fill, a.dtype)])

    slots = (TILES + BODY) * P
    src = padded(inputs["src"], slots, N_NODES).reshape(-1, HALF, P)
    dst = padded(inputs["dst"], slots, FAR).reshape(-1, HALF, P)
    first = padded(np.asarray(inputs["dst"])[::2 * P], PAIRS + 8, N_NODES)[:PAIRS]
    ea = padded(inputs["edge_attr_32"], TILES * P, 0).reshape(TILES, P, DE)
    w = padded(inputs["L1_gnn_hyperedge_weight"], HP, 0)
    arrays = {
        "x": padded(inputs["x"], NP, 0),
        "meta_d": np.concatenate([src.transpose(0, 2, 1), dst.transpose(0, 2, 1)], axis=2),
        "src_d": src,
        "src_tiles": src.reshape(-1, P, 1), "dst_tiles": dst.reshape(-1, P, 1),
        "dst_pt": dst.reshape(-1, P)[:TILES].T,
        "pair_first": first,
        "ea_d": ea.transpose(0, 2, 1),
        "W1": inputs["L0_gnn_W1"], "b1": inputs["L0_gnn_b1"], "g1_d": inputs["L0_gnn_g1"],
        "be1_d": inputs["L0_gnn_be1"], "W2T": np.asarray(inputs["L0_gnn_W2"]).T, "b2": inputs["L0_gnn_b2"],
        "Wu": inputs["L0_gnn_Wu"], "bu": inputs["L0_gnn_bu"], "gu_d": inputs["L0_gnn_gu"],
        "beu_d": inputs["L0_gnn_beu"], "w_d": w.reshape(HP, 1), "w_pt_d": w.reshape(HT, P).T,
        "LWT": np.asarray(inputs["L1_gnn_W"]).T, "lb_d": inputs["L1_gnn_b"],
    }
    arrays = {n: np.ascontiguousarray(a) for n, a in arrays.items()}
    nc = bacc.Bacc("TRN2", target_bir_lowering=False, num_devices=1)
    dram = {n: nc.dram_tensor(n, a.shape, mybir.dt.from_np(a.dtype), kind="ExternalInput").ap()
            for n, a in arrays.items()}
    for name, cols in (("p_tab", HID), ("hwu_tab", D), ("xh_tab", D), ("x1_tab", D), ("xp_tab", D)):
        dram[name] = nc.dram_tensor(name, (NP, cols), F32).ap()
    dram["g_tab"] = nc.dram_tensor("g_tab", (HP, D), F32).ap()
    dram["acc"] = [nc.dram_tensor(f"acc{r}", (NP + P, D), F32).ap() for r in range(4)]
    dram["out"] = nc.dram_tensor("out", (N_NODES, D), F32, kind="ExternalOutput").ap()
    program(nc, dram)
    return run_bass_kernel_spmd(nc, [arrays], core_ids=[0]).results[0]["out"]
```

```python
import concourse.bass as bass
from concourse import mybir
from contextlib import ExitStack

F32 = mybir.dt.float32
BF16 = mybir.dt.bfloat16
I32 = mybir.dt.int32
ALU = mybir.AluOpType
ACT = mybir.ActivationFunctionType
AXX = mybir.AxisListType.X
ds = bass.ds

P = 128
N_NODES, N_EDGES, N_HYPER = 12500, 200000, 2500
D, HID, DE = 128, 256, 32
EPS = 1e-5
GROUP = 4
HALF = 2 * GROUP
BODY = 2 * HALF
TILES = -(-N_EDGES // (P * BODY)) * BODY
BODIES = TILES // BODY
PAIRS = TILES // 2
WIN = 32
NT = -(-N_NODES // P)
NP = NT * P
UCOLS = max(N_NODES + WIN, NP)
NG = 7
NGROUPS = NT // NG
HT = -(-N_HYPER // P)
HP = HT * P
EA_A = ((0, 0), (0, 1), (0, 2), (1, 0))
EA_B = ((1, 1), (2, 0))
FAR_COLS = NP // 32
FAR_CHUNKS = NP // FAR_COLS
FAR_HCHUNKS = -(-HP // FAR_COLS)
FAR = 1 << 20
assert FAR_COLS <= 512 and FAR_CHUNKS * FAR_COLS == NP
assert NT % (2 * NG) == 0 and TILES % BODY == 0


class Places:

    def __init__(self, dram):
        self.x, self.meta_d, self.src_d = dram["x"], dram["meta_d"], dram["src_d"]
        self.src_tiles, self.dst_tiles, self.dst_pt = dram["src_tiles"], dram["dst_tiles"], dram["dst_pt"]
        self.pair_first, self.ea_d, self.W1 = dram["pair_first"], dram["ea_d"], dram["W1"]
        self.b1, self.g1_d, self.be1_d = dram["b1"], dram["g1_d"], dram["be1_d"]
        self.W2T, self.b2, self.Wu = dram["W2T"], dram["b2"], dram["Wu"]
        self.bu, self.gu_d, self.beu_d = dram["bu"], dram["gu_d"], dram["beu_d"]
        self.w_d, self.w_pt_d, self.LWT = dram["w_d"], dram["w_pt_d"], dram["LWT"]
        self.lb_d, self.p_tab, self.hwu_tab = dram["lb_d"], dram["p_tab"], dram["hwu_tab"]
        self.xh_tab, self.x1_tab, self.xp_tab = dram["xh_tab"], dram["x1_tab"], dram["xp_tab"]
        self.ea_parts, self.g_tab, self.src_pt = dram["ea_parts"], dram["g_tab"], dram["src_pt"]
        self.acc, self.out, self.digit_tab = dram["acc"], dram["out"], dram["digit_tab"]


def wait_apart(k, eng, sem, value):
    eng.wait_ge(sem, value)
    eng.sem_inc(k.s_apart, 1)


class Order:

    def __init__(self, eng, sem, base=0):
        self.eng, self.sem, self.base, self.n = eng, sem, base, 0

    def __call__(self, ins):
        ins.then_inc(self.sem, 1)
        self.n += 1
        return self.base + self.n

    def wait(self, value=None):
        self.eng.wait_ge(self.sem, self.base + self.n if value is None else value)



def setup_phase(nc, k):
    s_w = k.sem("weights_loaded")
    s_d = k.sem("dst_loaded")
    s_iota = k.sem("pool_constants")
    s_v = k.sem("setup_vector_order")
    s_fold = k.sem("folded_products")
    s_row = k.sem("row_maxima")
    s_z = k.sem("setup_tables_written")
    s_dig = k.sem("digits_ready")
    s_wp = k.sem("edge_weight_parts")
    s_parts = k.sem("edge_weights_stacked")
    NW = 14
    dst_all = k.U[:, 0:TILES].bitcast(I32)
    active = k.U[:, TILES:2 * TILES]
    reach = k.U[:, 2 * TILES:3 * TILES]
    tile_no = k.U[:, 3 * TILES:4 * TILES]
    local = k.U[:, 4 * TILES:5 * TILES]
    low = k.U[:, 5 * TILES:6 * TILES]
    w2t = k.U[:, 6 * TILES:6 * TILES + HID]
    wu_bot = k.U[:, 6 * TILES + HID:6 * TILES + HID + D]
    b2col = k.U[:, 6 * TILES + HID + D:6 * TILES + HID + D + 1]
    most = k.U[:, 6 * TILES + HID + D + 2:6 * TILES + HID + D + 4]
    mean = k.U[:, 6 * TILES + HID + D + 4:6 * TILES + HID + D + 7]
    rowmax = k.U[0:1, 6 * TILES + HID + D + 8:6 * TILES + HID + D + 16]
    w_part = k.U[0:DE, 6 * TILES + HID + D + 16:6 * TILES + HID + D + 16 + 3 * HID // 2].bitcast(BF16)\
        .rearrange("p (m d) -> p m d", d=HID)
    w_rest = k.U[0:DE, 6 * TILES + 3 * HID + D + 16:6 * TILES + 4 * HID + D + 16]
    zero = k.U[:, 7 * TILES:7 * TILES + NT * D // 2]
    at = 7 * TILES + NT * D // 2
    src_all, low_bits, high_bits = (k.U[:, at + i * TILES:at + (i + 1) * TILES].bitcast(I32) for i in range(3))
    at += 3 * TILES
    digits = k.U[:, at:at + 3 * TILES].rearrange("p (h d j) -> p h d j", d=3, j=HALF)
    with nc.Block() as block:

        @block.sync
        def _(sp):
            sp.dma_start(dst_all, k.dst_pt).then_inc(s_d, 16)
            sp.dma_start(src_all, k.src_pt).then_inc(s_d, 16)
            sp.dma_start(k.firsts[:, :], k.pair_first.partition_broadcast(P)).then_inc(s_d, 16)
            sp.dma_start(k.w0[:, 0:HID], k.W1[0:D, :]).then_inc(s_w, 16)
            sp.dma_start(k.w0[:, HID:HID + D], k.Wu[0:D, :]).then_inc(s_w, 16)
            sp.dma_start(k.w1b[:, :], k.W1[D:D + DE, :]).then_inc(s_w, 16)
            sp.dma_start(k.bias0[:, 0:HID], k.b1.partition_broadcast(P)).then_inc(s_w, 16)
            sp.dma_start(k.bias0[:, HID:HID + D], k.bu.partition_broadcast(P)).then_inc(s_w, 16)
            sp.dma_start(k.g1[:, :], k.g1_d.partition_broadcast(P)).then_inc(s_w, 16)
            sp.dma_start(k.be1[:, :], k.be1_d.partition_broadcast(P)).then_inc(s_w, 16)
            sp.dma_start(k.gu[:, :], k.gu_d.partition_broadcast(P)).then_inc(s_w, 16)
            sp.dma_start(k.beu[:, :], k.beu_d.partition_broadcast(P)).then_inc(s_w, 16)
            sp.dma_start(w2t, k.W2T).then_inc(s_w, 16)
            sp.dma_start(wu_bot, k.Wu[D:2 * D, :]).then_inc(s_w, 16)
            sp.dma_start(b2col, k.b2.rearrange("(p o) -> p o", o=1)).then_inc(s_w, 16)
            sp.dma_start(k.lw[:, :], k.LWT).then_inc(s_w, 16)
            sp.dma_start(k.lb[:, :], k.lb_d.partition_broadcast(P)).then_inc(s_w, 16)
            sp.wait_ge(s_iota, 2)
            n = 0
            for r in range(k.R):
                t = k.acc[r][0:NP, :].rearrange("(c p t) d -> c p (t d)", c=2, p=P)
                for c in range(2):
                    sp.dma_start(t[c], zero).then_inc(s_z, 16)
                    n += 16
            sp.wait_ge(s_dig, 1)
            sp.dma_start(k.digit_tab.rearrange("p h c -> p (h c)"),
                         digits.rearrange("p h d j -> p (h d j)")).then_inc(s_z, 16)
            n += 16
            sp.wait_ge(s_wp, 1)
            for to, blocks in ((k.wA, EA_A), (k.wB, EA_B)):
                for i, (_, m) in enumerate(blocks):
                    sp.dma_start(to[DE * i:DE * (i + 1), :], w_part[:, m, :]).then_inc(s_parts, 16)
            sp.wait_ge(s_parts, 16 * len(EA_A + EA_B))
            sp.wait_ge(s_z, n)

        @block.gpsimd
        def _(gp):
            gp.memset(k.neghalf[:, :], -0.5).then_inc(s_iota, 1)
            gp.memset(zero, 0.0).then_inc(s_iota, 1)
            gp.memset(k.ident[:, :], 0.0).then_inc(s_iota, 1)
            gp.memset(k.before[:, :], 1.0).then_inc(s_iota, 1)
            gp.memset(k.ones[:, :], 1.0).then_inc(s_iota, 1)
            gp.memset(k.ones_bf[:, :], 1.0).then_inc(s_iota, 1)
            gp.memset(k.zerob[:, :], 0.0).then_inc(s_iota, 1)
            gp.iota(k.iota[:, :], [[1, P]], base=0, channel_multiplier=0,
                    allow_small_or_imprecise_dtypes=True).then_inc(s_iota, 1)
            gp.iota(k.iotab[:, :], [[1, P]], base=0, channel_multiplier=0,
                    allow_small_or_imprecise_dtypes=True).then_inc(s_iota, 1)
            gp.iota(k.junk[:, :], [[0, 1]], base=NP, channel_multiplier=1,
                    allow_small_or_imprecise_dtypes=True).then_inc(s_iota, 1)
            gp.iota(tile_no, [[1, TILES]], base=1, channel_multiplier=0,
                    allow_small_or_imprecise_dtypes=True).then_inc(s_iota, 1)
            gp.wait_ge(s_iota, 11)
            gp.affine_select(out=k.ident[:, :], in_=k.ident[:, :], compare_op=ALU.not_equal, fill=1.0,
                             base=0, pattern=[[-1, P]], channel_multiplier=1).then_inc(s_iota, 1)
            gp.affine_select(out=k.before[:, :], in_=k.before[:, :], compare_op=ALU.is_ge, fill=0.0,
                             base=-1, pattern=[[-1, P]], channel_multiplier=1).then_inc(s_iota, 1)

        @block.vector
        def _(v):
            o = Order(v, s_v)
            v.wait_ge(s_iota, 13)
            v.wait_ge(s_d, 48)
            o(v.tensor_scalar(active, dst_all, float(N_HYPER), None, ALU.is_lt))
            firsts = k.firsts[:, :].unsqueeze(2).to_broadcast([P, PAIRS, 2])
            o(v.tensor_tensor(local.rearrange("p (a b) -> p a b", b=2),
                              dst_all.rearrange("p (a b) -> p a b", b=2), firsts, ALU.subtract))
            o.wait()
            o(v.tensor_copy(digits[:, :, 0, :], local.rearrange("p (h j) -> p h j", j=HALF)))
            o(v.tensor_scalar(low_bits, src_all, P - 1, None, ALU.bitwise_and))
            o(v.tensor_scalar(high_bits, src_all, P.bit_length() - 1, None, ALU.logical_shift_right))
            o.wait()
            o(v.tensor_copy(digits[:, :, 1, :], low_bits.rearrange("p (h j) -> p h j", j=HALF)))
            o(v.scalar_tensor_tensor(digits[:, :, 2, :], active.rearrange("p (h j) -> p h j", j=HALF), -4.0 * P,
                                     high_bits.rearrange("p (h j) -> p h j", j=HALF), ALU.mult, ALU.subtract))
            o(v.tensor_tensor(reach, active, tile_no, ALU.mult))
            o(v.tensor_scalar(low, local, 0.0, None, ALU.is_lt))
            o.wait()
            o(v.tensor_reduce(most[:, 0:1], reach, AXX, ALU.max))
            o(v.tensor_scalar(local, local, float(WIN), None, ALU.is_ge))
            o.wait()
            o(v.tensor_tensor(low, low, local, ALU.max))
            o(v.tensor_scalar(active, dst_all, float(N_NODES), None, ALU.is_lt))
            o.wait()
            o(v.tensor_tensor(low, low, active, ALU.mult))
            o.wait()
            o(v.tensor_reduce(most[:, 1:2], low, AXX, ALU.max))
            o.wait()
            v.sem_inc(s_row, 1)
            v.sem_inc(s_dig, 1)
            v.wait_ge(s_w, 16 * NW)
            o(v.tensor_reduce(mean[:, 0:1], k.w0[:, 0:HID], AXX, ALU.add))
            o(v.tensor_reduce(mean[0:DE, 1:2], k.w1b[:, :], AXX, ALU.add))
            o(v.tensor_reduce(mean[:, 2:3], k.bias0[:, 0:HID], AXX, ALU.add))
            o.wait()
            o(v.tensor_scalar(mean[:, 0:3:2], mean[:, 0:3:2], 1.0 / HID, None, ALU.mult))
            o(v.tensor_scalar(mean[0:DE, 1:2], mean[0:DE, 1:2], 1.0 / HID, None, ALU.mult))
            o.wait()
            o(v.tensor_scalar(k.w0[:, 0:HID], k.w0[:, 0:HID], mean[:, 0:1], None, ALU.subtract))
            o(v.tensor_scalar(k.w1b[:, :], k.w1b[:, :], mean[0:DE, 1:2], None, ALU.subtract))
            o(v.tensor_scalar(k.bias0[:, 0:HID], k.bias0[:, 0:HID], mean[:, 2:3], None, ALU.subtract))
            o.wait()
            o(v.tensor_copy(w_part[:, 0, :], k.w1b[:, :]))
            o.wait()
            o(v.tensor_tensor(w_rest, k.w1b[:, :], w_part[:, 0, :], ALU.subtract))
            o.wait()
            o(v.tensor_copy(w_part[:, 1, :], w_rest))
            o.wait()
            o(v.tensor_tensor(w_part[:, 2, :], w_rest, w_part[:, 1, :], ALU.subtract))
            o.wait()
            v.sem_inc(s_wp, 1)
            v.wait_ge(s_row, 2)
            o(v.tensor_reduce(rowmax[:, 0:1], k.psA[0:1, 0:P], AXX, ALU.max))
            o(v.tensor_reduce(rowmax[:, 1:2], k.psA[0:1, P:2 * P], AXX, ALU.max))
            o.wait()
            o(v.tensor_scalar(k.bounds[:, 0:1], rowmax[:, 0:1], float(BODY - 1), float(BODY), ALU.add, ALU.max))
            for i, most_trips in ((1, PAIRS), (2, FAR_CHUNKS), (3, FAR_HCHUNKS)):
                o(v.tensor_scalar(k.bounds[:, i:i + 1], rowmax[:, 1:2], float(most_trips - 1), 1.0, ALU.mult, ALU.add))
            o.wait()
            o(v.tensor_scalar(k.bounds[:, 0:1], k.bounds[:, 0:1], BODY.bit_length() - 1, None,
                              ALU.logical_shift_right))
            v.wait_ge(s_fold, 1)
            o(v.tensor_copy(k.w2u[:, 0:D], k.psB[:, 0:D]))
            o(v.tensor_copy(k.w2u[:, D:2 * D], k.psB[:, D:2 * D]))
            o(v.tensor_copy(k.b2u[0:1, :], k.psB[0:1, 2 * D:3 * D]))
            o.wait()

        @block.tensor
        def _(pe):
            pe.wait_ge(s_iota, 13)
            pe.wait_ge(s_row, 1)
            nc.tensor.matmul(k.psA[0:1, 0:P], most[:, 0:1], k.ident[:, :], start=True, stop=True)
            nc.tensor.matmul(k.psA[0:1, P:2 * P], most[:, 1:2], k.ident[:, :], start=True,
                             stop=True).then_inc(s_row, 1)
            pe.wait_ge(s_w, 16 * NW)
            nc.tensor.matmul(k.psB[:, 0:D], w2t[:, 0:D], wu_bot, start=True, stop=True)
            nc.tensor.matmul(k.psB[:, D:2 * D], w2t[:, D:2 * D], wu_bot, start=True, stop=True)
            nc.tensor.matmul(k.psB[0:1, 2 * D:3 * D], b2col, wu_bot, start=True, stop=True).then_inc(s_fold, 1)


def node_tables(nc, k):
    s_x = [k.sem(f"x_loaded{h}") for h in range(2)]
    s_var = k.sem("x_variance")
    s_rstd = k.sem("x_rstd")
    s_h = k.sem("h_ready")
    s_xh = k.sem("xh_ready")
    s_t = k.sem("hT_in_psum")
    s_hT = k.sem("hT_ready")
    s_p = k.sem("table_product")
    s_pw = k.sem("table_rows_ready")
    s_st = [k.sem(f"tables_stored{h}") for h in range(2)]
    s_xs = [k.sem(f"xh_stored{h}") for h in range(2)]
    s_v = k.sem("tables_vector_order")
    at = [0]

    def take(n):
        at[0] += n
        return k.U[:, at[0] - n:at[0]]

    xg = [take(NG * D).rearrange("p (t d) -> p t d", d=D) for _ in range(2)]
    hg = [take(NG * D).rearrange("p (t d) -> p t d", d=D) for _ in range(2)]
    xh = [take(NG * D).rearrange("p (t d) -> p t d", d=D) for _ in range(2)]
    rows = [take(NG * (HID + D)).rearrange("p (t d) -> p t d", d=HID + D) for _ in range(2)]
    hT = [take(P) for _ in range(2)]
    stats = [take(NG * 6).rearrange("p (t d) -> p t d", d=6) for _ in range(2)]
    mv = [take(NG * 2).rearrange("p (t d) -> p t d", d=2) for _ in range(2)]
    var = [take(NG) for _ in range(2)]
    rstd = [take(NG) for _ in range(2)]
    psT = [k.psA, k.psB]
    psP = [k.psH[0], k.psH[1]]
    x_v = k.x.rearrange("(g t p) d -> g p t d", p=P, t=NG)
    xh_v = k.xh_tab.rearrange("(g t p) d -> g p t d", p=P, t=NG)
    p_v = k.p_tab.rearrange("(g t p) d -> g p t d", p=P, t=NG)
    hwu_v = k.hwu_tab.rearrange("(g t p) d -> g p t d", p=P, t=NG)
    LAST = NGROUPS // 2 - 1

    with nc.Block() as block:

        @block.sync
        def _(sp):
            def load(g, h):
                sp.dma_start(xg[h], x_v[ds(g, 1)].rearrange("o p t d -> (o p) t d")).then_inc(s_x[h], 16)

            def store(g, h):
                sp.wait_ge(s_xh, g + 1)
                sp.dma_start(xh_v[ds(g, 1)].rearrange("o p t d -> (o p) t d"), xh[h]).then_inc(s_xs[h], 16)
                sp.wait_ge(s_pw, NG * (g + 1))
                sp.dma_start(p_v[ds(g, 1)].rearrange("o p t d -> (o p) t d"),
                             rows[h][:, :, 0:HID]).then_inc(s_st[h], 16)
                sp.dma_start(hwu_v[ds(g, 1)].rearrange("o p t d -> (o p) t d"),
                             rows[h][:, :, HID:HID + D]).then_inc(s_st[h], 16)

            for h in range(2):
                sp.sem_inc(s_st[h], 32)
                sp.sem_inc(s_xs[h], 16)
                load(h, h)
            with sp.Fori(0, LAST) as b:
                for h in range(2):
                    sp.wait_ge(s_xh, 2 * b + h + 1)
                    load(2 * b + 2 + h, h)
                    store(2 * b + h, h)
            for h in range(2):
                store(2 * LAST + h, h)
            for h in range(2):
                sp.wait_ge(s_st[h], 32 * (LAST + 2))
                sp.wait_ge(s_xs[h], 16 * (LAST + 2))

        @block.gpsimd
        def _(gp):
            with gp.Fori(0, LAST + 1) as b:
                for h in range(2):
                    g = 2 * b + h
                    gp.wait_ge(s_var, g + 1)
                    gp.tensor_tensor(rstd[h], var[h], k.neghalf[:, 0:NG], ALU.pow).then_inc(s_rstd, 1)
                    gp.wait_ge(s_h, g + 1)
                    gp.wait_ge(s_xs[h], 16 * b + 16)
                    gp.tensor_tensor(xh[h], xg[h], hg[h], ALU.add).then_inc(s_xh, 1)

        @block.vector
        def _(v):
            K = 3 * NG

            def products(g, h):
                v.wait_ge(s_st[h], 16 * (g - h) + 32)
                for t in range(NG):
                    v.wait_ge(s_p, NG * g + t + 1 + 2)
                    v.tensor_tensor(rows[h][:, t, :], psP[(NG * h + t) % 2][:, 0:HID + D], k.bias0[:, :],
                                    ALU.add).then_inc(s_pw, 1)

            def slot(g, h, prev):
                o = Order(v, s_v, K * g)
                v.wait_ge(s_x[h], 8 * (g - h) + 16)
                for t in range(NG):
                    o(v.bn_stats(stats[h][:, t, :], xg[h][:, t, :]))
                for t in range(NG):
                    wait_apart(k, v, s_v, o.base + t + 1)
                    o(v.bn_aggr(mv[h][:, t, :], stats[h][:, t, :]))
                o.wait()
                v.tensor_scalar(var[h], mv[h][:, :, 1], EPS, None, ALU.add).then_inc(s_var, 1)
                if prev:
                    products(g - 1, 1 - h)
                    if not isinstance(g, int) or g >= 2:
                        v.wait_ge(s_xh, g - 1)
                v.wait_ge(s_rstd, g + 1)
                for t in range(NG):
                    o(v.tensor_scalar(hg[h][:, t, :], xg[h][:, t, :], mv[h][:, t, 0:1], rstd[h][:, t:t + 1],
                                      ALU.subtract, ALU.mult))
                o.wait()
                v.tensor_scalar(hg[h], hg[h], 0.0, None, ALU.max).then_inc(s_h, 1)

            slot(0, 0, False)
            slot(1, 1, True)
            with v.Fori(1, LAST + 1) as b:
                for h in range(2):
                    slot(2 * b + h, h, True)
            products(2 * LAST + 1, 1)

        @block.scalar
        def _(a):
            with a.Fori(0, LAST + 1) as b:
                for n in range(2 * NG):
                    a.wait_ge(s_t, 2 * NG * b + n + 1)
                    a.wait_ge(s_p, 2 * NG * b + n + 1)
                    a.copy(hT[n % 2], psT[n % 2][:, 0:P]).then_inc(s_hT, 1)

        @block.tensor
        def _(pe):
            pe.sem_inc(s_p, 2)

            def transpose(b, n):
                h, t = divmod(n, NG)
                if t == 0:
                    pe.wait_ge(s_h, 2 * b + h + 1)
                if isinstance(b, int) and 2 * NG * b + n < 2:
                    pass
                else:
                    pe.wait_ge(s_hT, 2 * NG * b + n - 1)
                nc.tensor.transpose(psT[n % 2][:, 0:P], hg[h][:, t, :], k.ident[:, :]).then_inc(s_t, 1)

            def product(b, n, first=False):
                pe.wait_ge(s_hT, 2 * NG * b + n + 1)
                if not (isinstance(b, int) and 2 * NG * b + n < 2):
                    pe.wait_ge(s_pw, 2 * NG * b + n - 1)
                nc.tensor.matmul(psP[n % 2][:, 0:HID + D], hT[n % 2], k.w0[:, :], start=True,
                                 stop=True).then_inc(s_p, 1)

            def body(b):
                for n in range(2 * NG):
                    transpose(b, n)
                    if n % NG:
                        product(b, n - 1)
                    if n % NG == NG - 1:
                        product(b, n)

            body(0)
            with pe.Fori(1, LAST + 1) as b:
                body(b)



def edge_parts(nc, k):
    s_ld = [k.sem(f"features_loaded{i}") for i in range(2)]
    s_hi = k.sem("features_high")
    s_r = k.sem("features_rest")
    s_mid = k.sem("features_middle")
    s_lo = k.sem("features_low")
    s_st = [k.sem(f"features_stored{i}") for i in range(2)]
    CH = 16
    C = TILES * DE // CH
    flat = k.ea_d.rearrange("a f e -> (a f e)").rearrange("(p c) -> p c", p=P)
    out = [t.rearrange("a f e -> (a f e)").rearrange("(p c) -> p c", p=P) for t in k.ea_parts]
    full = [k.U[:, i * C:(i + 1) * C] for i in range(2)]
    rest = [k.U[:, (2 + i) * C:(3 + i) * C] for i in range(2)]
    half = k.U[:, 4 * C:7 * C].bitcast(BF16)
    part = [[half[:, (3 * i + n) * C:(3 * i + n + 1) * C] for n in range(3)] for i in range(2)]
    LAST = CH // 2

    with nc.Block() as block:

        @block.sync
        def _(sp):
            def load(c, i):
                sp.dma_start(full[i], flat[:, ds(c * C, C)]).then_inc(s_ld[i], 16)

            def store(c, i):
                wait_apart(k, sp, s_lo, c + 1)
                for n in range(3):
                    sp.dma_start(out[n][:, ds(c * C, C)], part[i][n]).then_inc(s_st[i], 16)

            for i in range(2):
                sp.sem_inc(s_st[i], 48)
                load(i, i)
            with sp.Fori(0, LAST - 1) as b:
                for i in range(2):
                    wait_apart(k, sp, s_lo, 2 * b + i + 1)
                    load(2 * b + 2 + i, i)
                    store(2 * b + i, i)
            for i in range(2):
                store(CH - 2 + i, i)
            for i in range(2):
                sp.wait_ge(s_st[i], 48 * (LAST + 1))

        @block.scalar
        def _(a):
            with a.Fori(0, LAST) as b:
                for i in range(2):
                    c = 2 * b + i
                    a.wait_ge(s_ld[i], 16 * b + 16)
                    a.wait_ge(s_st[i], 48 * b + 48)
                    a.copy(part[i][0], full[i]).then_inc(s_hi, 1)
                    a.wait_ge(s_r, c + 1)
                    a.copy(part[i][1], rest[i]).then_inc(s_mid, 1)

        @block.vector
        def _(v):
            with v.Fori(0, LAST) as b:
                for i in range(2):
                    c = 2 * b + i
                    v.wait_ge(s_hi, c + 1)
                    v.tensor_tensor(rest[i], full[i], part[i][0], ALU.subtract).then_inc(s_r, 1)
                    v.wait_ge(s_mid, c + 1)
                    v.tensor_tensor(part[i][2], rest[i], part[i][1], ALU.subtract).then_inc(s_lo, 1)


def edge_messages(nc, k):
    s_meta = [k.sem(f"indices_loaded{h}") for h in range(2)]
    s_ea = [k.sem(f"edge_features_loaded{h}") for h in range(2)]
    s_g = [k.sem(f"rows_gathered{j}") for j in range(HALF)]
    s_tile = k.sem("tile_in_psum")
    s_add = k.sem("hidden_ready")
    s_sq = k.sem("squares_summed")
    s_var = k.sem("edge_variance")
    s_rstd = k.sem("edge_rstd")
    s_z = k.sem("normalised")
    s_gelu = k.sem("gelu_done")
    s_dig = [k.sem(f"digits_loaded{h}") for h in range(2)]
    s_oh = k.sem("window_masks")
    s_lo = k.sem("histogram_low_masks")
    s_far = k.sem("histogram_distances")
    s_hi = k.sem("histogram_high_masks")
    s_hist = k.sem("histogram_added")
    s_seg = k.sem("windows_summed")
    s_u = k.sem("windows_kept")
    s_v = k.sem("edge_vector_order")
    s_u0 = k.sem("sums_zeroed")
    HALVES = 2 * BODIES
    PH = HALF // 2

    rows = k.stage[:, 0:HALF * HID].rearrange("p (j d) -> p j d", d=HID)
    z = [k.stage[:, HALF * (1 + h) * HID:HALF * (2 + h) * HID].rearrange("p (j d) -> p j d", d=HID) for h in range(2)]
    psH = [k.psH[q // 2][:, (q % 2) * 2 * HID:(q % 2 + 1) * 2 * HID].rearrange("p (j d) -> p j d", d=HID)
           for q in range(PH)]
    psU = [t[:, 0:2 * 3 * WIN].rearrange("p (q c w) -> p q c w", q=2, c=3) for t in (k.psA, k.psB)]
    psC = k.psC[:, 0:NT]
    U3 = k.U[:, :].rearrange("p (c n) -> p c n", c=3)
    oh_bf = [t[:, :, :].bitcast(BF16)[:, :, 1:2 * WIN:2] for t in k.oh]

    with nc.Block() as block:

        @block.sync
        def _(sp):
            def load_meta(b, h):
                sp.dma_start(k.meta[h][:, :], k.meta_d[ds(2 * b + h, 1)].rearrange("o p c -> (o p) c"))\
                  .then_inc(s_meta[h], 16)

            def load_digits(b, h):
                sp.dma_start(k.digits[h][:, 0:3 * HALF], k.digit_tab[:, ds(2 * b + h, 1), :]
                             .rearrange("p o c -> p (o c)")).then_inc(s_dig[h], 16)

            def load_ea(b, h):
                for to, blocks in ((k.eaA[h], EA_A), (k.eaB[h], EA_B)):
                    for i, (n, _) in enumerate(blocks):
                        sp.dma_start(to[DE * i:DE * (i + 1), :].rearrange("f (q e) -> f q e", e=2 * P),
                                     k.ea_parts[n][ds(2 * PH * b + PH * h, PH)].rearrange("q f e -> f q e"))\
                          .then_inc(s_ea[h], 16)

            for h in range(2):
                load_meta(0, h)
                load_digits(0, h)
                load_ea(0, h)
            with sp.Fori(0, BODIES - 1) as b:
                for h in range(2):
                    wait_apart(k, sp, s_tile, BODY * b + HALF * (h + 1))
                    load_ea(b + 1, h)
                    wait_apart(k, sp, s_lo, 2 * b + h + 1)
                    wait_apart(k, sp, s_oh, 2 * b + h + 1)
                    wait_apart(k, sp, s_far, 2 * b + h + 1)
                    load_digits(b + 1, h)
                    wait_apart(k, sp, s_add, PH * (2 * b + h + 1))
                    load_meta(b + 1, h)

        @block.gpsimd
        def _(gp):
            def gather(h, j):
                gp.indirect_dma_start(out=rows[:, j, :], out_offset=None, in_=k.p_tab[:, :],
                                      in_offset=bass.IndirectOffsetOnAxis(ap=k.meta[h][:, j:j + 1], axis=0))\
                  .then_inc(s_g[j], 16)

            def rstd(unit, i):
                gp.wait_ge(s_var, unit + 1)
                gp.tensor_tensor(k.rstd[i][:, :], k.var[i][:, :], k.neghalf[:, 0:HALF], ALU.pow)\
                  .then_inc(s_rstd, 1)

            def half(b, h, lead):
                H = 2 * b + h
                wait_apart(k, gp, s_meta[h], 16 * b + 16)
                for j in range(HALF):
                    if j % 2 == 0 and not (lead and h == 0):
                        wait_apart(k, gp, s_add, PH * (H - 1) + j // 2 + 1)
                    if j == GROUP - 1 and not (lead and h == 0):
                        rstd(H - 1, 1 - h)
                    gather(h, j)

            gp.sem_inc(s_rstd, 1)
            for h in range(2):
                half(0, h, True)
            with gp.Fori(1, BODIES) as b:
                for h in range(2):
                    half(b, h, False)
            rstd(HALVES - 1, 1)
            rstd(HALVES, 0)

        @block.tensor
        def _(pe):
            def product(b, h, q, lead):
                H = 2 * b + h
                if q == 0:
                    pe.wait_ge(s_ea[h], 16 * len(EA_A + EA_B) * (b + 1))
                if not (lead and h == 0):
                    pe.wait_ge(s_add, PH * (H - 1) + q + 1)
                for t in range(2):
                    e = (2 * q + t) * P
                    nc.tensor.matmul(psH[q][:, t, :], k.eaA[h][:, e:e + P], k.wA[:, :], start=True, stop=False)
                    nc.tensor.matmul(psH[q][:, t, :], k.eaB[h][:, e:e + P], k.wB[:, :], start=False,
                                     stop=True).then_inc(s_tile, 1)

            def histogram(H, h):
                pe.wait_ge(s_lo, H + 1)
                pe.wait_ge(s_hi, H + 1)
                for j in range(HALF):
                    last = nc.tensor.matmul(psC, k.lo[h][:, j, :], k.hi[h][:, j, :], start=False, stop=False)
                last.then_inc(s_hist, 1)

            def window_sums(gg, h, g, first):
                pe.wait_ge(s_gelu, gg + 1)
                if not first:
                    pe.wait_ge(s_u, gg)
                for q in range(2):
                    for c in range(3):
                        for i in range(2):
                            j = GROUP * g + 2 * q + i
                            left, right = ((z[h][:, j, c * P:(c + 1) * P], k.oh[h][:, j, :]) if c < 2 else
                                           (k.ones_bf[:, :], oh_bf[h][:, j, :]))
                            last = nc.tensor.matmul(psU[g][:, q, c, :], left, right, start=i == 0, stop=i == 1)
                last.then_inc(s_seg, 1)

            def slot(b, h, lead, ahead=True):
                H = 2 * b + h
                o = 1 - h
                if ahead:
                    product(b + h, o, 0, False)
                if not lead:
                    window_sums(2 * (H - 2) + 1, h, 1, False)
                if ahead:
                    product(b + h, o, 1, False)
                if not (lead and h == 0):
                    histogram(H - 1, o)
                if not (lead and h == 0):
                    window_sums(2 * (H - 1), o, 0, lead)
                if ahead:
                    product(b + h, o, 2, False)
                    product(b + h, o, 3, False)

            nc.tensor.matmul(psC, k.zerob[:, :], k.zerob[:, 0:NT], start=True, stop=False)
            for q in range(PH):
                product(0, 0, q, True)
            for h in range(2):
                slot(0, h, True)
            with pe.Fori(1, BODIES - 1) as b:
                for h in range(2):
                    slot(b, h, False)
            for h in range(2):
                slot(BODIES - 1, h, False, ahead=h == 0)
            window_sums(2 * (HALVES - 2) + 1, 0, 1, False)
            histogram(HALVES - 1, 1)
            window_sums(2 * (HALVES - 1), 1, 0, False)
            window_sums(2 * (HALVES - 1) + 1, 1, 1, False)
            nc.tensor.matmul(psC, k.zerob[:, :], k.zerob[:, 0:NT], start=False, stop=True).then_inc(s_hist, 1)

        @block.scalar
        def _(a):
            def square(H, h, j, lead):
                a.wait_ge(s_add, PH * H + j // 2 + 1)
                if not (lead and h == 0 and j < GROUP):
                    a.wait_ge(s_sq, HALF * H + j - GROUP + 1)
                i, at = (h, GROUP + j) if j < GROUP else (1 - h, j - GROUP)
                if j == 0 and not lead:
                    a.wait_ge(s_var, H - 1)
                if j == GROUP and not (lead and h == 0):
                    a.wait_ge(s_var, H)
                nc.scalar.activation(k.scratch[:, j % GROUP, :], z[h][:, j, :], ACT.Square, scale=HID ** -0.5,
                                     accum_out=k.ssq[i][:, at:at + 1]).then_inc(s_sq, 1)

            def gelu(gg, h, g):
                a.wait_ge(s_z, gg + 1)
                part = z[h][:, GROUP * g:GROUP * (g + 1), :]
                nc.scalar.activation(part, part, ACT.Gelu).then_inc(s_gelu, 1)

            def high_masks(b, h, lead):
                H = 2 * b + h
                a.wait_ge(s_dig[h], 16 * b + 16)
                if not lead:
                    a.wait_ge(s_hist, H - 1)
                for j in range(HALF):
                    last = nc.scalar.activation(k.hi[h][:, j, :], k.iota[:, 0:NT], ACT.Square,
                                                bias=k.digits[h][:, 2 * HALF + j:2 * HALF + j + 1])
                last.then_inc(s_far, 1)
                a.wait_ge(s_far, H + 1)
                nc.scalar.activation(k.hi[h][:, :, :], k.hi[h][:, :, :], ACT.Relu, scale=-1.0,
                                     bias=k.ones[:, 0:1]).then_inc(s_hi, 1)

            def slot(b, h, lead):
                H = 2 * b + h
                for j in range(GROUP):
                    square(H, h, j, lead)
                if not (lead and h == 0):
                    gelu(2 * (H - 1), 1 - h, 0)
                high_masks(b, h, lead)
                for j in (4, 5):
                    square(H, h, j, lead)
                if not (lead and h == 0):
                    gelu(2 * (H - 1) + 1, 1 - h, 1)
                for j in (6, 7):
                    square(H, h, j, lead)

            for h in range(2):
                slot(0, h, True)
            with a.Fori(1, BODIES) as b:
                for h in range(2):
                    slot(b, h, False)
            for g in range(2):
                gelu(2 * (HALVES - 1) + g, 1, g)

        @block.vector
        def _(v):
            def low_masks(b, h, part, lead):
                H = 2 * b + h
                if part == 0:
                    v.wait_ge(s_dig[h], 16 * b + 16)
                if not lead and part == 0:
                    v.wait_ge(s_hist, H - 1)
                for j in range(GROUP * part, GROUP * (part + 1)):
                    last = v.tensor_scalar(k.lo[h][:, j, :], k.iotab[:, :], k.digits[h][:, HALF + j:HALF + j + 1], None, ALU.is_equal)
                if part:
                    last.then_inc(s_lo, 1)

            def window_masks(H, h, lead):
                if not lead:
                    v.wait_ge(s_seg, 2 * H - 2)
                v.tensor_tensor(k.oh[h][:, :, :], k.iota[:, 0:WIN].unsqueeze(1).to_broadcast([P, HALF, WIN]),
                                k.digits[h][:, 0:HALF].unsqueeze(2).to_broadcast([P, HALF, WIN]),
                                ALU.is_equal).then_inc(s_oh, 1)

            def add(b, h, q, lead):
                H = 2 * b + h
                if not lead and q % 2 == 0:
                    v.wait_ge(s_seg, 2 * H - 4 + q // 2 + 1)
                v.wait_ge(s_tile, HALF * H + 2 * q + 2)
                for j in (2 * q, 2 * q + 1):
                    v.wait_ge(s_g[j], 16 * H + 16)
                v.tensor_tensor(z[h][:, 2 * q:2 * q + 2, :], psH[q], rows[:, 2 * q:2 * q + 2, :],
                                ALU.add).then_inc(s_add, 1)

            def variance(unit, i, lead, part=slice(0, HALF)):
                v.wait_ge(s_sq, HALF * unit + GROUP if part.stop == HALF else HALF * unit)
                if not lead:
                    v.wait_ge(s_rstd, unit)
                v.tensor_scalar(k.var[i][:, part], k.ssq[i][:, part], EPS, None, ALU.add).then_inc(s_var, 1)

            def scale(o, H, h, g):
                v.wait_ge(s_rstd, H + g + 2)
                for t in range(GROUP):
                    j = GROUP * g + t
                    root = k.rstd[1 - h][:, t:t + 1] if g else k.rstd[h][:, GROUP + t:GROUP + t + 1]
                    o(v.scalar_tensor_tensor(z[h][:, j, :], z[h][:, j, :], root, k.g1[:, :], ALU.mult, ALU.mult))

            def shift(o, h, g, scaled):
                o.wait(o.base + scaled)
                part = z[h][:, GROUP * g:GROUP * (g + 1), :]
                v.tensor_tensor(part, part, k.be1[:, :].unsqueeze(1).to_broadcast([P, GROUP, HID]),
                                ALU.add).then_inc(s_z, 1)

            def starts(H):
                _, at = nc.values_load_multi_w_load_instructions(
                    k.firsts[0:1, ds(PH * H, PH)], engines=[mybir.EngineType.DVE], min_val=0, max_val=N_NODES)
                return at

            def keep(o, gg, g, q, at):
                if q == 0:
                    v.wait_ge(s_u, gg + 1)
                    v.wait_ge(s_seg, gg + 1)
                else:
                    o.wait(kept[0])
                to = U3[:, :, ds(at[2 * g + q], WIN)]
                ins = v.tensor_tensor(to, to, psU[g][:, q], ALU.add)
                if q == 0:
                    kept[0] = o(ins)
                else:
                    ins.then_inc(s_u, 1)

            kept = [None]

            def slot(o, b, h, lead):
                H = 2 * b + h
                p = 1 - h
                follow = not (lead and h == 0)
                at = None if lead else starts(H - 2)
                add(b, h, 0, lead)
                if not lead:
                    keep(o, 2 * (H - 2), 0, 0, at)
                if follow:
                    scale(o, H - 1, p, 0)
                    scaled = o.n
                add(b, h, 1, lead)
                if not lead:
                    keep(o, 2 * (H - 2), 0, 1, at)
                if follow:
                    shift(o, p, 0, scaled)
                variance(H, h, lead, slice(0 if follow else GROUP, HALF))
                low_masks(b, h, 0, lead)
                low_masks(b, h, 1, lead)
                window_masks(H, h, lead)
                add(b, h, 2, lead)
                if not lead:
                    keep(o, 2 * (H - 2) + 1, 1, 0, at)
                if follow:
                    scale(o, H - 1, p, 1)
                    scaled = o.n
                if not lead:
                    keep(o, 2 * (H - 2) + 1, 1, 1, at)
                if follow:
                    shift(o, p, 1, scaled)
                add(b, h, 3, lead)

            v.memset(k.var[0][:, 0:GROUP], 1.0).then_inc(s_u0, 1)
            v.memset(k.U[:, :], 0.0).then_inc(s_u0, 1)
            v.wait_ge(s_u0, 2)
            v.sem_inc(s_u, 1)
            o = Order(v, s_v)
            for h in range(2):
                slot(o, 0, h, True)
            start = o.n
            K = 2 * (HALF + 2)
            with v.Fori(1, BODIES) as b:
                o = Order(v, s_v, start + K * (b - 1))
                for h in range(2):
                    slot(o, b, h, False)
                assert o.n == K, (o.n, K)
            o = Order(v, s_v, start + K * (BODIES - 1))
            H = HALVES - 1
            at = starts(H - 1)
            for q in range(2):
                keep(o, 2 * (H - 1), 0, q, at)
            variance(HALVES, 0, False, slice(0, GROUP))
            for g in range(2):
                scale(o, H, 1, g)
                shift(o, 1, g, o.n)
            for q in range(2):
                keep(o, 2 * H - 1, 1, q, at)
            at = starts(H)
            for g in range(2):
                for q in range(2):
                    keep(o, 2 * H + g, g, q, at)
            v.wait_ge(s_u, 2 * HALVES + 1)
            v.wait_ge(s_hist, HALVES + 1)
            v.tensor_copy(k.beyond_count[:, :], psC)


def far_edges(nc, k, messages):
    layer = "far_messages" if messages else "far_hyperedges"
    chunks = FAR_CHUNKS if messages else FAR_HCHUNKS
    s_ld = k.sem(f"{layer}_loaded")
    s_g = k.sem(f"{layer}_rows_gathered")
    s_h = k.sem(f"{layer}_hidden")
    s_sq = k.sem(f"{layer}_squares")
    s_var = k.sem(f"{layer}_variance")
    s_rs = k.sem(f"{layer}_rstd")
    s_n = k.sem(f"{layer}_normalised")
    s_z = k.sem(f"{layer}_rows_ready")
    s_m = [k.sem(f"{layer}_masks{i}") for i in range(2)]
    s_p = [k.sem(f"{layer}_products{i}") for i in range(2)]
    s_k = [k.sem(f"{layer}_kept{i}") for i in range(2)]
    s_t = k.sem(f"{layer}_tiles_done")
    s_i = k.sem(f"{layer}_columns")
    s_f = [k.sem(f"{layer}_destinations{i}") for i in range(2)]
    s_v = k.sem(f"{layer}_vector_order")
    cols = HID if messages else D
    loads = 48 if messages else 32
    parts = 3 if messages else 1
    table = k.p_tab if messages else k.xp_tab
    rows = k.stage[:, 0:cols]
    columns = k.stage[:, HID:HID + FAR_COLS]
    mask = k.stage[:, HID + FAR_COLS:HID + 2 * FAR_COLS]
    at = HID + 2 * FAR_COLS
    z = k.stage[:, at:at + HID]
    square = k.stage[:, at + HID:at + 2 * HID]
    ea = k.stage[0:DE, at + 2 * HID:at + 2 * HID + P]
    at += 2 * HID + P
    local, low, high, far, ssq, rstd = (k.stage[:, at + i:at + i + 1] for i in range(6))
    src = k.stage[:, at + 6:at + 7].bitcast(I32)
    dst = k.stage[:, at + 7:at + 8].bitcast(I32)
    ps = [k.psA, k.psB, k.psC]
    sums = k.U[:, :].rearrange("p (c n) -> p c n", c=3)

    def trips(eng):
        return (eng.value_load(k.bounds[0:1, 1:2], min_val=1, max_val=PAIRS),
                eng.value_load(k.bounds[0:1, 2 if messages else 3:3 if messages else 4], min_val=1, max_val=chunks))

    with nc.Block() as block:

        @block.sync
        def _(sp):
            n_pairs, _ = trips(sp)
            sp.sem_inc(s_t, 1)
            with sp.Fori(0, n_pairs) as b:
                for i in range(2):
                    tile = 2 * b + i
                    sp.wait_ge(s_t, tile + 1)
                    sp.dma_start(src, k.src_tiles[ds(tile, 1)].rearrange("o e c -> (o e) c")).then_inc(s_ld, 16)
                    sp.dma_start(dst, k.dst_tiles[ds(tile, 1)].rearrange("o e c -> (o e) c")).then_inc(s_ld, 16)
                    if messages:
                        sp.dma_start(ea, k.ea_d[ds(b, 1), :, i * P:(i + 1) * P].rearrange("o f e -> (o f) e")).then_inc(s_ld, 16)

        @block.gpsimd
        def _(gp):
            n_pairs, _ = trips(gp)
            gp.iota(columns, [[1, FAR_COLS]], base=1, channel_multiplier=0,
                    allow_small_or_imprecise_dtypes=True).then_inc(s_i, 1)
            with gp.Fori(0, n_pairs) as b:
                for i in range(2):
                    tile = 2 * b + i
                    wait_apart(k, gp, s_ld, loads * tile + loads)
                    gp.indirect_dma_start(out=rows, out_offset=None, in_=table[:, :],
                                          in_offset=bass.IndirectOffsetOnAxis(ap=src, axis=0)).then_inc(s_g, 16)
                    if messages:
                        gp.wait_ge(s_var, tile + 1)
                        gp.tensor_tensor(rstd, ssq, k.neghalf[:, 0:1], ALU.pow).then_inc(s_rs, 1)

        @block.scalar
        def _(a):
            n_pairs, _ = trips(a)
            if messages:
                with a.Fori(0, n_pairs) as b:
                    for i in range(2):
                        tile = 2 * b + i
                        a.wait_ge(s_h, tile + 1)
                        nc.scalar.activation(square, k.psH[0][:, 0:HID], ACT.Square, scale=HID ** -0.5,
                                             accum_out=ssq).then_inc(s_sq, 1)
                        a.wait_ge(s_n, tile + 1)
                        nc.scalar.activation(z, z, ACT.Gelu).then_inc(s_z, 1)

        @block.tensor
        def _(pe):
            n_pairs, n_chunks = trips(pe)
            with pe.Fori(0, n_pairs) as b:
                for i in range(2):
                    tile = 2 * b + i
                    wait_apart(k, pe, s_g, 16 * tile + 16)
                    if messages:
                        pe.wait_ge(s_ld, loads * tile + loads)
                        nc.tensor.matmul(k.psH[0][:, 0:HID], ea, k.w1b[:, :], start=True, stop=False)
                        nc.tensor.matmul(k.psH[0][:, 0:HID], k.ident[:, :], rows, start=False, stop=True).then_inc(s_h, 1)
                        wait_apart(k, pe, s_z, tile + 1)
                        left = [z[:, 0:P], z[:, P:HID], k.ones[:, :]]
                    else:
                        left = [rows]
                    with pe.Fori(0, n_chunks) as c:
                        pe.wait_ge(s_m[i], chunks * b + c + 1)
                        for m in range(parts):
                            last = nc.tensor.matmul(ps[m][:, 0:FAR_COLS], left[m], mask, start=True, stop=True)
                        last.then_inc(s_p[i], 1)

        @block.vector
        def _(v):
            n_pairs, n_chunks = trips(v)
            K = 7 if messages else 5
            v.wait_ge(s_i, 1)
            for i in range(2):
                v.sem_inc(s_k[i], 1)
            with v.Fori(0, n_pairs) as b:
                for i in range(2):
                    tile = 2 * b + i
                    o = Order(v, s_v, K * tile)
                    v.wait_ge(s_ld, loads * tile + loads)
                    o(v.tensor_tensor(local, dst, k.firsts[:, ds(b, 1)], ALU.subtract))
                    o(v.tensor_scalar(far, dst, 1.0, None, ALU.add))
                    o.wait()
                    o(v.tensor_scalar(low, local, 0.0, None, ALU.is_lt))
                    o(v.tensor_scalar(high, local, float(WIN), None, ALU.is_ge))
                    o.wait()
                    o(v.tensor_tensor(low, low, high, ALU.max))
                    o.wait()
                    v.tensor_tensor(far, far, low, ALU.mult).then_inc(s_f[i], 1)
                    if messages:
                        v.wait_ge(s_sq, tile + 1)
                        o(v.tensor_scalar(ssq, ssq, EPS, None, ALU.add))
                        o.wait()
                        v.sem_inc(s_var, 1)
                        v.wait_ge(s_rs, tile + 1)
                        o(v.scalar_tensor_tensor(z, k.psH[0][:, 0:HID], rstd, k.g1[:, :], ALU.mult, ALU.mult))
                        o.wait()
                        v.tensor_tensor(z, z, k.be1[:, :], ALU.add).then_inc(s_n, 1)
                    with v.Fori(0, n_chunks) as c:
                        step = chunks * b + c
                        wait_apart(k, v, s_f[i], b + step + 1)
                        v.wait_ge(s_k[i], step + 1)
                        v.tensor_scalar(mask, columns, far, None, ALU.is_equal).then_inc(s_m[i], 1)
                        v.wait_ge(s_p[i], step + 1)
                        v.tensor_scalar(far, far, -float(FAR_COLS), None, ALU.add).then_inc(s_f[i], 1)
                        for m in range(parts):
                            to = sums[:, m, ds(c * FAR_COLS, FAR_COLS)]
                            last = v.tensor_tensor(to, to, ps[m][:, 0:FAR_COLS], ALU.add)
                        last.then_inc(s_k[i], 1)
                    v.wait_ge(s_k[i], chunks * b + n_chunks + 1)
                    v.sem_inc(s_t, 1)


def far_messages(nc, k):
    far_edges(nc, k, True)


def far_hyperedges(nc, k):
    far_edges(nc, k, False)


def hyper_degrees(nc, k):
    s_meta = [k.sem(f"deg_indices_loaded{h}") for h in range(2)]
    s_ix = k.sem("deg_indices_ready")
    s_wg = [k.sem(f"weights_gathered{h}") for h in range(2)]
    s_m = k.sem("deg_masks")
    s_mu = k.sem("deg_added")
    s_v = k.sem("deg_vector_order")
    s_ld = k.sem("deg_constants_loaded")
    s_pow = k.sem("deg_base")
    s_dv = k.sem("deg_sum_order")
    s_end = k.sem("deg_done")
    psV = k.psA[:, 0:NT]
    psD = k.psB[:, 0:HT]
    IX = 7

    with nc.Block() as block:

        @block.sync
        def _(sp):
            n_bodies = sp.value_load(k.bounds[0:1, 0:1], min_val=1, max_val=BODIES)

            def load_meta(b, h):
                sp.dma_start(k.meta[h][:, :], k.meta_d[ds(2 * b + h, 1)].rearrange("o p c -> (o p) c"))\
                  .then_inc(s_meta[h], 16)

            sp.dma_start(k.w_last[:, :], k.w_d[N_HYPER - 1:N_HYPER, :].partition_broadcast(P)
                         .rearrange("p a b -> p (a b)")).then_inc(s_ld, 16)
            sp.dma_start(k.w_pt[:, :], k.w_pt_d).then_inc(s_ld, 16)
            for h in range(2):
                load_meta(0, h)
            with sp.Fori(0, n_bodies) as b:
                for h in range(2):
                    sp.wait_ge(s_wg[h], 16 * HALF * (b + 1))
                    load_meta(b + 1, h)
            for h in range(2):
                wait_apart(k, sp, s_meta[h], 16 * n_bodies + 16)

        @block.gpsimd
        def _(gp):
            n_bodies = gp.value_load(k.bounds[0:1, 0:1], min_val=1, max_val=BODIES)
            with gp.Fori(0, n_bodies) as b:
                for h in range(2):
                    wait_apart(k, gp, s_ix, 2 * b + h + 1)
                    for j in range(HALF):
                        gp.indirect_dma_start(out=k.w_row[h][:, j:j + 1], out_offset=None, in_=k.w_d[:, :],
                                              in_offset=bass.IndirectOffsetOnAxis(ap=k.gidx[h][:, j:j + 1], axis=0))\
                          .then_inc(s_wg[h], 16)
            gp.wait_ge(s_pow, 1)
            gp.tensor_tensor(k.dvr[:, :], k.dvr[:, :], k.neghalf[:, 0:NT], ALU.pow).then_inc(s_end, 1)

        @block.tensor
        def _(pe):
            n_bodies = pe.value_load(k.bounds[0:1, 0:1], min_val=1, max_val=BODIES)
            pe.sem_inc(s_mu, 2)
            nc.tensor.matmul(psV, k.zerob[:, :], k.zerob[:, 0:NT], start=True, stop=False)
            nc.tensor.matmul(psD, k.zerob[:, :], k.zerob[:, 0:HT], start=True, stop=False)
            with pe.Fori(0, n_bodies) as b:
                for n in range(BODY):
                    pe.wait_ge(s_m, BODY * b + n + 1)
                    nc.tensor.matmul(psV, k.mask_lo[n % 2][:, :], k.mask_hi[n % 2][:, 0:NT], start=False, stop=False)
                    nc.tensor.matmul(psD, k.ohb[n % 2][:, :], k.oha[n % 2][:, 0:HT], start=False,
                                     stop=False).then_inc(s_mu, 1)
            nc.tensor.matmul(psV, k.zerob[:, :], k.zerob[:, 0:NT], start=False, stop=True)
            nc.tensor.matmul(psD, k.zerob[:, :], k.zerob[:, 0:HT], start=False, stop=True).then_inc(s_mu, 1)

        @block.vector
        def _(v):
            n_bodies = v.value_load(k.bounds[0:1, 0:1], min_val=1, max_val=BODIES)
            v.wait_ge(s_ld, 32)
            K = 2 * (IX + 1)

            def indices(o, b, h):
                v.wait_ge(s_meta[h], 16 * b + 16)
                src, dst = k.meta[h][:, 0:HALF], k.meta[h][:, HALF:2 * HALF]
                o(v.tensor_scalar(k.gidx[h][:, :], dst, float(N_HYPER - 1), None, ALU.min))
                o(v.tensor_scalar(k.beyond[h][:, :], dst, float(N_HYPER), None, ALU.is_lt))
                o(v.tensor_scalar(k.bits[h][:, 0:HALF], src, P - 1, None, ALU.bitwise_and))
                o(v.tensor_scalar(k.bits[h][:, HALF:2 * HALF], src, P.bit_length() - 1, None, ALU.logical_shift_right))
                o(v.tensor_scalar(k.bits[h][:, 2 * HALF:3 * HALF], dst, P - 1, None, ALU.bitwise_and))
                o(v.tensor_scalar(k.bits[h][:, 3 * HALF:4 * HALF], dst, P.bit_length() - 1, None, ALU.logical_shift_right))
                o.wait()
                o(v.tensor_copy(k.digits[h][:, :], k.bits[h][:, :]))
                o.wait()
                v.sem_inc(s_ix, 1)

            def masks(o, b, h):
                v.wait_ge(s_wg[h], 16 * HALF * (b + 1))
                o(v.tensor_tensor(k.w_act[h][:, :], k.w_row[h][:, :], k.beyond[h][:, :], ALU.mult))
                o.wait()
                for j in range(HALF):
                    n = HALF * h + j
                    v.wait_ge(s_mu, BODY * b + n + 1)
                    i = n % 2
                    v.tensor_scalar(k.mask_lo[i][:, :], k.iota[:, :], k.src_lo[h][:, j:j + 1], None, ALU.is_equal)
                    v.tensor_scalar(k.mask_hi[i][:, 0:NT], k.iota[:, 0:NT], k.src_hi[h][:, j:j + 1],
                                    k.w_act[h][:, j:j + 1], ALU.is_equal, ALU.mult)
                    v.tensor_scalar(k.ohb[i][:, :], k.iotab[:, :], k.dst_lo[h][:, j:j + 1], None, ALU.is_equal)
                    v.tensor_scalar(k.oha[i][:, 0:HT], k.iotab[:, 0:HT], k.dst_hi[h][:, j:j + 1], None,
                                    ALU.is_equal).then_inc(s_m, 1)

            o = Order(v, s_v)
            indices(o, 0, 0)
            with v.Fori(0, n_bodies) as b:
                o = Order(v, s_v, K * b + IX)
                indices(o, b, 1)
                masks(o, b, 0)
                indices(o, b + 1, 0)
                masks(o, b, 1)
                assert o.n == K, (o.n, K)
            last = n_bodies * BODY
            v.wait_ge(s_mu, last + 3)
            o = Order(v, s_dv)
            o(v.scalar_tensor_tensor(k.dvr[:, :], k.beyond_count[:, :], k.w_last[:, 0:1], psV, ALU.mult, ALU.add))
            o(v.tensor_scalar(k.w_de[:, :], psD, 1.0, None, ALU.max))
            o.wait()
            o(v.tensor_scalar(k.dvr[:, :], k.dvr[:, :], 1.0, None, ALU.max))
            o(v.reciprocal(k.w_de[:, :], k.w_de[:, :]))
            o.wait()
            o(v.tensor_tensor(k.w_de[:, :], k.w_de[:, :], k.w_pt[:, :], ALU.mult))
            v.sem_inc(s_pow, 1)


def node_update(nc, k):
    s_ld = [k.sem(f"update_loaded{h}") for h in range(2)]
    s_ut = k.sem("sums_copied")
    s_ps = k.sem("update_product")
    s_u = k.sem("update_taken")
    s_var = k.sem("update_variance")
    s_rs = k.sem("update_rstd")
    s_n = k.sem("update_scaled")
    s_b = k.sem("update_biased")
    s_g = k.sem("update_gelu")
    s_x1 = k.sem("x1_ready")
    s_xp = k.sem("xp_ready")
    s_st = [k.sem(f"update_stored{h}") for h in range(2)]
    s_v = k.sem("update_vector_order")
    W = NG * D
    LAST = NGROUPS // 2

    def grp(i):
        return k.stage[:, i * W:(i + 1) * W].rearrange("p (t d) -> p t d", d=D)

    u, xh, xp = [grp(0), grp(1)], [grp(2), grp(3)], [grp(4), grp(5)]
    U3 = k.U[:, :].rearrange("p (c n) -> p c n", c=3)
    ps = [k.psA, k.psB]
    view = {n: t.rearrange("(g t p) d -> g p t d", p=P, t=NG)
            for n, t in (("hwu", k.hwu_tab), ("xh", k.xh_tab), ("x1", k.x1_tab), ("xp", k.xp_tab))}

    def rows(n, g):
        return view[n][ds(g, 1)].rearrange("o p t d -> (o p) t d")

    with nc.Block() as block:

        @block.sync
        def _(sp):
            def load(g, h):
                sp.dma_start(u[h], rows("hwu", g)).then_inc(s_ld[h], 16)
                sp.dma_start(xh[h], rows("xh", g)).then_inc(s_ld[h], 16)

            def store(g, h):
                sp.wait_ge(s_x1, g + 1)
                sp.dma_start(rows("x1", g), xh[h]).then_inc(s_st[h], 16)
                sp.wait_ge(s_xp, g + 1)
                sp.dma_start(rows("xp", g), xp[h]).then_inc(s_st[h], 16)

            for h in range(2):
                load(h, h)
            with sp.Fori(0, LAST - 1) as b:
                for h in range(2):
                    store(2 * b + h, h)
                    sp.wait_ge(s_st[h], 32 * b + 32)
                    load(2 * b + 2 + h, h)
            for h in range(2):
                store(2 * LAST - 2 + h, h)
            for h in range(2):
                sp.wait_ge(s_st[h], 32 * LAST)

        @block.scalar
        def _(a):
            with a.Fori(0, LAST) as b:
                for h in range(2):
                    for t in range(NG):
                        n = NG * h + t
                        a.wait_ge(s_ps, 2 * NG * b + n + 1)
                        a.copy(k.ut[n % 2][:, :, :], U3[:, :, ds(2 * NG * P * b + n * P, P)]).then_inc(s_ut, 1)
                    a.wait_ge(s_b, 2 * b + h + 1)
                    nc.scalar.activation(u[h], u[h], ACT.Gelu).then_inc(s_g, 1)

        @block.tensor
        def _(pe):
            pe.sem_inc(s_ps, 2)
            with pe.Fori(0, LAST) as b:
                for n in range(2 * NG):
                    pe.wait_ge(s_ut, 2 * NG * b + n + 1)
                    pe.wait_ge(s_u, 2 * NG * b + n + 1)
                    i = n % 2
                    nc.tensor.matmul(ps[i][:, 0:D], k.ut[i][:, 0, :], k.w2u[:, 0:D], start=True, stop=False)
                    nc.tensor.matmul(ps[i][:, 0:D], k.ut[i][:, 1, :], k.w2u[:, D:2 * D], start=False, stop=False)
                    nc.tensor.matmul(ps[i][:, 0:D], k.ut[i][0:1, 2, :], k.b2u[0:1, :], start=False,
                                     stop=True).then_inc(s_ps, 1)

        @block.gpsimd
        def _(gp):
            with gp.Fori(0, LAST) as b:
                for h in range(2):
                    g = 2 * b + h
                    gp.wait_ge(s_var, 2 * g + 1)
                    gp.tensor_tensor(k.nrs[h][:, 0:NG], k.nvar[h][:, 0:NG], k.neghalf[:, 0:NG], ALU.pow).then_inc(s_rs, 1)
                    gp.wait_ge(s_n, g + 1)
                    gp.tensor_tensor(u[h], u[h], k.beu[:, :].unsqueeze(1).to_broadcast([P, NG, D]), ALU.add).then_inc(s_b, 1)
                    gp.wait_ge(s_g, g + 1)
                    gp.tensor_tensor(xh[h], xh[h], u[h], ALU.add).then_inc(s_x1, 1)
                    gp.wait_ge(s_var, 2 * g + 2)
                    gp.tensor_tensor(k.nrs[h][:, NG:2 * NG], k.nvar[h][:, NG:2 * NG], k.neghalf[:, 0:NG],
                                     ALU.pow).then_inc(s_rs, 1)

        @block.vector
        def _(v):
            K = 6 * NG + 1
            v.sem_inc(s_u, 2)

            def stats(o, x, h, part):
                first = o.n
                for t in range(NG):
                    o(v.bn_stats(k.nst[h][:, t, :], x[:, t, :]))
                for t in range(NG):
                    wait_apart(k, v, s_v, o.base + first + t + 1)
                    o(v.bn_aggr(k.nmv[h][:, NG * part + t, :], k.nst[h][:, t, :]))
                o.wait()
                v.tensor_scalar(k.nvar[h][:, NG * part:NG * part + NG], k.nmv[h][:, NG * part:NG * part + NG, 1],
                                EPS, None, ALU.add).then_inc(s_var, 1)

            with v.Fori(0, LAST) as b:
                o = Order(v, s_v, 2 * K * b)
                for h in range(2):
                    g = 2 * b + h
                    v.wait_ge(s_ld[h], 32 * b + 32)
                    for t in range(NG):
                        n = 2 * NG * b + NG * h + t
                        v.wait_ge(s_ps, n + 3)
                        v.tensor_tensor(u[h][:, t, :], ps[(NG * h + t) % 2][:, 0:D], u[h][:, t, :], ALU.add).then_inc(s_u, 1)
                    v.wait_ge(s_u, 2 * NG * b + NG * (h + 1) + 2)
                    stats(o, u[h], h, 0)
                    v.wait_ge(s_rs, 2 * g + 1)
                    for t in range(NG):
                        o(v.tensor_scalar(u[h][:, t, :], u[h][:, t, :], k.nmv[h][:, t, 0:1], k.nrs[h][:, t:t + 1],
                                          ALU.subtract, ALU.mult))
                    o.wait()
                    v.tensor_tensor(u[h], u[h], k.gu[:, :].unsqueeze(1).to_broadcast([P, NG, D]), ALU.mult).then_inc(s_n, 1)
                    v.wait_ge(s_x1, g + 1)
                    stats(o, xh[h], h, 1)
                    v.wait_ge(s_rs, 2 * g + 2)
                    o(v.tensor_tensor(k.nrs[h][:, NG:2 * NG], k.nrs[h][:, NG:2 * NG], k.dvr[:, ds(NG * g, NG)], ALU.mult))
                    o.wait()
                    v.wait_ge(s_ld[h], 32 * b + 32)
                    for t in range(NG):
                        o(v.tensor_scalar(xp[h][:, t, :], xh[h][:, t, :], k.nmv[h][:, NG + t, 0:1],
                                          k.nrs[h][:, NG + t:NG + t + 1], ALU.subtract, ALU.mult))
                    o.wait()
                    v.tensor_scalar(xp[h], xp[h], 0.0, None, ALU.max).then_inc(s_xp, 1)
                assert o.n == 2 * K, (o.n, 2 * K)



def hyperedge_sums(nc, k):
    s_meta = [k.sem(f"he_indices_loaded{h}") for h in range(2)]
    s_g = [k.sem(f"he_rows_gathered{j}") for j in range(HALF)]
    s_loc = k.sem("he_indices_taken")
    s_oh = k.sem("he_window_masks")
    s_seg = k.sem("he_windows_summed")
    s_u = k.sem("he_windows_kept")
    s_v = k.sem("he_vector_order")
    s_z = k.sem("he_sums_zeroed")
    heT = k.U[:, 0:UCOLS]
    rows = k.stage[:, 0:HALF * D].rearrange("p (j d) -> p j d", d=D)
    psU = [k.psA[:, 0:WIN], k.psC[:, 0:WIN]]

    with nc.Block() as block:

        @block.sync
        def _(sp):
            n_bodies = sp.value_load(k.bounds[0:1, 0:1], min_val=1, max_val=BODIES)

            def load_meta(b, h):
                sp.dma_start(k.meta[h][:, :], k.meta_d[ds(2 * b + h, 1)].rearrange("o p c -> (o p) c"))\
                  .then_inc(s_meta[h], 16)

            for h in range(2):
                load_meta(0, h)
            with sp.Fori(0, n_bodies) as b:
                for h in range(2):
                    sp.wait_ge(s_seg, 8 * b + 4 * h + 8)
                    load_meta(b + 1, h)
            for h in range(2):
                wait_apart(k, sp, s_meta[h], 16 * n_bodies + 16)

        @block.gpsimd
        def _(gp):
            n_bodies = gp.value_load(k.bounds[0:1, 0:1], min_val=1, max_val=BODIES)
            gp.memset(heT, 0.0).then_inc(s_z, 1)
            gp.sem_inc(s_seg, 4)
            with gp.Fori(0, n_bodies) as b:
                for h in range(2):
                    wait_apart(k, gp, s_meta[h], 16 * b + 16)
                    for j in range(HALF):
                        if j % 2 == 0:
                            wait_apart(k, gp, s_seg, 8 * b + 4 * h + j // 2 + 1)
                        gp.indirect_dma_start(out=rows[:, j, :], out_offset=None, in_=k.xp_tab[:, :],
                                              in_offset=bass.IndirectOffsetOnAxis(ap=k.meta[h][:, j:j + 1], axis=0))\
                          .then_inc(s_g[j], 16)

        @block.tensor
        def _(pe):
            n_bodies = pe.value_load(k.bounds[0:1, 0:1], min_val=1, max_val=BODIES)
            pe.sem_inc(s_u, 2)
            with pe.Fori(0, n_bodies) as b:
                for h in range(2):
                    pe.wait_ge(s_oh, 2 * b + h + 1)
                    for q in range(HALF // 2):
                        pe.wait_ge(s_u, 8 * b + 4 * h + q + 1)
                        for i in range(2):
                            j = 2 * q + i
                            pe.wait_ge(s_g[j], 16 * (2 * b + h) + 16)
                            last = nc.tensor.matmul(psU[q % 2], rows[:, j, :], k.oh[h][:, j, :],
                                                    start=i == 0, stop=i == 1)
                        last.then_inc(s_seg, 1)

        @block.vector
        def _(v):
            n_bodies = v.value_load(k.bounds[0:1, 0:1], min_val=1, max_val=BODIES)
            v.wait_ge(s_z, 1)
            with v.Fori(0, n_bodies) as b:
                for h in range(2):
                    v.wait_ge(s_meta[h], 16 * b + 16)
                    dst = k.meta[h][:, HALF:2 * HALF]
                    first = k.firsts[:, ds(8 * b + 4 * h, 4)].unsqueeze(2).to_broadcast([P, 4, 2])
                    v.tensor_tensor(k.local[h][:, :].rearrange("p (a c) -> p a c", c=2),
                                    dst.rearrange("p (a c) -> p a c", c=2), first, ALU.subtract).then_inc(s_loc, 1)
                    v.wait_ge(s_loc, 2 * b + h + 1)
                    v.tensor_tensor(k.oh[h][:, :, :], k.iota[:, 0:WIN].unsqueeze(1).to_broadcast([P, HALF, WIN]),
                                    k.local[h][:, :].unsqueeze(2).to_broadcast([P, HALF, WIN]),
                                    ALU.is_equal).then_inc(s_oh, 1)
                    for q in range(HALF // 2):
                        w = 8 * b + 4 * h + q
                        first = v.value_load(k.firsts[0:1, ds(w, 1)], min_val=0, max_val=N_NODES)
                        v.wait_ge(s_seg, w + 1 + 4)
                        v.wait_ge(s_u, w + 2)
                        v.tensor_tensor(heT[:, ds(first, WIN)], heT[:, ds(first, WIN)], psU[q % 2],
                                        ALU.add).then_inc(s_u, 1)
            wait_apart(k, v, s_u, 8 * n_bodies + 2)


def hyperedge_rows(nc, k):
    s_gp = k.sem("he_product")
    s_gr = k.sem("he_rows_ready")
    s_st = k.sem("he_rows_stored")
    heT = k.U[:, 0:UCOLS]
    g_rows = k.stage[:, 0:HT * D].rearrange("p (t d) -> p t d", d=D)
    psG = [k.psA, k.psB]

    with nc.Block() as block:

        @block.sync
        def _(sp):
            sp.wait_ge(s_gr, HT)
            sp.dma_start(k.g_tab.rearrange("(t p) d -> p t d", p=P), g_rows).then_inc(s_st, 16)
            sp.wait_ge(s_st, 16)

        @block.tensor
        def _(pe):
            for t in range(HT):
                if t >= 2:
                    pe.wait_ge(s_gr, t - 1)
                nc.tensor.matmul(psG[t % 2][:, 0:D], heT[:, t * P:(t + 1) * P], k.lw[:, :], start=True,
                                 stop=True).then_inc(s_gp, 1)

        @block.vector
        def _(v):
            for t in range(HT):
                v.wait_ge(s_gp, t + 1)
                v.tensor_scalar(g_rows[:, t, :], psG[t % 2][:, 0:D], k.w_de[:, t:t + 1], None, ALU.mult).then_inc(s_gr, 1)


def scatter_rows(nc, k):
    s_meta = [k.sem(f"sc_indices_loaded{h}") for h in range(2)]
    s_row = [k.sem(f"sc_sources_loaded{h}") for h in range(2)]
    s_ix = k.sem("sc_indices_ready")
    s_g = [k.sem(f"sc_rows_gathered{j}") for j in range(HALF)]
    s_same = k.sem("sc_same_source")
    s_ps = k.sem("sc_tile_summed")
    s_c = k.sem("sc_rows_copied")
    s_to = k.sem("sc_targets_ready")
    s_sc = [k.sem(f"sc_scattered{r}") for r in range(k.R)]
    s_v = k.sem("sc_vector_order")
    s_sz = k.sem("sc_zeros")
    rows = k.stage[:, 0:HALF * D].rearrange("p (j d) -> p j d", d=D)
    at = HALF * D
    summed = k.stage[:, at:at + k.R * D].rearrange("p (j d) -> p j d", d=D)
    src_row = [k.U[:, i * HALF * P:(i + 1) * HALF * P].bitcast(I32).rearrange("p (j e) -> p j e", e=P)
               for i in range(2)]
    same = k.U[:, 2 * HALF * P:3 * HALF * P].rearrange("p (j e) -> p j e", e=P)
    waste = k.U[:, 3 * HALF * P:4 * HALF * P].rearrange("p (j e) -> p j e", e=P)
    at = 4 * HALF * P
    earlier = k.U[:, at:at + 2 * HALF].rearrange("p (i j) -> p i j", i=2)
    away = k.U[:, at + 2 * HALF:at + 4 * HALF].rearrange("p (i j) -> p i j", i=2)
    ps = [k.psA, k.psB]
    R = k.R

    with nc.Block() as block:

        @block.sync
        def _(sp):
            n_bodies = sp.value_load(k.bounds[0:1, 0:1], min_val=1, max_val=BODIES)

            def load(b, h):
                sp.dma_start(k.meta[h][:, :], k.meta_d[ds(2 * b + h, 1)].rearrange("o p c -> (o p) c"))\
                  .then_inc(s_meta[h], 16)
                sp.dma_start(src_row[h], k.src_d[ds(2 * b + h, 1)].rearrange("o j e -> (o j) e").partition_broadcast(P))\
                  .then_inc(s_row[h], 16)

            for h in range(2):
                load(0, h)
            with sp.Fori(0, n_bodies) as b:
                for h in range(2):
                    sp.wait_ge(s_to, 2 * b + h + 1)
                    load(b + 1, h)
            for h in range(2):
                wait_apart(k, sp, s_meta[h], 16 * n_bodies + 16)
                wait_apart(k, sp, s_row[h], 16 * n_bodies + 16)

        @block.gpsimd
        def _(gp):
            n_bodies = gp.value_load(k.bounds[0:1, 0:1], min_val=1, max_val=BODIES)
            gp.sem_inc(s_ps, HALF)
            gp.memset(summed, 0.0).then_inc(s_sz, 1)
            gp.wait_ge(s_sz, 1)
            for r in range(R):
                gp.dma_start(k.acc[r][NP:NP + P, :], summed[:, r, :]).then_inc(s_sc[r], 16)

            with gp.Fori(0, n_bodies) as b:
                for h in range(2):
                    wait_apart(k, gp, s_ix, 2 * b + h + 1)
                    for j in range(HALF):
                        n = HALF * h + j
                        wait_apart(k, gp, s_ps, BODY * b + n + 1)
                        gp.indirect_dma_start(out=rows[:, j, :], out_offset=None, in_=k.g_tab[:, :],
                                              in_offset=bass.IndirectOffsetOnAxis(ap=k.gidx[h][:, j:j + 1], axis=0))\
                          .then_inc(s_g[j], 16)
                    wait_apart(k, gp, s_to, 2 * b + h + 1)
                    for j in range(HALF):
                        n = HALF * h + j
                        r = j % R
                        wait_apart(k, gp, s_c, BODY * b + n + 3)
                        wait_apart(k, gp, s_sc[r], 16 * (BODY // R * b + n // R) + 16)
                        gp.indirect_dma_start(out=k.acc[r], out_offset=bass.IndirectOffsetOnAxis(
                            ap=k.target[h][:, j:j + 1], axis=0), in_=summed[:, r, :], in_offset=None,
                            compute_op=ALU.add).then_inc(s_sc[r], 16)
            for r in range(R):
                wait_apart(k, gp, s_sc[r], 16 * (BODY // R) * n_bodies + 16)

        @block.tensor
        def _(pe):
            n_bodies = pe.value_load(k.bounds[0:1, 0:1], min_val=1, max_val=BODIES)
            pe.sem_inc(s_c, 2)
            with pe.Fori(0, n_bodies) as b:
                for n in range(BODY):
                    j = n % HALF
                    h = n // HALF
                    if j == 0:
                        pe.wait_ge(s_same, 2 * b + h + 1)
                    pe.wait_ge(s_g[j], 16 * (2 * b + h) + 16)
                    pe.wait_ge(s_c, BODY * b + n + 1)
                    nc.tensor.matmul(ps[n % 2][:, 0:D], same[:, j, :], rows[:, j, :], start=True,
                                     stop=True).then_inc(s_ps, 1)

        @block.scalar
        def _(a):
            n_bodies = a.value_load(k.bounds[0:1, 0:1], min_val=1, max_val=BODIES)
            with a.Fori(0, n_bodies) as b:
                for n in range(BODY):
                    r = n % R
                    a.wait_ge(s_ps, BODY * b + n + 1 + HALF)
                    a.wait_ge(s_sc[r], 16 * (BODY // R * b + n // R) + 16)
                    a.copy(summed[:, r, :], ps[n % 2][:, 0:D]).then_inc(s_c, 1)

        @block.vector
        def _(v):
            n_bodies = v.value_load(k.bounds[0:1, 0:1], min_val=1, max_val=BODIES)
            K = 2 * (2 + 2 * HALF + 3)
            with v.Fori(0, n_bodies) as b:
                o = Order(v, s_v, K * b)
                for h in range(2):
                    v.wait_ge(s_meta[h], 16 * b + 16)
                    src, dst = k.meta[h][:, 0:HALF], k.meta[h][:, HALF:2 * HALF]
                    o(v.tensor_scalar(k.beyond[h][:, :], dst, float(N_HYPER), None, ALU.is_lt))
                    o(v.tensor_scalar(k.gidx[h][:, :], dst, float(N_HYPER - 1), None, ALU.min))
                    o.wait()
                    v.sem_inc(s_ix, 1)
                    v.wait_ge(s_row[h], 16 * b + 16)
                    v.wait_ge(s_ps, BODY * b + HALF * h + HALF)
                    for j in range(HALF):
                        o(v.tensor_scalar(same[:, j, :], src_row[h][:, j, :], src[:, j:j + 1], None, ALU.is_equal))
                    for j in range(HALF):
                        o.wait(o.base + o.n - HALF + 1)
                        o(v.tensor_tensor_reduce(waste[:, j, :], same[:, j, :], k.before[:, :], 1.0, 0.0, ALU.mult,
                                                 ALU.add, earlier[:, h, j:j + 1]))
                    o.wait()
                    v.tensor_tensor(same[:, :, :], same[:, :, :],
                                    k.beyond[h][:, :].unsqueeze(2).to_broadcast([P, HALF, P]),
                                    ALU.mult).then_inc(s_same, 1)
                    o(v.tensor_scalar(earlier[:, h, :], earlier[:, h, :], 1.0, None, ALU.min))
                    o(v.tensor_scalar(away[:, h, :], src, -1.0, k.junk[:, 0:1], ALU.mult, ALU.add))
                    o.wait()
                    o(v.tensor_tensor(away[:, h, :], away[:, h, :], earlier[:, h, :], ALU.mult))
                    o.wait()
                    v.tensor_tensor(k.target[h][:, :], away[:, h, :], src, ALU.add).then_inc(s_to, 1)
                assert o.n == K, (o.n, K)


def output_rows(nc, k):
    s_ld = [k.sem(f"out_loaded{h}") for h in range(2)]
    s_c = k.sem("out_constants")
    s_v = k.sem("out_vector_order")
    s_s = k.sem("out_summed")
    s_o = k.sem("out_ready")
    s_st = [k.sem(f"out_stored{h}") for h in range(2)]
    R = k.R
    W = NG * D

    def grp(i):
        return k.U[:, i * W:(i + 1) * W].rearrange("p (t d) -> p t d", d=D)

    x1 = [grp(0), grp(1)]
    acc = [[grp(2 + R * h + r) for r in range(R)] for h in range(2)]
    g_last = k.U[:, (2 + 2 * R) * W:(2 + 2 * R) * W + D]
    x1_v = k.x1_tab.rearrange("(g t p) d -> g p t d", p=P, t=NG)
    acc_v = [k.acc[r][0:NP, :].rearrange("(g t p) d -> g p t d", p=P, t=NG) for r in range(R)]
    FULL = N_NODES // (NG * P)

    with nc.Block() as block:

        @block.sync
        def _(sp):
            sp.dma_start(g_last, k.g_tab[N_HYPER - 1:N_HYPER, :].partition_broadcast(P)
                         .rearrange("p a d -> p (a d)")).then_inc(s_c, 16)

            def load(g, h):
                sp.dma_start(x1[h], x1_v[ds(g, 1)].rearrange("o p t d -> (o p) t d")).then_inc(s_ld[h], 16)
                for r in range(R):
                    sp.dma_start(acc[h][r], acc_v[r][ds(g, 1)].rearrange("o p t d -> (o p) t d")).then_inc(s_ld[h], 16)

            def store(g, h):
                sp.wait_ge(s_o, g + 1)
                sp.dma_start(k.out[ds(g * NG * P, NG * P), :].rearrange("(t p) d -> p t d", p=P),
                             x1[h]).then_inc(s_st[h], 16)

            for h in range(2):
                load(h, h)
            with sp.Fori(0, NGROUPS // 2 - 1) as b:
                for h in range(2):
                    store(2 * b + h, h)
                    sp.wait_ge(s_st[h], 16 * b + 16)
                    load(2 * b + 2 + h, h)
            store(NGROUPS - 2, 0)
            g = NGROUPS - 1
            whole = (N_NODES - g * NG * P) // P
            rest = N_NODES - g * NG * P - whole * P
            sp.wait_ge(s_o, g + 1)
            sp.dma_start(k.out[g * NG * P:g * NG * P + whole * P, :].rearrange("(t p) d -> p t d", p=P),
                         x1[1][:, 0:whole, :]).then_inc(s_st[1], 16)
            sp.dma_start(k.out[N_NODES - rest:N_NODES, :], x1[1][0:rest, whole, :]).then_inc(s_st[1], 16)
            sp.wait_ge(s_st[0], 16 * (NGROUPS // 2))
            sp.wait_ge(s_st[1], 16 * (NGROUPS // 2) + 16)

        @block.gpsimd
        def _(gp):
            with gp.Fori(0, NGROUPS // 2) as b:
                for h in range(2):
                    gp.wait_ge(s_ld[h], 16 * (1 + R) * (b + 1))
                    gp.tensor_tensor(x1[h], x1[h], k.lb[:, :].unsqueeze(1).to_broadcast([P, NG, D]), ALU.add).then_inc(s_s, 1)

        @block.vector
        def _(v):
            K = 2 * (R - 1 + NG)
            v.wait_ge(s_c, 16)
            with v.Fori(0, NGROUPS // 2) as b:
                o = Order(v, s_v, K * b)
                for h in range(2):
                    g = 2 * b + h
                    v.wait_ge(s_ld[h], 16 * (1 + R) * (b + 1))
                    for r in range(1, R):
                        o(v.tensor_tensor(acc[h][0], acc[h][0], acc[h][r], ALU.add))
                        o.wait()
                    for t in range(NG):
                        o(v.scalar_tensor_tensor(acc[h][0][:, t, :], g_last, k.beyond_count[:, ds(NG * g + t, 1)],
                                                 acc[h][0][:, t, :], ALU.mult, ALU.add))
                    v.wait_ge(s_s, g + 1)
                    o.wait()
                    for t in range(NG):
                        last = v.scalar_tensor_tensor(x1[h][:, t, :], acc[h][0][:, t, :], k.dvr[:, ds(NG * g + t, 1)],
                                                      x1[h][:, t, :], ALU.mult, ALU.add)
                    last.then_inc(s_o, 1)
                assert o.n == K, (o.n, K)




PHASES = (setup_phase, node_tables, edge_parts, edge_messages, far_messages, hyper_degrees, node_update,
          hyperedge_sums, far_hyperedges, hyperedge_rows, scatter_rows, output_rows)


def message_passing(nc, k):
    for phase in PHASES:
        taken = []

        def sem(name):
            taken.append(nc.alloc_semaphore(name=name))
            return taken[-1]

        k.sem = sem
        phase(nc, k)
        nc.clear_and_free_semaphores(taken)
        nc.all_engine_barrier()


def program(nc, dram):
    with ExitStack() as ctx:
        k = Places(dram)

        def sb(name, shape, dt=F32):
            return ctx.enter_context(nc.sbuf_tensor(name, shape, dt))

        def pair(name, shape, dt=F32, n=2):
            return [sb(f"{name}{i}", shape, dt) for i in range(n)]

        k.R = 4
        k.s_apart = ctx.enter_context(nc.semaphore('waits_taken_apart'))
        k.U = sb("sums", [P, 3 * UCOLS])
        k.stage = sb("stage", [P, 6 * NG * D + 6 * P])
        k.firsts = sb("window_starts", [P, PAIRS], I32)
        k.bounds = sb("loop_bounds", [1, 4], I32)
        both = sb("table_weights_and_bias", [P, 2 * (HID + D)])
        k.w0, k.bias0 = both[:, 0:HID + D], both[:, HID + D:2 * (HID + D)]
        k.scratch = both[:, 0:GROUP * HID // 2].bitcast(BF16).rearrange("p (j d) -> p j d", d=HID)
        k.w1b = sb("edge_weights", [DE, HID])
        k.g1, k.be1 = sb("g1", [P, HID]), sb("be1", [P, HID])
        k.gu, k.beu = sb("gu", [P, D]), sb("beu", [P, D])
        k.w2u, k.b2u = sb("w2u", [P, 2 * D]), sb("b2u", [1, D])
        k.lw, k.lb = sb("lw", [P, D]), sb("lb", [P, D])
        k.ident, k.before, k.ones = sb("identity", [P, P]), sb("before", [P, P]), sb("ones", [P, P])
        k.iota, k.iotab = sb("iota", [P, P]), sb("iota_bf16", [P, P], BF16)
        k.zerob = sb("zeros_bf16", [P, P], BF16)
        k.junk = sb("spare_rows", [P, 1])
        k.neghalf = sb("minus_half", [P, NT])
        k.meta = pair("indices", [P, 2 * HALF], I32)
        k.eaA = pair("edge_features_a", [DE * len(EA_A), HALF * P], BF16)
        k.eaB = pair("edge_features_b", [DE * len(EA_B), HALF * P], BF16)
        k.wA, k.wB = (sb(f"edge_weights_{n}", [DE * len(e), HID], BF16) for n, e in (("a", EA_A), ("b", EA_B)))
        k.local, k.beyond = pair("local", [P, HALF]), pair("beyond", [P, HALF])
        k.bits, k.digits = pair("bits", [P, 4 * HALF], I32), pair("digits", [P, 4 * HALF])
        k.src_lo, k.src_hi, k.dst_lo, k.dst_hi = ([d[:, i * HALF:(i + 1) * HALF] for d in k.digits] for i in range(4))
        k.gidx, k.target = pair("hyper_index", [P, HALF], I32), pair("target", [P, HALF], I32)
        k.w_row, k.w_act = pair("w_row", [P, HALF]), pair("w_act", [P, HALF])
        k.oh = pair("window_mask", [P, HALF, WIN])
        k.lo, k.hi = pair("low_mask", [P, HALF, P], BF16), pair("high_mask", [P, HALF, NT], BF16)
        k.ones_bf = sb("ones_bf16", [P, P], BF16)
        k.ohb, k.oha = [t[:, 0, :] for t in k.lo], [t[:, 0, :] for t in k.hi]
        k.ssq, k.var, k.rstd = pair("ssq", [P, HALF]), pair("var", [P, HALF]), pair("rstd", [P, HALF])
        k.beyond_count, k.dvr = sb("beyond_count", [P, NT]), sb("dvr", [P, NT])
        k.w_last, k.w_pt, k.w_de = sb("w_last", [P, 1]), sb("w_pt", [P, HT]), sb("w_de", [P, HT])
        k.nst = [both[:, i * 6 * NG:(i + 1) * 6 * NG].rearrange("p (t s) -> p t s", s=6) for i in range(2)]
        k.nmv = [both[:, (12 + 4 * i) * NG:(16 + 4 * i) * NG].rearrange("p (t s) -> p t s", s=2) for i in range(2)]
        k.nvar, k.nrs = ([both[:, (20 + 4 * n + 2 * i) * NG:(22 + 4 * n + 2 * i) * NG] for i in range(2)]
                         for n in range(2))
        k.mask_lo = [k.stage[:, i * P:(i + 1) * P] for i in range(2)]
        k.mask_hi = [k.stage[:, (2 + i) * P:(3 + i) * P] for i in range(2)]
        k.ut = [k.stage[:, 6 * NG * D + 3 * P * i:6 * NG * D + 3 * P * (i + 1)].rearrange("p (c n) -> p c n", c=3)
                for i in range(2)]

        def pb(name, cols):
            return ctx.enter_context(nc.psum_tensor(name, [P, cols], F32))

        k.psH = [pb("ps_tiles0", GROUP * HID), pb("ps_tiles1", GROUP * HID)]
        k.psA, k.psB, k.psC = pb("ps_a", 512), pb("ps_b", 512), pb("ps_c", 512)
        message_passing(nc, k)


def kernel(**inputs):
    import numpy as np
    import concourse.bacc as bacc
    from concourse.bass_utils import run_bass_kernel_spmd

    def padded(a, n, fill):
        a = np.asarray(a)
        return np.concatenate([a, np.full((n - a.shape[0],) + a.shape[1:], fill, a.dtype)])

    slots = (TILES + BODY) * P
    src = padded(inputs["src"], slots, N_NODES).reshape(-1, HALF, P)
    dst = padded(inputs["dst"], slots, FAR).reshape(-1, HALF, P)
    first = padded(np.asarray(inputs["dst"])[::2 * P], PAIRS + 8, N_NODES)[:PAIRS]
    ea = padded(inputs["edge_attr_32"], TILES * P, 0).reshape(PAIRS, 2 * P, DE)
    w = padded(inputs["L1_gnn_hyperedge_weight"], HP, 0)
    arrays = {
        "x": padded(inputs["x"], NP, 0),
        "meta_d": np.concatenate([src.transpose(0, 2, 1), dst.transpose(0, 2, 1)], axis=2),
        "src_d": src,
        "src_pt": src.reshape(-1, P)[:TILES].T,
        "src_tiles": src.reshape(-1, P, 1), "dst_tiles": dst.reshape(-1, P, 1),
        "dst_pt": dst.reshape(-1, P)[:TILES].T,
        "pair_first": first,
        "ea_d": ea.transpose(0, 2, 1),
        "W1": inputs["L0_gnn_W1"], "b1": inputs["L0_gnn_b1"], "g1_d": inputs["L0_gnn_g1"],
        "be1_d": inputs["L0_gnn_be1"], "W2T": np.asarray(inputs["L0_gnn_W2"]).T, "b2": inputs["L0_gnn_b2"],
        "Wu": inputs["L0_gnn_Wu"], "bu": inputs["L0_gnn_bu"], "gu_d": inputs["L0_gnn_gu"],
        "beu_d": inputs["L0_gnn_beu"], "w_d": w.reshape(HP, 1), "w_pt_d": w.reshape(HT, P).T,
        "LWT": np.asarray(inputs["L1_gnn_W"]).T, "lb_d": inputs["L1_gnn_b"],
    }
    arrays = {n: np.ascontiguousarray(a) for n, a in arrays.items()}
    nc = bacc.Bacc("TRN2", target_bir_lowering=False, num_devices=1)
    dram = {n: nc.dram_tensor(n, a.shape, mybir.dt.from_np(a.dtype), kind="ExternalInput").ap()
            for n, a in arrays.items()}
    for name, cols in (("p_tab", HID), ("hwu_tab", D), ("xh_tab", D), ("x1_tab", D), ("xp_tab", D)):
        dram[name] = nc.dram_tensor(name, (NP, cols), F32).ap()
    dram["ea_parts"] = [nc.dram_tensor(f"ea_part{n}", (PAIRS, DE, 2 * P), BF16).ap() for n in range(3)]
    dram["digit_tab"] = nc.dram_tensor("digit_tab", (P, 2 * BODIES, 3 * HALF), F32).ap()
    dram["g_tab"] = nc.dram_tensor("g_tab", (HP, D), F32).ap()
    dram["acc"] = [nc.dram_tensor(f"acc{r}", (NP + P, D), F32).ap() for r in range(4)]
    dram["out"] = nc.dram_tensor("out", (N_NODES, D), F32, kind="ExternalOutput").ap()
    program(nc, dram)
    return run_bass_kernel_spmd(nc, [arrays], core_ids=[0]).results[0]["out"]
```

```python
import concourse.bass as bass
from concourse import mybir
from contextlib import ExitStack

F32 = mybir.dt.float32
BF16 = mybir.dt.bfloat16
I32 = mybir.dt.int32
ALU = mybir.AluOpType
ACT = mybir.ActivationFunctionType
AXX = mybir.AxisListType.X
ds = bass.ds

P = 128
N_NODES, N_EDGES, N_HYPER = 12500, 200000, 2500
D, HID, DE = 128, 256, 32
EPS = 1e-5
GROUP = 4
HALF = 2 * GROUP
BODY = 2 * HALF
TILES = -(-N_EDGES // (P * BODY)) * BODY
BODIES = TILES // BODY
PAIRS = TILES // 2
WIN = 32
NT = -(-N_NODES // P)
NP = NT * P
UCOLS = max(N_NODES + WIN, NP)
SCATTER_TABLES = 4
NG = 7
NGROUPS = NT // NG
HT = -(-N_HYPER // P)
HP = HT * P
EA_A = ((0, 0), (0, 1), (0, 2), (1, 0))
EA_B = ((1, 1), (2, 0))
FAR_COLS = NP // 32
FAR_CHUNKS = NP // FAR_COLS
FAR_HCHUNKS = -(-HP // FAR_COLS)
FAR = 1 << 20
assert FAR_COLS <= 512 and FAR_CHUNKS * FAR_COLS == NP
assert NT % (2 * NG) == 0 and TILES % BODY == 0


class Places:

    def __init__(self, dram):
        self.x, self.meta_d, self.src_d = dram["x"], dram["meta_d"], dram["src_d"]
        self.src_tiles, self.dst_tiles, self.dst_pt = dram["src_tiles"], dram["dst_tiles"], dram["dst_pt"]
        self.pair_first, self.ea_d, self.W1 = dram["pair_first"], dram["ea_d"], dram["W1"]
        self.b1, self.g1_d, self.be1_d = dram["b1"], dram["g1_d"], dram["be1_d"]
        self.W2T, self.b2, self.Wu = dram["W2T"], dram["b2"], dram["Wu"]
        self.bu, self.gu_d, self.beu_d = dram["bu"], dram["gu_d"], dram["beu_d"]
        self.w_d, self.w_pt_d, self.LWT = dram["w_d"], dram["w_pt_d"], dram["LWT"]
        self.lb_d, self.p_tab, self.hwu_tab = dram["lb_d"], dram["p_tab"], dram["hwu_tab"]
        self.xh_tab, self.x1_tab, self.xp_tab = dram["xh_tab"], dram["x1_tab"], dram["xp_tab"]
        self.ea_parts, self.g_tab, self.src_pt = dram["ea_parts"], dram["g_tab"], dram["src_pt"]
        self.acc, self.out, self.digit_tab = dram["acc"], dram["out"], dram["digit_tab"]
        self.w_flat = dram["w_flat"]


def wait_apart(k, eng, sem, value):
    eng.wait_ge(sem, value)
    eng.sem_inc(k.s_apart, 1)


class Order:

    def __init__(self, eng, sem, base=0):
        self.eng, self.sem, self.base, self.n = eng, sem, base, 0

    def __call__(self, ins):
        ins.then_inc(self.sem, 1)
        self.n += 1
        return self.base + self.n

    def wait(self, value=None):
        self.eng.wait_ge(self.sem, self.base + self.n if value is None else value)



def setup_phase(nc, k):
    s_w = k.sem("weights_loaded")
    s_d = k.sem("dst_loaded")
    s_iota = k.sem("pool_constants")
    s_v = k.sem("setup_vector_order")
    s_fold = k.sem("folded_products")
    s_row = k.sem("row_maxima")
    s_z = k.sem("setup_tables_written")
    s_dig = k.sem("digits_ready")
    s_wp = k.sem("edge_weight_parts")
    s_parts = k.sem("edge_weights_stacked")
    NW = 14
    dst_all = k.U[:, 0:TILES].bitcast(I32)
    active = k.U[:, TILES:2 * TILES]
    reach = k.U[:, 2 * TILES:3 * TILES]
    tile_no = k.U[:, 3 * TILES:4 * TILES]
    local = k.U[:, 4 * TILES:5 * TILES]
    low = k.U[:, 5 * TILES:6 * TILES]
    w2t = k.U[:, 6 * TILES:6 * TILES + HID]
    wu_bot = k.U[:, 6 * TILES + HID:6 * TILES + HID + D]
    b2col = k.U[:, 6 * TILES + HID + D:6 * TILES + HID + D + 1]
    most = k.U[:, 6 * TILES + HID + D + 2:6 * TILES + HID + D + 4]
    mean = k.U[:, 6 * TILES + HID + D + 4:6 * TILES + HID + D + 7]
    rowmax = k.U[0:1, 6 * TILES + HID + D + 8:6 * TILES + HID + D + 16]
    w_part = k.U[0:DE, 6 * TILES + HID + D + 16:6 * TILES + HID + D + 16 + 3 * HID // 2].bitcast(BF16)\
        .rearrange("p (m d) -> p m d", d=HID)
    w_rest = k.U[0:DE, 6 * TILES + 3 * HID + D + 16:6 * TILES + 4 * HID + D + 16]
    at = 7 * TILES
    src_all, low_bits, high_bits = (k.U[:, at + i * TILES:at + (i + 1) * TILES].bitcast(I32) for i in range(3))
    at += 3 * TILES
    digits = k.U[:, at:at + 3 * TILES].rearrange("p (h d j) -> p h d j", d=3, j=HALF)
    with nc.Block() as block:

        @block.sync
        def _(sp):
            sp.dma_start(dst_all, k.dst_pt).then_inc(s_d, 16)
            sp.dma_start(src_all, k.src_pt).then_inc(s_d, 16)
            sp.dma_start(k.firsts[:, :], k.pair_first.partition_broadcast(P)).then_inc(s_d, 16)
            sp.dma_start(k.w0[:, 0:HID], k.W1[0:D, :]).then_inc(s_w, 16)
            sp.dma_start(k.w0[:, HID:HID + D], k.Wu[0:D, :]).then_inc(s_w, 16)
            sp.dma_start(k.w1b[:, :], k.W1[D:D + DE, :]).then_inc(s_w, 16)
            sp.dma_start(k.bias0[:, 0:HID], k.b1.partition_broadcast(P)).then_inc(s_w, 16)
            sp.dma_start(k.bias0[:, HID:HID + D], k.bu.partition_broadcast(P)).then_inc(s_w, 16)
            sp.dma_start(k.g1[:, :], k.g1_d.partition_broadcast(P)).then_inc(s_w, 16)
            sp.dma_start(k.be1[:, :], k.be1_d.partition_broadcast(P)).then_inc(s_w, 16)
            sp.dma_start(k.gu[:, :], k.gu_d.partition_broadcast(P)).then_inc(s_w, 16)
            sp.dma_start(k.beu[:, :], k.beu_d.partition_broadcast(P)).then_inc(s_w, 16)
            sp.dma_start(w2t, k.W2T).then_inc(s_w, 16)
            sp.dma_start(wu_bot, k.Wu[D:2 * D, :]).then_inc(s_w, 16)
            sp.dma_start(b2col, k.b2.rearrange("(p o) -> p o", o=1)).then_inc(s_w, 16)
            sp.dma_start(k.lw[:, :], k.LWT).then_inc(s_w, 16)
            sp.dma_start(k.lb[:, :], k.lb_d.partition_broadcast(P)).then_inc(s_w, 16)
            n = 0
            sp.wait_ge(s_dig, 1)
            sp.dma_start(k.digit_tab[:, 0:2 * BODIES, :].rearrange("p h c -> p (h c)"),
                         digits.rearrange("p h d j -> p (h d j)")).then_inc(s_z, 16)
            sp.dma_start(k.digit_tab[:, 2 * BODIES:2 * BODIES + 2, :].rearrange("p h c -> p (h c)"),
                         digits[:, 0:2, :, :].rearrange("p h d j -> p (h d j)")).then_inc(s_z, 16)
            n += 32
            sp.wait_ge(s_wp, 1)
            for to, blocks in ((k.wA, EA_A), (k.wB, EA_B)):
                for i, (_, m) in enumerate(blocks):
                    sp.dma_start(to[DE * i:DE * (i + 1), :], w_part[:, m, :]).then_inc(s_parts, 16)
            sp.wait_ge(s_parts, 16 * len(EA_A + EA_B))
            sp.wait_ge(s_z, n)

        @block.gpsimd
        def _(gp):
            gp.memset(k.neghalf[:, :], -0.5).then_inc(s_iota, 1)
            gp.memset(k.ident[:, :], 0.0).then_inc(s_iota, 1)
            gp.memset(k.before[:, :], 1.0).then_inc(s_iota, 1)
            gp.memset(k.ones[:, :], 1.0).then_inc(s_iota, 1)
            gp.memset(k.ones_bf[:, :], 1.0).then_inc(s_iota, 1)
            gp.memset(k.zerob[:, :], 0.0).then_inc(s_iota, 1)
            gp.iota(k.iota[:, :], [[1, P]], base=0, channel_multiplier=0,
                    allow_small_or_imprecise_dtypes=True).then_inc(s_iota, 1)
            gp.iota(k.iotab[:, :], [[1, P]], base=0, channel_multiplier=0,
                    allow_small_or_imprecise_dtypes=True).then_inc(s_iota, 1)
            gp.iota(k.junk[:, :], [[0, 1]], base=NP, channel_multiplier=1,
                    allow_small_or_imprecise_dtypes=True).then_inc(s_iota, 1)
            gp.iota(tile_no, [[1, TILES]], base=1, channel_multiplier=0,
                    allow_small_or_imprecise_dtypes=True).then_inc(s_iota, 1)
            gp.wait_ge(s_iota, 10)
            gp.affine_select(out=k.ident[:, :], in_=k.ident[:, :], compare_op=ALU.not_equal, fill=1.0,
                             base=0, pattern=[[-1, P]], channel_multiplier=1).then_inc(s_iota, 1)
            gp.affine_select(out=k.before[:, :], in_=k.before[:, :], compare_op=ALU.is_ge, fill=0.0,
                             base=-1, pattern=[[-1, P]], channel_multiplier=1).then_inc(s_iota, 1)

        @block.vector
        def _(v):
            o = Order(v, s_v)
            v.wait_ge(s_iota, 12)
            v.wait_ge(s_d, 48)
            o(v.tensor_scalar(active, dst_all, float(N_HYPER), None, ALU.is_lt))
            firsts = k.firsts[:, 0:PAIRS].unsqueeze(2).to_broadcast([P, PAIRS, 2])
            o(v.tensor_tensor(local.rearrange("p (a b) -> p a b", b=2),
                              dst_all.rearrange("p (a b) -> p a b", b=2), firsts, ALU.subtract))
            o.wait()
            o(v.tensor_copy(digits[:, :, 0, :], local.rearrange("p (h j) -> p h j", j=HALF)))
            o(v.tensor_scalar(low_bits, src_all, P - 1, None, ALU.bitwise_and))
            o(v.tensor_scalar(high_bits, src_all, P.bit_length() - 1, None, ALU.logical_shift_right))
            o.wait()
            o(v.tensor_copy(digits[:, :, 1, :], low_bits.rearrange("p (h j) -> p h j", j=HALF)))
            o(v.scalar_tensor_tensor(digits[:, :, 2, :], active.rearrange("p (h j) -> p h j", j=HALF), -4.0 * P,
                                     high_bits.rearrange("p (h j) -> p h j", j=HALF), ALU.mult, ALU.subtract))
            o(v.tensor_tensor(reach, active, tile_no, ALU.mult))
            o(v.tensor_scalar(low, local, 0.0, None, ALU.is_lt))
            o.wait()
            o(v.tensor_reduce(most[:, 0:1], reach, AXX, ALU.max))
            o(v.tensor_scalar(local, local, float(WIN), None, ALU.is_ge))
            o.wait()
            o(v.tensor_tensor(low, low, local, ALU.max))
            o(v.tensor_scalar(active, dst_all, float(N_NODES), None, ALU.is_lt))
            o.wait()
            o(v.tensor_tensor(low, low, active, ALU.mult))
            o.wait()
            o(v.tensor_reduce(most[:, 1:2], low, AXX, ALU.max))
            o.wait()
            v.sem_inc(s_row, 1)
            v.sem_inc(s_dig, 1)
            v.wait_ge(s_w, 16 * NW)
            o(v.tensor_reduce(mean[:, 0:1], k.w0[:, 0:HID], AXX, ALU.add))
            o(v.tensor_reduce(mean[0:DE, 1:2], k.w1b[:, :], AXX, ALU.add))
            o(v.tensor_reduce(mean[:, 2:3], k.bias0[:, 0:HID], AXX, ALU.add))
            o.wait()
            o(v.tensor_scalar(mean[:, 0:3:2], mean[:, 0:3:2], 1.0 / HID, None, ALU.mult))
            o(v.tensor_scalar(mean[0:DE, 1:2], mean[0:DE, 1:2], 1.0 / HID, None, ALU.mult))
            o.wait()
            o(v.tensor_scalar(k.w0[:, 0:HID], k.w0[:, 0:HID], mean[:, 0:1], None, ALU.subtract))
            o(v.tensor_scalar(k.w1b[:, :], k.w1b[:, :], mean[0:DE, 1:2], None, ALU.subtract))
            o(v.tensor_scalar(k.bias0[:, 0:HID], k.bias0[:, 0:HID], mean[:, 2:3], None, ALU.subtract))
            o.wait()
            o(v.tensor_copy(w_part[:, 0, :], k.w1b[:, :]))
            o.wait()
            o(v.tensor_tensor(w_rest, k.w1b[:, :], w_part[:, 0, :], ALU.subtract))
            o.wait()
            o(v.tensor_copy(w_part[:, 1, :], w_rest))
            o.wait()
            o(v.tensor_tensor(w_part[:, 2, :], w_rest, w_part[:, 1, :], ALU.subtract))
            o.wait()
            v.sem_inc(s_wp, 1)
            v.wait_ge(s_row, 2)
            o(v.tensor_reduce(rowmax[:, 0:1], k.psA[0:1, 0:P], AXX, ALU.max))
            o(v.tensor_reduce(rowmax[:, 1:2], k.psA[0:1, P:2 * P], AXX, ALU.max))
            o.wait()
            o(v.tensor_scalar(k.bounds[:, 0:1], rowmax[:, 0:1], float(BODY - 1), float(BODY), ALU.add, ALU.max))
            for i, most_trips in ((1, PAIRS), (2, FAR_CHUNKS), (3, FAR_HCHUNKS), (4, BODIES)):
                o(v.tensor_scalar(k.bounds[:, i:i + 1], rowmax[:, 1:2], float(most_trips - 1), 1.0, ALU.mult, ALU.add))
            o.wait()
            o(v.tensor_scalar(k.bounds[:, 0:1], k.bounds[:, 0:1], BODY.bit_length() - 1, None,
                              ALU.logical_shift_right))
            v.wait_ge(s_fold, 1)
            o(v.tensor_copy(k.w2u[:, 0:D], k.psB[:, 0:D]))
            o(v.tensor_copy(k.w2u[:, D:2 * D], k.psB[:, D:2 * D]))
            o(v.tensor_copy(k.b2u[0:1, :], k.psB[0:1, 2 * D:3 * D]))
            o.wait()

        @block.tensor
        def _(pe):
            pe.wait_ge(s_iota, 12)
            pe.wait_ge(s_row, 1)
            nc.tensor.matmul(k.psA[0:1, 0:P], most[:, 0:1], k.ident[:, :], start=True, stop=True)
            nc.tensor.matmul(k.psA[0:1, P:2 * P], most[:, 1:2], k.ident[:, :], start=True,
                             stop=True).then_inc(s_row, 1)
            pe.wait_ge(s_w, 16 * NW)
            nc.tensor.matmul(k.psB[:, 0:D], w2t[:, 0:D], wu_bot, start=True, stop=True)
            nc.tensor.matmul(k.psB[:, D:2 * D], w2t[:, D:2 * D], wu_bot, start=True, stop=True)
            nc.tensor.matmul(k.psB[0:1, 2 * D:3 * D], b2col, wu_bot, start=True, stop=True).then_inc(s_fold, 1)


def node_tables(nc, k):
    s_x = [k.sem(f"x_loaded{h}") for h in range(2)]
    s_var = k.sem("x_variance")
    s_rstd = k.sem("x_rstd")
    s_h = k.sem("h_ready")
    s_xh = k.sem("xh_ready")
    s_t = k.sem("hT_in_psum")
    s_hT = k.sem("hT_ready")
    s_p = k.sem("table_product")
    s_pw = k.sem("table_rows_ready")
    s_st = [k.sem(f"tables_stored{h}") for h in range(2)]
    s_xs = [k.sem(f"xh_stored{h}") for h in range(2)]
    s_v = k.sem("tables_vector_order")
    s_ef = [k.sem(f"features_loaded{h}") for h in range(2)]
    s_hi = k.sem("features_high")
    s_r = k.sem("features_rest")
    s_mid = k.sem("features_middle")
    s_lo = k.sem("features_low")
    s_es = [k.sem(f"feature_parts_stored{h}") for h in range(2)]
    at = [0]

    def take(n):
        at[0] += n
        return k.U[:, at[0] - n:at[0]]

    xg = [take(NG * D).rearrange("p (t d) -> p t d", d=D) for _ in range(2)]
    hg = [take(NG * D).rearrange("p (t d) -> p t d", d=D) for _ in range(2)]
    xh = [take(NG * D).rearrange("p (t d) -> p t d", d=D) for _ in range(2)]
    rows = [take(NG * (HID + D)).rearrange("p (t d) -> p t d", d=HID + D) for _ in range(2)]
    hT = [take(P) for _ in range(2)]
    stats = [take(NG * 6).rearrange("p (t d) -> p t d", d=6) for _ in range(2)]
    mv = [take(NG * 2).rearrange("p (t d) -> p t d", d=2) for _ in range(2)]
    var = [take(NG) for _ in range(2)]
    rstd = [take(NG) for _ in range(2)]
    C = TILES * DE // NGROUPS
    flat = k.ea_d.rearrange("a f e -> (a f e)").rearrange("(p c) -> p c", p=P)
    parts_v = [t.rearrange("a f e -> (a f e)").rearrange("(p c) -> p c", p=P) for t in k.ea_parts]
    full, rest = [take(C) for _ in range(2)], [take(C) for _ in range(2)]
    part = [take(3 * C // 2).bitcast(BF16).rearrange("p (n c) -> p n c", n=3) for _ in range(2)]
    assert at[0] <= 3 * UCOLS
    psT = [k.psA, k.psB]
    psP = [k.psH[0], k.psH[1]]
    x_v = k.x.rearrange("(g t p) d -> g p t d", p=P, t=NG)
    xh_v = k.xh_tab.rearrange("(g t p) d -> g p t d", p=P, t=NG)
    p_v = k.p_tab.rearrange("(g t p) d -> g p t d", p=P, t=NG)
    hwu_v = k.hwu_tab.rearrange("(g t p) d -> g p t d", p=P, t=NG)
    LAST = NGROUPS // 2 - 1

    with nc.Block() as block:

        @block.sync
        def _(sp):
            def load(g, h):
                sp.dma_start(xg[h], x_v[ds(g, 1)].rearrange("o p t d -> (o p) t d")).then_inc(s_x[h], 16)

            def store(g, h):
                sp.wait_ge(s_xh, g + 1)
                sp.dma_start(xh_v[ds(g, 1)].rearrange("o p t d -> (o p) t d"), xh[h]).then_inc(s_xs[h], 16)
                sp.wait_ge(s_pw, NG * (g + 1))
                sp.dma_start(p_v[ds(g, 1)].rearrange("o p t d -> (o p) t d"),
                             rows[h][:, :, 0:HID]).then_inc(s_st[h], 16)
                sp.dma_start(hwu_v[ds(g, 1)].rearrange("o p t d -> (o p) t d"),
                             rows[h][:, :, HID:HID + D]).then_inc(s_st[h], 16)

            def load_features(g, h):
                sp.dma_start(full[h], flat[:, ds(g * C, C)]).then_inc(s_ef[h], 16)

            def store_parts(g, h):
                for n in range(3):
                    sp.dma_start(parts_v[n][:, ds(g * C, C)], part[h][:, n, :]).then_inc(s_es[h], 16)

            for h in range(2):
                sp.sem_inc(s_st[h], 32)
                sp.sem_inc(s_xs[h], 16)
                sp.sem_inc(s_es[h], 48)
                load(h, h)
            for h in range(2):
                load_features(h, h)
            with sp.Fori(0, LAST) as b:
                for h in range(2):
                    sp.wait_ge(s_xh, 2 * b + h + 1)
                    load(2 * b + 2 + h, h)
                    wait_apart(k, sp, s_r, 2 * b + h + 1)
                    load_features(2 * b + 2 + h, h)
                    store(2 * b + h, h)
                    wait_apart(k, sp, s_lo, 2 * b + h + 1)
                    store_parts(2 * b + h, h)
            for h in range(2):
                store(2 * LAST + h, h)
                sp.wait_ge(s_lo, 2 * LAST + h + 1)
                store_parts(2 * LAST + h, h)
            for h in range(2):
                sp.wait_ge(s_st[h], 32 * (LAST + 2))
                sp.wait_ge(s_xs[h], 16 * (LAST + 2))
                sp.wait_ge(s_es[h], 48 * (LAST + 2))

        @block.gpsimd
        def _(gp):
            with gp.Fori(0, LAST + 1) as b:
                for h in range(2):
                    g = 2 * b + h
                    gp.wait_ge(s_var, g + 1)
                    gp.tensor_tensor(rstd[h], var[h], k.neghalf[:, 0:NG], ALU.pow).then_inc(s_rstd, 1)
                    gp.wait_ge(s_h, g + 1)
                    gp.wait_ge(s_xs[h], 16 * b + 16)
                    gp.tensor_tensor(xh[h], xg[h], hg[h], ALU.add).then_inc(s_xh, 1)

        @block.vector
        def _(v):
            K = 3 * NG

            def products(g, h):
                v.wait_ge(s_st[h], 16 * (g - h) + 32)
                for t in range(NG):
                    v.wait_ge(s_p, NG * g + t + 1 + 2)
                    v.tensor_tensor(rows[h][:, t, :], psP[(NG * h + t) % 2][:, 0:HID + D], k.bias0[:, :],
                                    ALU.add).then_inc(s_pw, 1)

            def low_part(g, h):
                v.wait_ge(s_mid, g + 1)
                v.tensor_tensor(part[h][:, 2, :], rest[h], part[h][:, 1, :], ALU.subtract).then_inc(s_lo, 1)

            def slot(g, h, prev):
                o = Order(v, s_v, K * g)
                v.wait_ge(s_x[h], 8 * (g - h) + 16)
                for t in range(NG):
                    o(v.bn_stats(stats[h][:, t, :], xg[h][:, t, :]))
                for t in range(NG):
                    wait_apart(k, v, s_v, o.base + t + 1)
                    o(v.bn_aggr(mv[h][:, t, :], stats[h][:, t, :]))
                o.wait()
                v.tensor_scalar(var[h], mv[h][:, :, 1], EPS, None, ALU.add).then_inc(s_var, 1)
                if prev:
                    products(g - 1, 1 - h)
                    low_part(g - 1, 1 - h)
                    if not isinstance(g, int) or g >= 2:
                        v.wait_ge(s_xh, g - 1)
                v.wait_ge(s_rstd, g + 1)
                for t in range(NG):
                    o(v.tensor_scalar(hg[h][:, t, :], xg[h][:, t, :], mv[h][:, t, 0:1], rstd[h][:, t:t + 1],
                                      ALU.subtract, ALU.mult))
                o.wait()
                v.tensor_scalar(hg[h], hg[h], 0.0, None, ALU.max).then_inc(s_h, 1)
                v.wait_ge(s_hi, g + 1)
                v.tensor_tensor(rest[h], full[h], part[h][:, 0, :], ALU.subtract).then_inc(s_r, 1)

            slot(0, 0, False)
            slot(1, 1, True)
            with v.Fori(1, LAST + 1) as b:
                for h in range(2):
                    slot(2 * b + h, h, True)
            products(2 * LAST + 1, 1)
            low_part(2 * LAST + 1, 1)

        @block.scalar
        def _(a):
            with a.Fori(0, LAST + 1) as b:
                for h in range(2):
                    g = 2 * b + h
                    a.wait_ge(s_ef[h], 16 * b + 16)
                    a.wait_ge(s_es[h], 48 * b + 48)
                    a.copy(part[h][:, 0, :], full[h]).then_inc(s_hi, 1)
                    for n in range(NG * h, NG * (h + 1)):
                        a.wait_ge(s_t, 2 * NG * b + n + 1)
                        a.wait_ge(s_p, 2 * NG * b + n + 1)
                        a.copy(hT[n % 2], psT[n % 2][:, 0:P]).then_inc(s_hT, 1)
                    a.wait_ge(s_r, g + 1)
                    a.copy(part[h][:, 1, :], rest[h]).then_inc(s_mid, 1)

        @block.tensor
        def _(pe):
            pe.sem_inc(s_p, 2)

            def transpose(b, n):
                h, t = divmod(n, NG)
                if t == 0:
                    pe.wait_ge(s_h, 2 * b + h + 1)
                if isinstance(b, int) and 2 * NG * b + n < 2:
                    pass
                else:
                    pe.wait_ge(s_hT, 2 * NG * b + n - 1)
                nc.tensor.transpose(psT[n % 2][:, 0:P], hg[h][:, t, :], k.ident[:, :]).then_inc(s_t, 1)

            def product(b, n, first=False):
                pe.wait_ge(s_hT, 2 * NG * b + n + 1)
                if not (isinstance(b, int) and 2 * NG * b + n < 2):
                    pe.wait_ge(s_pw, 2 * NG * b + n - 1)
                nc.tensor.matmul(psP[n % 2][:, 0:HID + D], hT[n % 2], k.w0[:, :], start=True,
                                 stop=True).then_inc(s_p, 1)

            def body(b):
                for n in range(2 * NG):
                    transpose(b, n)
                    if n % NG:
                        product(b, n - 1)
                    if n % NG == NG - 1:
                        product(b, n)

            body(0)
            with pe.Fori(1, LAST + 1) as b:
                body(b)



def edge_messages(nc, k):
    s_meta = [k.sem(f"indices_loaded{h}") for h in range(2)]
    s_ea = [k.sem(f"edge_features_loaded{h}") for h in range(2)]
    s_g = [k.sem(f"rows_gathered{j}") for j in range(HALF)]
    s_tile = k.sem("tile_in_psum")
    s_add = k.sem("hidden_ready")
    s_sq = k.sem("squares_summed")
    s_var = k.sem("edge_variance")
    s_rstd = k.sem("edge_rstd")
    s_z = k.sem("normalised")
    s_gelu = k.sem("gelu_done")
    s_dig = [k.sem(f"digits_loaded{h}") for h in range(2)]
    s_oh = k.sem("window_masks")
    s_lo = k.sem("histogram_low_masks")
    s_far = k.sem("histogram_distances")
    s_hi = k.sem("histogram_high_masks")
    s_hist = k.sem("histogram_added")
    s_seg = k.sem("windows_summed")
    s_u = k.sem("windows_kept")
    s_v = k.sem("edge_vector_order")
    s_u0 = k.sem("sums_zeroed")
    s_acc = k.sem("scatter_tables_zeroed")
    HALVES = 2 * BODIES
    PH = HALF // 2

    rows = k.stage[:, 0:HALF * HID].rearrange("p (j d) -> p j d", d=HID)
    z = [k.stage[:, HALF * (1 + h) * HID:HALF * (2 + h) * HID].rearrange("p (j d) -> p j d", d=HID) for h in range(2)]
    psH = [k.psH[q // 2][:, (q % 2) * 2 * HID:(q % 2 + 1) * 2 * HID].rearrange("p (j d) -> p j d", d=HID)
           for q in range(PH)]
    psU = [t[:, 0:2 * 3 * WIN].rearrange("p (q c w) -> p q c w", q=2, c=3) for t in (k.psA, k.psB)]
    psC = k.psC[:, 0:NT]
    U3 = k.U[:, :].rearrange("p (c n) -> p c n", c=3)
    oh_bf = [t[:, :, :].bitcast(BF16)[:, :, 1:2 * WIN:2] for t in k.oh]

    with nc.Block() as block:

        @block.sync
        def _(sp):
            def load_meta(b, h):
                sp.dma_start(k.meta[h][:, :], k.meta_d[ds(2 * b + h, 1)].rearrange("o p c -> (o p) c"))\
                  .then_inc(s_meta[h], 16)

            def load_digits(b, h):
                sp.dma_start(k.digits[h][:, :], k.digit_tab[:, ds(2 * b + h, 1), :]
                             .rearrange("p o c -> p (o c)")).then_inc(s_dig[h], 16)

            def load_ea(b, h):
                for to, blocks in ((k.eaA[h], EA_A), (k.eaB[h], EA_B)):
                    for i, (n, _) in enumerate(blocks):
                        sp.dma_start(to[DE * i:DE * (i + 1), :].rearrange("f (q e) -> f q e", e=2 * P),
                                     k.ea_parts[n][ds(2 * PH * b + PH * h, PH)].rearrange("q f e -> f q e"))\
                          .then_inc(s_ea[h], 16)

            def zero_rows(n):
                for r in range(SCATTER_TABLES):
                    sp.dma_start(k.acc[r][ds(n * P, P), :].rearrange("p (i d) -> p i d", i=2),
                                 k.zerob[:, :].bitcast(F32).unsqueeze(1).to_broadcast([P, 2, D // 2]))\
                      .then_inc(s_acc, 16)

            for h in range(2):
                load_meta(0, h)
                load_digits(0, h)
                load_ea(0, h)
            with sp.Fori(0, BODIES - 1) as b:
                zero_rows(b)
                for h in range(2):
                    wait_apart(k, sp, s_tile, BODY * b + HALF * (h + 1))
                    load_ea(b + 1, h)
                    wait_apart(k, sp, s_lo, 2 * b + h + 1)
                    wait_apart(k, sp, s_oh, 2 * b + h + 1)
                    wait_apart(k, sp, s_far, 2 * b + h + 1)
                    load_digits(b + 1, h)
                    wait_apart(k, sp, s_add, PH * (2 * b + h + 1))
                    load_meta(b + 1, h)
            for n in range(BODIES - 1, NT):
                zero_rows(n)
            sp.wait_ge(s_acc, 16 * SCATTER_TABLES * NT)

        @block.gpsimd
        def _(gp):
            def gather(h, j):
                gp.indirect_dma_start(out=rows[:, j, :], out_offset=None, in_=k.p_tab[:, :],
                                      in_offset=bass.IndirectOffsetOnAxis(ap=k.meta[h][:, j:j + 1], axis=0))\
                  .then_inc(s_g[j], 16)

            def rstd(unit, i):
                gp.wait_ge(s_var, unit + 1)
                gp.tensor_tensor(k.rstd[i][:, :], k.var[i][:, :], k.neghalf[:, 0:HALF], ALU.pow)\
                  .then_inc(s_rstd, 1)

            def half(b, h, lead):
                H = 2 * b + h
                wait_apart(k, gp, s_meta[h], 16 * b + 16)
                for j in range(HALF):
                    if j % 2 == 0 and not (lead and h == 0):
                        wait_apart(k, gp, s_add, PH * (H - 1) + j // 2 + 1)
                    if j == GROUP - 1 and not (lead and h == 0):
                        rstd(H - 1, 1 - h)
                    gather(h, j)

            gp.sem_inc(s_rstd, 1)
            half(0, 0, True)
            gp.memset(k.U[:, 2 * UCOLS:3 * UCOLS], 0.0).then_inc(s_u0, 1)
            half(0, 1, True)
            with gp.Fori(1, BODIES) as b:
                for h in range(2):
                    half(b, h, False)
            rstd(HALVES - 1, 1)
            rstd(HALVES, 0)

        @block.tensor
        def _(pe):
            def product(b, h, q, lead):
                H = 2 * b + h
                if q == 0:
                    pe.wait_ge(s_ea[h], 16 * len(EA_A + EA_B) * (b + 1))
                if not (lead and h == 0):
                    pe.wait_ge(s_add, PH * (H - 1) + q + 1)
                for t in range(2):
                    e = (2 * q + t) * P
                    nc.tensor.matmul(psH[q][:, t, :], k.eaA[h][:, e:e + P], k.wA[:, :], start=True, stop=False)
                    nc.tensor.matmul(psH[q][:, t, :], k.eaB[h][:, e:e + P], k.wB[:, :], start=False,
                                     stop=True).then_inc(s_tile, 1)

            def histogram(H, h):
                pe.wait_ge(s_lo, H + 1)
                pe.wait_ge(s_hi, H + 1)
                for j in range(HALF):
                    last = nc.tensor.matmul(psC, k.lo[h][:, j, :], k.hi[h][:, j, :], start=False, stop=False)
                last.then_inc(s_hist, 1)

            def window_sums(gg, h, g, first):
                pe.wait_ge(s_gelu, gg + 1)
                if not first:
                    pe.wait_ge(s_u, gg)
                for q in range(2):
                    for c in range(3):
                        for i in range(2):
                            j = GROUP * g + 2 * q + i
                            left, right = ((z[h][:, j, c * P:(c + 1) * P], k.oh[h][:, j, :]) if c < 2 else
                                           (k.ones_bf[:, :], oh_bf[h][:, j, :]))
                            last = nc.tensor.matmul(psU[g][:, q, c, :], left, right, start=i == 0, stop=i == 1)
                last.then_inc(s_seg, 1)

            def slot(b, h, lead, ahead=True):
                H = 2 * b + h
                o = 1 - h
                if ahead:
                    product(b + h, o, 0, False)
                if not lead:
                    window_sums(2 * (H - 2) + 1, h, 1, False)
                if ahead:
                    product(b + h, o, 1, False)
                if not (lead and h == 0):
                    histogram(H - 1, o)
                if not (lead and h == 0):
                    window_sums(2 * (H - 1), o, 0, lead)
                if ahead:
                    product(b + h, o, 2, False)
                    product(b + h, o, 3, False)

            nc.tensor.matmul(psC, k.zerob[:, :], k.zerob[:, 0:NT], start=True, stop=False)
            for q in range(PH):
                product(0, 0, q, True)
            for h in range(2):
                slot(0, h, True)
            with pe.Fori(1, BODIES - 1) as b:
                for h in range(2):
                    slot(b, h, False)
            for h in range(2):
                slot(BODIES - 1, h, False, ahead=h == 0)
            window_sums(2 * (HALVES - 2) + 1, 0, 1, False)
            histogram(HALVES - 1, 1)
            window_sums(2 * (HALVES - 1), 1, 0, False)
            window_sums(2 * (HALVES - 1) + 1, 1, 1, False)
            nc.tensor.matmul(psC, k.zerob[:, :], k.zerob[:, 0:NT], start=False, stop=True).then_inc(s_hist, 1)

        @block.scalar
        def _(a):
            def square(H, h, j, lead):
                a.wait_ge(s_add, PH * H + j // 2 + 1)
                if not (lead and h == 0 and j < GROUP):
                    a.wait_ge(s_sq, HALF * H + j - GROUP + 1)
                i, at = (h, GROUP + j) if j < GROUP else (1 - h, j - GROUP)
                if j == 0 and not lead:
                    a.wait_ge(s_var, H - 1)
                if j == GROUP and not (lead and h == 0):
                    a.wait_ge(s_var, H)
                nc.scalar.activation(k.scratch[:, j % GROUP, :], z[h][:, j, :], ACT.Square, scale=HID ** -0.5,
                                     accum_out=k.ssq[i][:, at:at + 1]).then_inc(s_sq, 1)

            def gelu(gg, h, g):
                a.wait_ge(s_z, gg + 1)
                part = z[h][:, GROUP * g:GROUP * (g + 1), :]
                nc.scalar.activation(part, part, ACT.Gelu).then_inc(s_gelu, 1)

            def high_masks(b, h, lead):
                H = 2 * b + h
                a.wait_ge(s_dig[h], 16 * b + 16)
                if not lead:
                    a.wait_ge(s_hist, H - 1)
                for j in range(HALF):
                    last = nc.scalar.activation(k.hi[h][:, j, :], k.iota[:, 0:NT], ACT.Square,
                                                bias=k.digits[h][:, 2 * HALF + j:2 * HALF + j + 1])
                for j in range(GROUP, HALF):
                    last = nc.scalar.activation(k.lo[h][:, j, :], k.iota[:, :], ACT.Square, scale=-1.0,
                                                bias=k.digits[h][:, HALF + j:HALF + j + 1])
                last.then_inc(s_far, 1)
                a.wait_ge(s_far, H + 1)
                part = k.lo[h][:, GROUP:HALF, :]
                nc.scalar.activation(part, part, ACT.Relu, scale=-1.0, bias=k.ones[:, 0:1])
                nc.scalar.activation(k.hi[h][:, :, :], k.hi[h][:, :, :], ACT.Relu, scale=-1.0,
                                     bias=k.ones[:, 0:1]).then_inc(s_hi, 1)

            def slot(b, h, lead):
                H = 2 * b + h
                for j in range(GROUP):
                    square(H, h, j, lead)
                if not (lead and h == 0):
                    gelu(2 * (H - 1), 1 - h, 0)
                high_masks(b, h, lead)
                for j in (4, 5):
                    square(H, h, j, lead)
                if not (lead and h == 0):
                    gelu(2 * (H - 1) + 1, 1 - h, 1)
                for j in (6, 7):
                    square(H, h, j, lead)

            for h in range(2):
                slot(0, h, True)
            with a.Fori(1, BODIES) as b:
                for h in range(2):
                    slot(b, h, False)
            for g in range(2):
                gelu(2 * (HALVES - 1) + g, 1, g)

        @block.vector
        def _(v):
            def low_masks(b, h, lead):
                v.wait_ge(s_dig[h], 16 * b + 16)
                if not lead:
                    v.wait_ge(s_hist, 2 * b + h - 1)
                for j in range(GROUP):
                    last = v.tensor_scalar(k.lo[h][:, j, :], k.iotab[:, :], k.digits[h][:, HALF + j:HALF + j + 1], None,
                                           ALU.is_equal)
                last.then_inc(s_lo, 1)

            def window_masks(H, h, lead):
                if not lead:
                    v.wait_ge(s_seg, 2 * H - 2)
                v.tensor_tensor(k.oh[h][:, :, :], k.iota[:, 0:WIN].unsqueeze(1).to_broadcast([P, HALF, WIN]),
                                k.digits[h][:, 0:HALF].unsqueeze(2).to_broadcast([P, HALF, WIN]),
                                ALU.is_equal).then_inc(s_oh, 1)

            def add(b, h, q, lead):
                H = 2 * b + h
                if not lead and q % 2 == 0:
                    v.wait_ge(s_seg, 2 * H - 4 + q // 2 + 1)
                v.wait_ge(s_tile, HALF * H + 2 * q + 2)
                for j in (2 * q, 2 * q + 1):
                    v.wait_ge(s_g[j], 16 * H + 16)
                v.tensor_tensor(z[h][:, 2 * q:2 * q + 2, :], psH[q], rows[:, 2 * q:2 * q + 2, :],
                                ALU.add).then_inc(s_add, 1)

            def variance(unit, i, lead, part=slice(0, HALF)):
                v.wait_ge(s_sq, HALF * unit + GROUP if part.stop == HALF else HALF * unit)
                if not lead:
                    v.wait_ge(s_rstd, unit)
                v.tensor_scalar(k.var[i][:, part], k.ssq[i][:, part], EPS, None, ALU.add).then_inc(s_var, 1)

            def scale(o, H, h, g):
                v.wait_ge(s_rstd, H + g + 2)
                for t in range(GROUP):
                    j = GROUP * g + t
                    root = k.rstd[1 - h][:, t:t + 1] if g else k.rstd[h][:, GROUP + t:GROUP + t + 1]
                    o(v.scalar_tensor_tensor(z[h][:, j, :], z[h][:, j, :], root, k.g1[:, :], ALU.mult, ALU.mult))

            def shift(o, h, g, scaled):
                o.wait(o.base + scaled)
                part = z[h][:, GROUP * g:GROUP * (g + 1), :]
                v.tensor_tensor(part, part, k.be1[:, :].unsqueeze(1).to_broadcast([P, GROUP, HID]),
                                ALU.add).then_inc(s_z, 1)

            def starts(H):
                _, at = nc.values_load_multi_w_load_instructions(
                    k.firsts[0:1, ds(PH * H, PH)], engines=[mybir.EngineType.DVE], min_val=0, max_val=N_NODES)
                return at

            def keep(o, gg, g, q, at):
                if q == 0:
                    v.wait_ge(s_u, gg + 1)
                    v.wait_ge(s_seg, gg + 1)
                else:
                    o.wait(kept[0])
                to = U3[:, :, ds(at[2 * g + q], WIN)]
                ins = v.tensor_tensor(to, to, psU[g][:, q], ALU.add)
                if q == 0:
                    kept[0] = o(ins)
                else:
                    ins.then_inc(s_u, 1)

            kept = [None]

            def slot(o, b, h, lead):
                H = 2 * b + h
                p = 1 - h
                follow = not (lead and h == 0)
                at = None if lead else starts(H - 2)
                add(b, h, 0, lead)
                if not lead:
                    keep(o, 2 * (H - 2), 0, 0, at)
                if follow:
                    scale(o, H - 1, p, 0)
                    scaled = o.n
                add(b, h, 1, lead)
                if not lead:
                    keep(o, 2 * (H - 2), 0, 1, at)
                if follow:
                    shift(o, p, 0, scaled)
                variance(H, h, lead, slice(0 if follow else GROUP, HALF))
                low_masks(b, h, lead)
                window_masks(H, h, lead)
                add(b, h, 2, lead)
                if not lead:
                    keep(o, 2 * (H - 2) + 1, 1, 0, at)
                if follow:
                    scale(o, H - 1, p, 1)
                    scaled = o.n
                if not lead:
                    keep(o, 2 * (H - 2) + 1, 1, 1, at)
                if follow:
                    shift(o, p, 1, scaled)
                add(b, h, 3, lead)

            v.memset(k.var[0][:, 0:GROUP], 1.0).then_inc(s_u0, 1)
            v.memset(k.U[:, 0:2 * UCOLS], 0.0).then_inc(s_u0, 1)
            v.wait_ge(s_u0, 3)
            v.sem_inc(s_u, 1)
            o = Order(v, s_v)
            for h in range(2):
                slot(o, 0, h, True)
            start = o.n
            K = 2 * (HALF + 2)
            with v.Fori(1, BODIES) as b:
                o = Order(v, s_v, start + K * (b - 1))
                for h in range(2):
                    slot(o, b, h, False)
                assert o.n == K, (o.n, K)
            o = Order(v, s_v, start + K * (BODIES - 1))
            H = HALVES - 1
            at = starts(H - 1)
            for q in range(2):
                keep(o, 2 * (H - 1), 0, q, at)
            variance(HALVES, 0, False, slice(0, GROUP))
            for g in range(2):
                scale(o, H, 1, g)
                shift(o, 1, g, o.n)
            for q in range(2):
                keep(o, 2 * H - 1, 1, q, at)
            at = starts(H)
            for g in range(2):
                for q in range(2):
                    keep(o, 2 * H + g, g, q, at)
            v.wait_ge(s_u, 2 * HALVES + 1)
            v.wait_ge(s_hist, HALVES + 1)
            v.tensor_copy(k.beyond_count[:, :], psC)


def far_edges(nc, k, messages):
    layer = "far_messages" if messages else "far_hyperedges"
    chunks = FAR_CHUNKS if messages else FAR_HCHUNKS
    s_ld = k.sem(f"{layer}_loaded")
    s_g = k.sem(f"{layer}_rows_gathered")
    s_h = k.sem(f"{layer}_hidden")
    s_sq = k.sem(f"{layer}_squares")
    s_var = k.sem(f"{layer}_variance")
    s_rs = k.sem(f"{layer}_rstd")
    s_n = k.sem(f"{layer}_normalised")
    s_z = k.sem(f"{layer}_rows_ready")
    s_m = [k.sem(f"{layer}_masks{i}") for i in range(2)]
    s_p = [k.sem(f"{layer}_products{i}") for i in range(2)]
    s_k = [k.sem(f"{layer}_kept{i}") for i in range(2)]
    s_t = k.sem(f"{layer}_tiles_done")
    s_i = k.sem(f"{layer}_columns")
    s_f = [k.sem(f"{layer}_destinations{i}") for i in range(2)]
    s_v = k.sem(f"{layer}_vector_order")
    cols = HID if messages else D
    loads = 48 if messages else 32
    parts = 3 if messages else 1
    table = k.p_tab if messages else k.xp_tab
    rows = k.stage[:, 0:cols]
    columns = k.stage[:, HID:HID + FAR_COLS]
    mask = k.stage[:, HID + FAR_COLS:HID + 2 * FAR_COLS]
    at = HID + 2 * FAR_COLS
    z = k.stage[:, at:at + HID]
    square = k.stage[:, at + HID:at + 2 * HID]
    ea = k.stage[0:DE, at + 2 * HID:at + 2 * HID + P]
    at += 2 * HID + P
    local, low, high, far, ssq, rstd = (k.stage[:, at + i:at + i + 1] for i in range(6))
    src = k.stage[:, at + 6:at + 7].bitcast(I32)
    dst = k.stage[:, at + 7:at + 8].bitcast(I32)
    ps = [k.psA, k.psB, k.psC]
    sums = k.U[:, :].rearrange("p (c n) -> p c n", c=3)

    def trips(eng):
        return (eng.value_load(k.bounds[0:1, 1:2], min_val=1, max_val=PAIRS),
                eng.value_load(k.bounds[0:1, 2 if messages else 3:3 if messages else 4], min_val=1, max_val=chunks))

    with nc.Block() as block:

        @block.sync
        def _(sp):
            n_pairs, _ = trips(sp)
            sp.sem_inc(s_t, 1)
            with sp.Fori(0, n_pairs) as b:
                for i in range(2):
                    tile = 2 * b + i
                    sp.wait_ge(s_t, tile + 1)
                    sp.dma_start(src, k.src_tiles[ds(tile, 1)].rearrange("o e c -> (o e) c")).then_inc(s_ld, 16)
                    sp.dma_start(dst, k.dst_tiles[ds(tile, 1)].rearrange("o e c -> (o e) c")).then_inc(s_ld, 16)
                    if messages:
                        sp.dma_start(ea, k.ea_d[ds(b, 1), :, i * P:(i + 1) * P]
                                     .rearrange("o f e -> (o f) e")).then_inc(s_ld, 16)

        @block.gpsimd
        def _(gp):
            n_pairs, _ = trips(gp)
            gp.iota(columns, [[1, FAR_COLS]], base=1, channel_multiplier=0,
                    allow_small_or_imprecise_dtypes=True).then_inc(s_i, 1)
            with gp.Fori(0, n_pairs) as b:
                for i in range(2):
                    tile = 2 * b + i
                    wait_apart(k, gp, s_ld, loads * tile + loads)
                    gp.indirect_dma_start(out=rows, out_offset=None, in_=table[:, :],
                                          in_offset=bass.IndirectOffsetOnAxis(ap=src, axis=0)).then_inc(s_g, 16)
                    if messages:
                        gp.wait_ge(s_var, tile + 1)
                        gp.tensor_tensor(rstd, ssq, k.neghalf[:, 0:1], ALU.pow).then_inc(s_rs, 1)

        @block.scalar
        def _(a):
            n_pairs, _ = trips(a)
            if messages:
                with a.Fori(0, n_pairs) as b:
                    for i in range(2):
                        tile = 2 * b + i
                        a.wait_ge(s_h, tile + 1)
                        nc.scalar.activation(square, k.psH[0][:, 0:HID], ACT.Square, scale=HID ** -0.5,
                                             accum_out=ssq).then_inc(s_sq, 1)
                        a.wait_ge(s_n, tile + 1)
                        nc.scalar.activation(z, z, ACT.Gelu).then_inc(s_z, 1)

        @block.tensor
        def _(pe):
            n_pairs, n_chunks = trips(pe)
            with pe.Fori(0, n_pairs) as b:
                for i in range(2):
                    tile = 2 * b + i
                    wait_apart(k, pe, s_g, 16 * tile + 16)
                    if messages:
                        pe.wait_ge(s_ld, loads * tile + loads)
                        nc.tensor.matmul(k.psH[0][:, 0:HID], ea, k.w1b[:, :], start=True, stop=False)
                        nc.tensor.matmul(k.psH[0][:, 0:HID], k.ident[:, :], rows, start=False,
                                         stop=True).then_inc(s_h, 1)
                        wait_apart(k, pe, s_z, tile + 1)
                        left = [z[:, 0:P], z[:, P:HID], k.ones[:, :]]
                    else:
                        left = [rows]
                    with pe.Fori(0, n_chunks) as c:
                        pe.wait_ge(s_m[i], chunks * b + c + 1)
                        for m in range(parts):
                            last = nc.tensor.matmul(ps[m][:, 0:FAR_COLS], left[m], mask, start=True, stop=True)
                        last.then_inc(s_p[i], 1)

        @block.vector
        def _(v):
            n_pairs, n_chunks = trips(v)
            K = 7 if messages else 5
            v.wait_ge(s_i, 1)
            for i in range(2):
                v.sem_inc(s_k[i], 1)
            with v.Fori(0, n_pairs) as b:
                for i in range(2):
                    tile = 2 * b + i
                    o = Order(v, s_v, K * tile)
                    v.wait_ge(s_ld, loads * tile + loads)
                    o(v.tensor_tensor(local, dst, k.firsts[:, ds(b, 1)], ALU.subtract))
                    o(v.tensor_scalar(far, dst, 1.0, None, ALU.add))
                    o.wait()
                    o(v.tensor_scalar(low, local, 0.0, None, ALU.is_lt))
                    o(v.tensor_scalar(high, local, float(WIN), None, ALU.is_ge))
                    o.wait()
                    o(v.tensor_tensor(low, low, high, ALU.max))
                    o.wait()
                    v.tensor_tensor(far, far, low, ALU.mult).then_inc(s_f[i], 1)
                    if messages:
                        v.wait_ge(s_sq, tile + 1)
                        o(v.tensor_scalar(ssq, ssq, EPS, None, ALU.add))
                        o.wait()
                        v.sem_inc(s_var, 1)
                        v.wait_ge(s_rs, tile + 1)
                        o(v.scalar_tensor_tensor(z, k.psH[0][:, 0:HID], rstd, k.g1[:, :], ALU.mult, ALU.mult))
                        o.wait()
                        v.tensor_tensor(z, z, k.be1[:, :], ALU.add).then_inc(s_n, 1)
                    with v.Fori(0, n_chunks) as c:
                        step = chunks * b + c
                        wait_apart(k, v, s_f[i], b + step + 1)
                        v.wait_ge(s_k[i], step + 1)
                        v.tensor_scalar(mask, columns, far, None, ALU.is_equal).then_inc(s_m[i], 1)
                        v.wait_ge(s_p[i], step + 1)
                        v.tensor_scalar(far, far, -float(FAR_COLS), None, ALU.add).then_inc(s_f[i], 1)
                        for m in range(parts):
                            to = sums[:, m, ds(c * FAR_COLS, FAR_COLS)]
                            last = v.tensor_tensor(to, to, ps[m][:, 0:FAR_COLS], ALU.add)
                        last.then_inc(s_k[i], 1)
                    v.wait_ge(s_k[i], chunks * b + n_chunks + 1)
                    v.sem_inc(s_t, 1)


def far_messages(nc, k):
    far_edges(nc, k, True)


def far_hyperedges(nc, k):
    far_edges(nc, k, False)


def far_degrees(nc, k):
    s_meta = [k.sem(f"far_deg_indices_loaded{h}") for h in range(2)]
    s_ix = k.sem("far_deg_indices_ready")
    s_wg = [k.sem(f"far_weights_gathered{h}") for h in range(2)]
    s_m = k.sem("far_deg_masks")
    s_mu = k.sem("far_deg_added")
    s_v = k.sem("far_deg_vector_order")
    psV = k.psA[:, 0:NT]
    IX = 10

    with nc.Block() as block:

        @block.sync
        def _(sp):
            n_bodies = sp.value_load(k.bounds[0:1, 4:5], min_val=1, max_val=BODIES)

            def load_meta(b, h):
                sp.dma_start(k.meta[h][:, :], k.meta_d[ds(2 * b + h, 1)].rearrange("o p c -> (o p) c"))\
                  .then_inc(s_meta[h], 16)

            for h in range(2):
                load_meta(0, h)
            with sp.Fori(0, n_bodies) as b:
                for h in range(2):
                    sp.wait_ge(s_wg[h], 16 * HALF * (b + 1))
                    load_meta(b + 1, h)
            for h in range(2):
                wait_apart(k, sp, s_meta[h], 16 * n_bodies + 16)

        @block.gpsimd
        def _(gp):
            n_bodies = gp.value_load(k.bounds[0:1, 4:5], min_val=1, max_val=BODIES)
            with gp.Fori(0, n_bodies) as b:
                for h in range(2):
                    wait_apart(k, gp, s_ix, 2 * b + h + 1)
                    for j in range(HALF):
                        gp.indirect_dma_start(out=k.w_row[h][:, j:j + 1], out_offset=None, in_=k.w_d[:, :],
                                              in_offset=bass.IndirectOffsetOnAxis(ap=k.gidx[h][:, j:j + 1], axis=0))\
                          .then_inc(s_wg[h], 16)

        @block.tensor
        def _(pe):
            n_bodies = pe.value_load(k.bounds[0:1, 4:5], min_val=1, max_val=BODIES)
            pe.sem_inc(s_mu, 2)
            nc.tensor.matmul(psV, k.zerob[:, :], k.zerob[:, 0:NT], start=True, stop=False)
            with pe.Fori(0, n_bodies) as b:
                for n in range(BODY):
                    pe.wait_ge(s_m, BODY * b + n + 1)
                    nc.tensor.matmul(psV, k.mask_lo[n % 2][:, :], k.mask_hi[n % 2][:, 0:NT], start=False,
                                     stop=False).then_inc(s_mu, 1)

        @block.vector
        def _(v):
            n_bodies = v.value_load(k.bounds[0:1, 4:5], min_val=1, max_val=BODIES)
            K = 2 * (IX + 1)

            def indices(o, b, h):
                v.wait_ge(s_meta[h], 16 * b + 16)
                src, dst = k.meta[h][:, 0:HALF], k.meta[h][:, HALF:2 * HALF]
                o(v.tensor_scalar(k.gidx[h][:, :], dst, float(N_HYPER - 1), None, ALU.min))
                o(v.tensor_scalar(k.beyond[h][:, :], dst, float(N_HYPER), None, ALU.is_lt))
                o(v.tensor_scalar(k.bits[h][:, 0:HALF], src, P - 1, None, ALU.bitwise_and))
                o(v.tensor_scalar(k.bits[h][:, HALF:2 * HALF], src, P.bit_length() - 1, None, ALU.logical_shift_right))
                first = k.firsts[:, ds(8 * b + 4 * h, 4)].unsqueeze(2).to_broadcast([P, 4, 2])
                o(v.tensor_tensor(k.local[h][:, :].rearrange("p (a c) -> p a c", c=2),
                                  dst.rearrange("p (a c) -> p a c", c=2), first, ALU.subtract))
                o.wait()
                o(v.tensor_scalar(k.outside[h][:, :], k.local[h][:, :], 0.0, None, ALU.is_lt))
                o(v.tensor_scalar(k.local[h][:, :], k.local[h][:, :], float(WIN), None, ALU.is_ge))
                o.wait()
                o(v.tensor_tensor(k.outside[h][:, :], k.outside[h][:, :], k.local[h][:, :], ALU.max))
                o.wait()
                o(v.tensor_tensor(k.beyond[h][:, :], k.beyond[h][:, :], k.outside[h][:, :], ALU.mult))
                o(v.tensor_copy(k.digits[h][:, 0:2 * HALF], k.bits[h][:, 0:2 * HALF]))
                o.wait()
                v.sem_inc(s_ix, 1)

            def masks(o, b, h):
                v.wait_ge(s_wg[h], 16 * HALF * (b + 1))
                o(v.tensor_tensor(k.w_act[h][:, :], k.w_row[h][:, :], k.beyond[h][:, :], ALU.mult))
                o.wait()
                for j in range(HALF):
                    n = HALF * h + j
                    v.wait_ge(s_mu, BODY * b + n + 1)
                    i = n % 2
                    v.tensor_scalar(k.mask_lo[i][:, :], k.iota[:, :], k.src_lo[h][:, j:j + 1], None, ALU.is_equal)
                    v.tensor_scalar(k.mask_hi[i][:, 0:NT], k.iota[:, 0:NT], k.src_hi[h][:, j:j + 1],
                                    k.w_act[h][:, j:j + 1], ALU.is_equal, ALU.mult).then_inc(s_m, 1)

            o = Order(v, s_v)
            indices(o, 0, 0)
            with v.Fori(0, n_bodies) as b:
                o = Order(v, s_v, K * b + IX)
                indices(o, b, 1)
                masks(o, b, 0)
                indices(o, b + 1, 0)
                masks(o, b, 1)
                assert o.n == K, (o.n, K)
            wait_apart(k, v, s_mu, n_bodies * BODY + 2)
            v.tensor_scalar(k.firsts[:, :], k.firsts[:, :], HP - WIN, None, ALU.min)


def hyper_degrees(nc, k):
    s_dig = [k.sem(f"deg_digits_loaded{h}") for h in range(2)]
    s_win = [k.sem(f"deg_weights_loaded{h}") for h in range(2)]
    s_w = k.sem("deg_weights_taken")
    s_hi = k.sem("deg_high_masks")
    s_dist = k.sem("deg_low_distances")
    s_lo = k.sem("deg_low_masks")
    s_mu = k.sem("deg_added")
    s_v = k.sem("deg_vector_order")
    s_ld = k.sem("deg_constants_loaded")
    s_cnt = k.sem("deg_counts_in_psum")
    s_pow = k.sem("deg_base")
    s_end = k.sem("deg_end_order")
    s_root = k.sem("deg_root_taken")
    psV = k.psA[:, 0:NT]
    psD = k.psB[:, 0:HT]
    PB, PH = BODY // 2, HALF // 2
    at = [0]

    def take(n):
        at[0] += n
        return k.stage[:, at[0] - n:at[0]]

    lo = [take(HALF * P).rearrange("p (j e) -> p j e", e=P) for _ in range(2)]
    hi = [take(HALF * NT).rearrange("p (j e) -> p j e", e=NT) for _ in range(2)]
    weights = [take(PH * WIN).rearrange("p (q w) -> p q w", w=WIN) for _ in range(2)]
    picked = take(HALF * WIN).rearrange("p (j w) -> p j w", w=WIN)
    columns = take(NT)

    with nc.Block() as block:

        @block.sync
        def _(sp):
            n_bodies = sp.value_load(k.bounds[0:1, 0:1], min_val=1, max_val=BODIES)

            def starts(b, h):
                _, at = nc.values_load_multi_w_load_instructions(
                    k.firsts[0:1, ds(PB * b + PH * h, PH)], engines=[mybir.EngineType.SP], min_val=0, max_val=HP - WIN)
                return at

            def load_weights(b, h):
                for q, first in enumerate(starts(b, h)):
                    sp.dma_start(weights[h][:, q, :], k.w_flat[ds(first, WIN)].partition_broadcast(P))\
                      .then_inc(s_win[h], 16)

            sp.dma_start(k.w_last[:, :], k.w_d[N_HYPER - 1:N_HYPER, :].partition_broadcast(P)
                         .rearrange("p a b -> p (a b)")).then_inc(s_ld, 16)
            sp.dma_start(k.w_pt[:, :], k.w_pt_d).then_inc(s_ld, 16)
            for h in range(2):
                load_weights(0, h)
            with sp.Fori(0, n_bodies) as b:
                for h in range(2):
                    wait_apart(k, sp, s_w, 2 * b + h + 1)
                    load_weights(b + 1, h)
            for h in range(2):
                wait_apart(k, sp, s_win[h], 16 * PH * n_bodies + 16 * PH)

        @block.scalar
        def _(a):
            n_bodies = a.value_load(k.bounds[0:1, 0:1], min_val=1, max_val=BODIES)
            a.sem_inc(s_lo, 1)

            def load_digits(b, h):
                nc.scalar.dma_start(k.digits[h][:, :], k.digit_tab[:, ds(2 * b + h, 1), :]
                                    .rearrange("p o c -> p (o c)")).then_inc(s_dig[h], 16)

            for h in range(2):
                load_digits(0, h)
            with a.Fori(0, n_bodies) as b:
                for h in range(2):
                    a.wait_ge(s_dig[h], 16 * b + 16)
                    a.wait_ge(s_mu, 2 * b + h + 1)
                    for j in range(HALF):
                        last = nc.scalar.activation(lo[h][:, j, :], k.iota[:, :], ACT.Square, scale=-1.0,
                                                    bias=k.digits[h][:, HALF + j:HALF + j + 1])
                    last.then_inc(s_dist, 1)
                    a.wait_ge(s_dist, 2 * b + h + 1)
                    nc.scalar.activation(lo[h], lo[h], ACT.Relu, scale=-1.0, bias=k.ones[:, 0:1]).then_inc(s_lo, 1)
                    wait_apart(k, a, s_hi, 2 * b + h + 1)
                    load_digits(b + 1, h)
            for h in range(2):
                wait_apart(k, a, s_dig[h], 16 * n_bodies + 16)

        @block.gpsimd
        def _(gp):
            gp.wait_ge(s_pow, 1)
            gp.tensor_tensor(k.dvr[:, :], k.dvr[:, :], k.neghalf[:, 0:NT], ALU.pow).then_inc(s_root, 1)

        @block.tensor
        def _(pe):
            n_bodies = pe.value_load(k.bounds[0:1, 0:1], min_val=1, max_val=BODIES)
            pe.sem_inc(s_mu, 2)
            for t in range(HT):
                last = nc.tensor.matmul(psD[:, t:t + 1], k.U[0:1, 2 * UCOLS + t * P:2 * UCOLS + (t + 1) * P],
                                        k.ones[0:1, 0:1], start=True, stop=True)
            last.then_inc(s_cnt, 1)
            with pe.Fori(0, n_bodies) as b:
                for h in range(2):
                    wait_apart(k, pe, s_hi, 2 * b + h + 1)
                    wait_apart(k, pe, s_lo, 2 * b + h + 2)
                    for j in range(HALF):
                        last = nc.tensor.matmul(psV, lo[h][:, j, :], hi[h][:, j, :], start=False, stop=False)
                    last.then_inc(s_mu, 1)
            nc.tensor.matmul(psV, k.zerob[:, :], k.zerob[:, 0:NT], start=False, stop=True).then_inc(s_mu, 1)

        @block.vector
        def _(v):
            n_bodies = v.value_load(k.bounds[0:1, 0:1], min_val=1, max_val=BODIES)
            K = 4
            v.wait_ge(s_ld, 32)
            o = Order(v, s_v)
            o(v.tensor_scalar(columns, k.iota[:, 0:NT], -1.0, -4.0 * P, ALU.mult, ALU.add))
            start = o.n
            with v.Fori(0, n_bodies) as b:
                o = Order(v, s_v, start + K * b)
                for h in range(2):
                    v.wait_ge(s_dig[h], 16 * b + 16)
                    o(v.tensor_tensor(k.oh[h][:, :, :], k.iota[:, 0:WIN].unsqueeze(1).to_broadcast([P, HALF, WIN]),
                                      k.digits[h][:, 0:HALF].unsqueeze(2).to_broadcast([P, HALF, WIN]), ALU.is_equal))
                    o.wait()
                    v.wait_ge(s_win[h], 16 * PH * b + 16 * PH)
                    o(v.tensor_tensor(picked.rearrange("p (q i) w -> p q i w", i=2),
                                      k.oh[h][:, :, :].rearrange("p (q i) w -> p q i w", i=2),
                                      weights[h].unsqueeze(2).to_broadcast([P, PH, 2, WIN]), ALU.mult))
                    o.wait()
                    v.tensor_reduce(k.w_act[h][:, :], picked, AXX, ALU.add).then_inc(s_w, 1)
                    v.wait_ge(s_w, 2 * b + h + 1)
                    v.wait_ge(s_mu, 2 * b + h + 1)
                    for j in range(HALF):
                        last = v.tensor_scalar(hi[h][:, j, :], columns, k.digits[h][:, 2 * HALF + j:2 * HALF + j + 1],
                                               k.w_act[h][:, j:j + 1], ALU.is_equal, ALU.mult)
                    last.then_inc(s_hi, 1)
                assert o.n == K, (o.n, K)
            v.wait_ge(s_cnt, 1)
            wait_apart(k, v, s_mu, 2 * n_bodies + 3)
            v.scalar_tensor_tensor(k.dvr[:, :], k.beyond_count[:, :], k.w_last[:, 0:1], psV, ALU.mult, ALU.add)\
             .then_inc(s_end, 1)
            v.tensor_scalar(k.w_de[:, :], psD, 1.0, None, ALU.max).then_inc(s_end, 1)
            v.wait_ge(s_end, 2)
            v.tensor_scalar(k.dvr[:, :], k.dvr[:, :], 1.0, None, ALU.max).then_inc(s_pow, 1)
            v.reciprocal(k.w_de[:, :], k.w_de[:, :]).then_inc(s_end, 1)
            v.wait_ge(s_end, 3)
            v.tensor_tensor(k.w_de[:, :], k.w_de[:, :], k.w_pt[:, :], ALU.mult)


def node_update(nc, k):
    s_ldu = [k.sem(f"hwu_loaded{h}") for h in range(2)]
    s_ldx = [k.sem(f"xh_loaded{h}") for h in range(2)]
    s_ut = k.sem("sums_copied")
    s_ps = k.sem("update_product")
    s_u = k.sem("update_taken")
    s_var = k.sem("update_variance")
    s_rs = k.sem("update_rstd")
    s_var1 = k.sem("x1_variance")
    s_rs1 = k.sem("x1_rstd")
    s_n = k.sem("update_normalised")
    s_g = k.sem("update_gelu")
    s_x1 = k.sem("x1_ready")
    s_xp = k.sem("xp_ready")
    s_st1 = [k.sem(f"x1_stored{h}") for h in range(2)]
    s_stp = [k.sem(f"xp_stored{h}") for h in range(2)]
    s_v = k.sem("update_vector_order")
    W = NG * D
    LAST = NGROUPS // 2

    def grp(i):
        return k.stage[:, i * W:(i + 1) * W].rearrange("p (t d) -> p t d", d=D)

    u, xh, xp = [grp(0), grp(1)], [grp(2), grp(3)], [grp(4), grp(5)]
    U3 = k.U[:, :].rearrange("p (c n) -> p c n", c=3)
    ps = [t[:, 0:W].rearrange("p (t d) -> p t d", d=D) for t in k.psH]
    view = {n: t.rearrange("(g t p) d -> g p t d", p=P, t=NG)
            for n, t in (("hwu", k.hwu_tab), ("xh", k.xh_tab), ("x1", k.x1_tab), ("xp", k.xp_tab))}

    def rows(n, g):
        return view[n][ds(g, 1)].rearrange("o p t d -> (o p) t d")

    with nc.Block() as block:

        @block.sync
        def _(sp):
            def turn(b, h, more):
                g = 2 * b + h
                wait_apart(k, sp, s_x1, g + 1)
                if more:
                    sp.dma_start(u[h], rows("hwu", g + 2)).then_inc(s_ldu[h], 16)
                sp.dma_start(rows("x1", g), xh[h]).then_inc(s_st1[h], 16)
                wait_apart(k, sp, s_xp, g + 1)
                sp.dma_start(rows("xp", g), xp[h]).then_inc(s_stp[h], 16)
                if more:
                    wait_apart(k, sp, s_st1[h], 16 * b + 16)
                    sp.dma_start(xh[h], rows("xh", g + 2)).then_inc(s_ldx[h], 16)

            for h in range(2):
                sp.dma_start(u[h], rows("hwu", h)).then_inc(s_ldu[h], 16)
                sp.dma_start(xh[h], rows("xh", h)).then_inc(s_ldx[h], 16)
                sp.sem_inc(s_stp[h], 16)
            with sp.Fori(0, LAST - 1) as b:
                for h in range(2):
                    turn(b, h, True)
            for h in range(2):
                turn(LAST - 1, h, False)
            for h in range(2):
                sp.wait_ge(s_st1[h], 16 * LAST)
                sp.wait_ge(s_stp[h], 16 * LAST + 16)

        @block.scalar
        def _(a):
            def copy(g, t, i):
                n = NG * g + t
                a.wait_ge(s_ps, n + 1)
                a.copy(k.ut[i][:, :, :], U3[:, :, ds(n * P, P)]).then_inc(s_ut, 1)

            def turn(b, h, more):
                g = 2 * b + h
                for t in range(NG + 1):
                    if t == NG // 2 + 1:
                        a.wait_ge(s_n, g + 1)
                        nc.scalar.activation(u[h], u[h], ACT.Gelu).then_inc(s_g, 1)
                    if more and t < NG:
                        copy(g + 1, t, (NG * (h + 1) + t) % 2)

            for t in range(NG):
                copy(0, t, t % 2)
            with a.Fori(0, LAST - 1) as b:
                for h in range(2):
                    turn(b, h, True)
            for h in range(2):
                turn(LAST - 1, h, h == 0)

        @block.tensor
        def _(pe):
            pe.sem_inc(s_ps, 2)
            with pe.Fori(0, LAST) as b:
                for h in range(2):
                    wait_apart(k, pe, s_u, 2 * b + h + 1)
                    for t in range(NG):
                        n = 2 * NG * b + NG * h + t
                        i = (NG * h + t) % 2
                        wait_apart(k, pe, s_ut, n + 1)
                        nc.tensor.matmul(ps[h][:, t, :], k.ut[i][:, 0, :], k.w2u[:, 0:D], start=True, stop=False)
                        nc.tensor.matmul(ps[h][:, t, :], k.ut[i][:, 1, :], k.w2u[:, D:2 * D], start=False, stop=False)
                        nc.tensor.matmul(ps[h][:, t, :], k.ut[i][0:1, 2, :], k.b2u[0:1, :], start=False,
                                         stop=True).then_inc(s_ps, 1)

        @block.gpsimd
        def _(gp):
            def first_root(g, h):
                gp.wait_ge(s_var, g + 1)
                gp.tensor_tensor(k.nrs[h][:, 0:NG], k.nvar[h][:, 0:NG], k.neghalf[:, 0:NG], ALU.pow).then_inc(s_rs, 1)

            def residual(b, h):
                g = 2 * b + h
                wait_apart(k, gp, s_ldx[h], 16 * b + 16)
                gp.wait_ge(s_g, g + 1)
                gp.tensor_tensor(xh[h], xh[h], u[h], ALU.add).then_inc(s_x1, 1)

            def second_root(g, h):
                gp.wait_ge(s_var1, g + 1)
                gp.tensor_tensor(k.nrs[h][:, NG:2 * NG], k.nvar[h][:, NG:2 * NG], k.neghalf[:, 0:NG],
                                 ALU.pow).then_inc(s_rs1, 1)

            first_root(0, 0)
            residual(0, 0)
            with gp.Fori(0, LAST - 1) as b:
                first_root(2 * b + 1, 1)
                second_root(2 * b, 0)
                residual(b, 1)
                first_root(2 * b + 2, 0)
                second_root(2 * b + 1, 1)
                residual(b + 1, 0)
            first_root(2 * LAST - 1, 1)
            second_root(2 * LAST - 2, 0)
            residual(LAST - 1, 1)
            second_root(2 * LAST - 1, 1)

        @block.vector
        def _(v):
            K = 6 * NG + 2
            v.sem_inc(s_u, 2)

            def stats(o, x, h, part, done):
                first = o.n
                for t in range(NG):
                    o(v.bn_stats(k.nst[h][:, t, :], x[:, t, :]))
                for t in range(NG):
                    wait_apart(k, v, s_v, o.base + first + t + 1)
                    o(v.bn_aggr(k.nmv[h][:, NG * part + t, :], k.nst[h][:, t, :]))
                o.wait()
                v.tensor_scalar(k.nvar[h][:, NG * part:NG * part + NG], k.nmv[h][:, NG * part:NG * part + NG, 1],
                                EPS, None, ALU.add).then_inc(done, 1)

            def update_rows(o, b, h):
                g = 2 * b + h
                v.wait_ge(s_ldu[h], 16 * b + 16)
                v.wait_ge(s_ps, NG * (g + 1) + 2)
                v.tensor_tensor(u[h], ps[h], u[h], ALU.add).then_inc(s_u, 1)
                v.wait_ge(s_u, g + 3)
                stats(o, u[h], h, 0, s_var)

            def normalise(o, b, h):
                g = 2 * b + h
                v.wait_ge(s_rs, g + 1)
                for t in range(NG):
                    o(v.tensor_scalar(u[h][:, t, :], u[h][:, t, :], k.nmv[h][:, t, 0:1], k.nrs[h][:, t:t + 1],
                                      ALU.subtract, ALU.mult))
                o.wait()
                o(v.tensor_tensor(u[h], u[h], k.gu[:, :].unsqueeze(1).to_broadcast([P, NG, D]), ALU.mult))
                o.wait()
                v.tensor_tensor(u[h], u[h], k.beu[:, :].unsqueeze(1).to_broadcast([P, NG, D]), ALU.add).then_inc(s_n, 1)

            def x1_stats(o, b, h):
                v.wait_ge(s_x1, 2 * b + h + 1)
                stats(o, xh[h], h, 1, s_var1)

            def hyper_input(o, b, h):
                g = 2 * b + h
                v.wait_ge(s_rs1, g + 1)
                o(v.tensor_tensor(k.nrs[h][:, NG:2 * NG], k.nrs[h][:, NG:2 * NG], k.dvr[:, ds(NG * g, NG)], ALU.mult))
                o.wait()
                v.wait_ge(s_stp[h], 16 * b + 16)
                for t in range(NG):
                    o(v.tensor_scalar(xp[h][:, t, :], xh[h][:, t, :], k.nmv[h][:, NG + t, 0:1],
                                      k.nrs[h][:, NG + t:NG + t + 1], ALU.subtract, ALU.mult))
                o.wait()
                v.tensor_scalar(xp[h], xp[h], 0.0, None, ALU.max).then_inc(s_xp, 1)

            def turn(o, b, h, follow):
                pb, p = (b, 0) if h else (b - 1, 1)
                update_rows(o, b, h)
                if follow:
                    x1_stats(o, pb, p)
                normalise(o, b, h)
                if follow:
                    hyper_input(o, pb, p)

            o = Order(v, s_v)
            turn(o, 0, 0, False)
            turn(o, 0, 1, True)
            start = o.n
            with v.Fori(1, LAST) as b:
                o = Order(v, s_v, start + 2 * K * (b - 1))
                for h in range(2):
                    turn(o, b, h, True)
                assert o.n == 2 * K, (o.n, 2 * K)
            o = Order(v, s_v, start + 2 * K * (LAST - 1))
            x1_stats(o, LAST - 1, 1)
            hyper_input(o, LAST - 1, 1)


def hyperedge_sums(nc, k):
    s_meta = [k.sem(f"he_indices_loaded{h}") for h in range(2)]
    s_g = [k.sem(f"he_rows_gathered{j}") for j in range(HALF)]
    s_loc = k.sem("he_indices_taken")
    s_oh = k.sem("he_window_masks")
    s_seg = k.sem("he_windows_summed")
    s_u = k.sem("he_windows_kept")
    s_z = k.sem("he_sums_zeroed")
    heT = k.U[:, 0:UCOLS]
    rows = k.stage[:, 0:HALF * D].rearrange("p (j d) -> p j d", d=D)
    psU = [k.psA[:, 0:WIN], k.psC[:, 0:WIN]]

    with nc.Block() as block:

        @block.sync
        def _(sp):
            n_bodies = sp.value_load(k.bounds[0:1, 0:1], min_val=1, max_val=BODIES)

            def load_meta(b, h):
                sp.dma_start(k.meta[h][:, :], k.meta_d[ds(2 * b + h, 1)].rearrange("o p c -> (o p) c"))\
                  .then_inc(s_meta[h], 16)

            for h in range(2):
                load_meta(0, h)
            with sp.Fori(0, n_bodies) as b:
                for h in range(2):
                    sp.wait_ge(s_seg, 8 * b + 4 * h + 8)
                    load_meta(b + 1, h)
            for h in range(2):
                wait_apart(k, sp, s_meta[h], 16 * n_bodies + 16)

        @block.gpsimd
        def _(gp):
            n_bodies = gp.value_load(k.bounds[0:1, 0:1], min_val=1, max_val=BODIES)
            gp.memset(heT[:, 0:FAR_HCHUNKS * FAR_COLS], 0.0).then_inc(s_z, 1)
            gp.sem_inc(s_seg, 4)
            with gp.Fori(0, n_bodies) as b:
                for h in range(2):
                    wait_apart(k, gp, s_meta[h], 16 * b + 16)
                    for j in range(HALF):
                        if j % 2 == 0:
                            wait_apart(k, gp, s_seg, 8 * b + 4 * h + j // 2 + 1)
                        gp.indirect_dma_start(out=rows[:, j, :], out_offset=None, in_=k.xp_tab[:, :],
                                              in_offset=bass.IndirectOffsetOnAxis(ap=k.meta[h][:, j:j + 1], axis=0))\
                          .then_inc(s_g[j], 16)

        @block.tensor
        def _(pe):
            n_bodies = pe.value_load(k.bounds[0:1, 0:1], min_val=1, max_val=BODIES)
            pe.sem_inc(s_u, 2)
            with pe.Fori(0, n_bodies) as b:
                for h in range(2):
                    pe.wait_ge(s_oh, 2 * b + h + 1)
                    for q in range(HALF // 2):
                        pe.wait_ge(s_u, 8 * b + 4 * h + q + 1)
                        for i in range(2):
                            j = 2 * q + i
                            pe.wait_ge(s_g[j], 16 * (2 * b + h) + 16)
                            last = nc.tensor.matmul(psU[q % 2], rows[:, j, :], k.oh[h][:, j, :],
                                                    start=i == 0, stop=i == 1)
                        last.then_inc(s_seg, 1)

        @block.vector
        def _(v):
            n_bodies = v.value_load(k.bounds[0:1, 0:1], min_val=1, max_val=BODIES)
            v.wait_ge(s_z, 1)
            with v.Fori(0, n_bodies) as b:
                for h in range(2):
                    v.wait_ge(s_meta[h], 16 * b + 16)
                    dst = k.meta[h][:, HALF:2 * HALF]
                    first = k.firsts[:, ds(8 * b + 4 * h, 4)].unsqueeze(2).to_broadcast([P, 4, 2])
                    v.tensor_tensor(k.local[h][:, :].rearrange("p (a c) -> p a c", c=2),
                                    dst.rearrange("p (a c) -> p a c", c=2), first, ALU.subtract).then_inc(s_loc, 1)
                    v.wait_ge(s_loc, 2 * b + h + 1)
                    v.tensor_tensor(k.oh[h][:, :, :], k.iota[:, 0:WIN].unsqueeze(1).to_broadcast([P, HALF, WIN]),
                                    k.local[h][:, :].unsqueeze(2).to_broadcast([P, HALF, WIN]),
                                    ALU.is_equal).then_inc(s_oh, 1)
                    for q in range(HALF // 2):
                        w = 8 * b + 4 * h + q
                        first = v.value_load(k.firsts[0:1, ds(w, 1)], min_val=0, max_val=N_NODES)
                        v.wait_ge(s_seg, w + 1 + 4)
                        v.wait_ge(s_u, w + 2)
                        v.tensor_tensor(heT[:, ds(first, WIN)], heT[:, ds(first, WIN)], psU[q % 2],
                                        ALU.add).then_inc(s_u, 1)
            wait_apart(k, v, s_u, 8 * n_bodies + 2)


def hyperedge_rows(nc, k):
    s_gp = k.sem("he_product")
    s_gr = k.sem("he_rows_ready")
    s_st = k.sem("he_rows_stored")
    heT = k.U[:, 0:UCOLS]
    g_rows = k.stage[:, 0:HT * D].rearrange("p (t d) -> p t d", d=D)
    psG = [k.psA, k.psB]

    with nc.Block() as block:

        @block.sync
        def _(sp):
            sp.wait_ge(s_gr, HT)
            sp.dma_start(k.g_tab.rearrange("(t p) d -> p t d", p=P), g_rows).then_inc(s_st, 16)
            sp.wait_ge(s_st, 16)

        @block.tensor
        def _(pe):
            for t in range(HT):
                if t >= 2:
                    pe.wait_ge(s_gr, t - 1)
                nc.tensor.matmul(psG[t % 2][:, 0:D], heT[:, t * P:(t + 1) * P], k.lw[:, :], start=True,
                                 stop=True).then_inc(s_gp, 1)

        @block.vector
        def _(v):
            for t in range(HT):
                v.wait_ge(s_gp, t + 1)
                v.tensor_scalar(g_rows[:, t, :], psG[t % 2][:, 0:D], k.w_de[:, t:t + 1], None,
                                ALU.mult).then_inc(s_gr, 1)


def scatter_rows(nc, k):
    s_meta = [k.sem(f"sc_indices_loaded{h}") for h in range(2)]
    s_row = [k.sem(f"sc_sources_loaded{h}") for h in range(2)]
    s_win = [k.sem(f"sc_windows_loaded{h}") for h in range(2)]
    s_same = k.sem("sc_masks_ready")
    s_mix = k.sem("sc_masks_multiplied")
    s_mc = k.sem("sc_masks_copied")
    s_ps = k.sem("sc_tile_summed")
    s_c = k.sem("sc_rows_copied")
    s_to = k.sem("sc_targets_ready")
    s_sc = [k.sem(f"sc_scattered{r}") for r in range(SCATTER_TABLES)]
    s_v = k.sem("sc_vector_order")
    s_sz = k.sem("sc_zeros")
    s_free = k.sem("sc_targets_used")
    R = SCATTER_TABLES
    PB, PH = BODY // 2, HALF // 2
    summed = k.stage[:, 0:R * D].rearrange("p (j d) -> p j d", d=D)
    at = [0]

    def take(n):
        at[0] += n
        return k.U[:, at[0] - n:at[0]]

    src_row = [take(HALF * P).bitcast(I32).rearrange("p (j e) -> p j e", e=P) for _ in range(2)]
    same = take(HALF * P).rearrange("p (j e) -> p j e", e=P)
    waste = take(HALF * P).rearrange("p (j e) -> p j e", e=P)
    window = [take(PH * D)[0:WIN, :].rearrange("p (q d) -> p q d", d=D) for _ in range(2)]
    mixed = [take(2 * P)[0:WIN, :].rearrange("p (i e) -> p i e", i=2) for _ in range(2)]
    earlier = take(2 * HALF).rearrange("p (i j) -> p i j", i=2)
    away = take(2 * HALF).rearrange("p (i j) -> p i j", i=2)
    psM = [t[0:WIN, 0:2 * P].rearrange("p (i e) -> p i e", i=2) for t in (k.psC, k.psH[0])]
    ps = [k.psA, k.psB]

    with nc.Block() as block:

        @block.sync
        def _(sp):
            n_bodies = sp.value_load(k.bounds[0:1, 0:1], min_val=1, max_val=BODIES)

            def load(b, h):
                sp.dma_start(k.meta[h][:, :], k.meta_d[ds(2 * b + h, 1)].rearrange("o p c -> (o p) c"))\
                  .then_inc(s_meta[h], 16)
                sp.dma_start(k.digits[h][:, :], k.digit_tab[:, ds(2 * b + h, 1), :]
                             .rearrange("p o c -> p (o c)")).then_inc(s_meta[h], 16)
                sp.dma_start(src_row[h], k.src_d[ds(2 * b + h, 1)].rearrange("o j e -> (o j) e")
                             .partition_broadcast(P)).then_inc(s_row[h], 16)

            def load_windows(b, h):
                _, at = nc.values_load_multi_w_load_instructions(
                    k.firsts[0:1, ds(PB * b + PH * h, PH)], engines=[mybir.EngineType.SP], min_val=0, max_val=HP - WIN)
                for q, first in enumerate(at):
                    sp.dma_start(window[h][:, q, :], k.g_tab[ds(first, WIN), :]).then_inc(s_win[h], 16)

            for h in range(2):
                load(0, h)
                load_windows(0, h)
            with sp.Fori(0, n_bodies) as b:
                for h in range(2):
                    wait_apart(k, sp, s_to, 2 * b + h + 1)
                    load(b + 1, h)
                    wait_apart(k, sp, s_ps, BODY * b + HALF * (h + 1) + 4)
                    load_windows(b + 1, h)
            for h in range(2):
                wait_apart(k, sp, s_meta[h], 32 * n_bodies + 32)
                wait_apart(k, sp, s_row[h], 16 * n_bodies + 16)
                wait_apart(k, sp, s_win[h], 16 * PH * n_bodies + 16 * PH)

        @block.gpsimd
        def _(gp):
            n_bodies = gp.value_load(k.bounds[0:1, 0:1], min_val=1, max_val=BODIES)
            gp.sem_inc(s_free, 1)
            gp.memset(summed, 0.0).then_inc(s_sz, 1)
            gp.wait_ge(s_sz, 1)
            for r in range(R):
                gp.dma_start(k.acc[r][NP:NP + P, :], summed[:, r, :]).then_inc(s_sc[r], 16)

            with gp.Fori(0, n_bodies) as b:
                for n in range(BODY):
                    h, j = divmod(n, HALF)
                    r = j % R
                    if j == 0:
                        wait_apart(k, gp, s_to, 2 * b + h + 1)
                    wait_apart(k, gp, s_c, BODY * b + n + 3)
                    wait_apart(k, gp, s_sc[r], 16 * (BODY // R * b + n // R) + 16)
                    gp.indirect_dma_start(out=k.acc[r], out_offset=bass.IndirectOffsetOnAxis(
                        ap=k.target[h][:, j:j + 1], axis=0), in_=summed[:, r, :], in_offset=None,
                        compute_op=ALU.add).then_inc(s_sc[r], 16)
                    if j == R - 1:
                        gp.sem_inc(s_free, 1)
            for r in range(R):
                wait_apart(k, gp, s_sc[r], 16 * (BODY // R) * n_bodies + 16)

        @block.tensor
        def _(pe):
            n_bodies = pe.value_load(k.bounds[0:1, 0:1], min_val=1, max_val=BODIES)
            pe.sem_inc(s_ps, 4)
            pe.sem_inc(s_mix, 4)

            def mix(b, m):
                h, q = divmod(m, PH)
                if q == 0:
                    pe.wait_ge(s_same, 2 * b + h + 1)
                pe.wait_ge(s_mc, PB * b + m + 1)
                for i in range(2):
                    last = nc.tensor.matmul(psM[m % 2][:, i, :], k.oh[h][:, 2 * q + i, :], same[:, 2 * q + i, :],
                                            start=True, stop=True)
                last.then_inc(s_mix, 1)

            def rows(b, m):
                h, q = divmod(m, PH)
                pe.wait_ge(s_mc, PB * b + m + 3)
                if q == 0:
                    wait_apart(k, pe, s_win[h], 16 * PH * (b + 1))
                for i in range(2):
                    pe.wait_ge(s_c, BODY * b + 2 * m + i + 1)
                    nc.tensor.matmul(ps[i][:, 0:D], mixed[m % 2][:, i, :], window[h][:, q, :], start=True,
                                     stop=True).then_inc(s_ps, 1)

            with pe.Fori(0, n_bodies) as b:
                mix(b, 0)
                for m in range(PB):
                    if m + 1 < PB:
                        mix(b, m + 1)
                    rows(b, m)

        @block.scalar
        def _(a):
            n_bodies = a.value_load(k.bounds[0:1, 0:1], min_val=1, max_val=BODIES)
            a.sem_inc(s_mc, 2)
            a.sem_inc(s_c, 2)

            def take_masks(b, m):
                a.wait_ge(s_mix, PB * b + m + 5)
                a.wait_ge(s_ps, BODY * b + 2 * m + 2)
                a.copy(mixed[m % 2], psM[m % 2]).then_inc(s_mc, 1)

            def take_rows(b, n):
                r = n % R
                a.wait_ge(s_ps, BODY * b + n + 5)
                a.wait_ge(s_sc[r], 16 * (BODY // R * b + n // R) + 16)
                a.copy(summed[:, r, :], ps[n % 2][:, 0:D]).then_inc(s_c, 1)

            with a.Fori(0, n_bodies) as b:
                take_masks(b, 0)
                for m in range(PB):
                    if m + 1 < PB:
                        take_masks(b, m + 1)
                    for i in range(2):
                        take_rows(b, 2 * m + i)

        @block.vector
        def _(v):
            n_bodies = v.value_load(k.bounds[0:1, 0:1], min_val=1, max_val=BODIES)
            K = 2 * (2 * HALF + 4)
            with v.Fori(0, n_bodies) as b:
                o = Order(v, s_v, K * b)
                for h in range(2):
                    v.wait_ge(s_meta[h], 32 * b + 32)
                    src = k.meta[h][:, 0:HALF]
                    v.wait_ge(s_row[h], 16 * b + 16)
                    v.wait_ge(s_mix, PB * b + PH * h + 4)
                    o(v.tensor_tensor(k.oh[h][:, :, :], k.iota[:, 0:WIN].unsqueeze(1).to_broadcast([P, HALF, WIN]),
                                      k.digits[h][:, 0:HALF].unsqueeze(2).to_broadcast([P, HALF, WIN]), ALU.is_equal))
                    for j in range(HALF):
                        o(v.tensor_scalar(same[:, j, :], src_row[h][:, j, :], src[:, j:j + 1], None, ALU.is_equal))
                    o.wait()
                    v.sem_inc(s_same, 1)
                    for j in range(HALF):
                        o(v.tensor_tensor_reduce(waste[:, j, :], same[:, j, :], k.before[:, :], 1.0, 0.0, ALU.mult,
                                                 ALU.add, earlier[:, h, j:j + 1]))
                    o.wait()
                    o(v.tensor_scalar(earlier[:, h, :], earlier[:, h, :], 1.0, None, ALU.min))
                    o(v.tensor_scalar(away[:, h, :], src, -1.0, k.junk[:, 0:1], ALU.mult, ALU.add))
                    o.wait()
                    o(v.tensor_tensor(away[:, h, :], away[:, h, :], earlier[:, h, :], ALU.mult))
                    o.wait()
                    v.wait_ge(s_free, 2 * b + h + 1)
                    v.tensor_tensor(k.target[h][:, :], away[:, h, :], src, ALU.add).then_inc(s_to, 1)
                assert o.n == K, (o.n, K)


def far_scatter(nc, k):
    s_meta = [k.sem(f"far_indices_loaded{h}") for h in range(2)]
    s_row = [k.sem(f"far_sources_loaded{h}") for h in range(2)]
    s_ix = k.sem("far_indices_ready")
    s_g = [k.sem(f"far_rows_gathered{j}") for j in range(HALF)]
    s_same = k.sem("far_same_source")
    s_ps = k.sem("far_tile_summed")
    s_c = k.sem("far_rows_copied")
    s_to = k.sem("far_targets_ready")
    s_sc = [k.sem(f"far_scattered{r}") for r in range(SCATTER_TABLES)]
    s_v = k.sem("far_vector_order")
    s_sz = k.sem("far_zeros")
    rows = k.stage[:, 0:HALF * D].rearrange("p (j d) -> p j d", d=D)
    at = HALF * D
    summed = k.stage[:, at:at + SCATTER_TABLES * D].rearrange("p (j d) -> p j d", d=D)
    src_row = [k.U[:, i * HALF * P:(i + 1) * HALF * P].bitcast(I32).rearrange("p (j e) -> p j e", e=P)
               for i in range(2)]
    same = k.U[:, 2 * HALF * P:3 * HALF * P].rearrange("p (j e) -> p j e", e=P)
    waste = k.U[:, 3 * HALF * P:4 * HALF * P].rearrange("p (j e) -> p j e", e=P)
    at = 4 * HALF * P
    earlier = k.U[:, at:at + 2 * HALF].rearrange("p (i j) -> p i j", i=2)
    away = k.U[:, at + 2 * HALF:at + 4 * HALF].rearrange("p (i j) -> p i j", i=2)
    ps = [k.psA, k.psB]
    R = SCATTER_TABLES

    with nc.Block() as block:

        @block.sync
        def _(sp):
            n_bodies = sp.value_load(k.bounds[0:1, 4:5], min_val=1, max_val=BODIES)

            def load(b, h):
                sp.dma_start(k.meta[h][:, :], k.meta_d[ds(2 * b + h, 1)].rearrange("o p c -> (o p) c"))\
                  .then_inc(s_meta[h], 16)
                sp.dma_start(k.digits[h][:, :], k.digit_tab[:, ds(2 * b + h, 1), :]
                             .rearrange("p o c -> p (o c)")).then_inc(s_meta[h], 16)
                sp.dma_start(src_row[h], k.src_d[ds(2 * b + h, 1)].rearrange("o j e -> (o j) e")
                             .partition_broadcast(P)).then_inc(s_row[h], 16)

            for h in range(2):
                load(0, h)
            with sp.Fori(0, n_bodies) as b:
                for h in range(2):
                    sp.wait_ge(s_to, 2 * b + h + 1)
                    load(b + 1, h)
            for h in range(2):
                wait_apart(k, sp, s_meta[h], 32 * n_bodies + 32)
                wait_apart(k, sp, s_row[h], 16 * n_bodies + 16)

        @block.gpsimd
        def _(gp):
            n_bodies = gp.value_load(k.bounds[0:1, 4:5], min_val=1, max_val=BODIES)
            gp.sem_inc(s_ps, HALF)
            gp.memset(summed, 0.0).then_inc(s_sz, 1)
            gp.wait_ge(s_sz, 1)
            for r in range(R):
                gp.dma_start(k.acc[r][NP:NP + P, :], summed[:, r, :]).then_inc(s_sc[r], 16)

            with gp.Fori(0, n_bodies) as b:
                for h in range(2):
                    wait_apart(k, gp, s_ix, 2 * b + h + 1)
                    for j in range(HALF):
                        n = HALF * h + j
                        wait_apart(k, gp, s_ps, BODY * b + n + 1)
                        gp.indirect_dma_start(out=rows[:, j, :], out_offset=None, in_=k.g_tab[:, :],
                                              in_offset=bass.IndirectOffsetOnAxis(ap=k.gidx[h][:, j:j + 1], axis=0))\
                          .then_inc(s_g[j], 16)
                    wait_apart(k, gp, s_to, 2 * b + h + 1)
                    for j in range(HALF):
                        n = HALF * h + j
                        r = j % R
                        wait_apart(k, gp, s_c, BODY * b + n + 3)
                        wait_apart(k, gp, s_sc[r], 16 * (BODY // R * b + n // R) + 16)
                        gp.indirect_dma_start(out=k.acc[r], out_offset=bass.IndirectOffsetOnAxis(
                            ap=k.target[h][:, j:j + 1], axis=0), in_=summed[:, r, :], in_offset=None,
                            compute_op=ALU.add).then_inc(s_sc[r], 16)
            for r in range(R):
                wait_apart(k, gp, s_sc[r], 16 * (BODY // R) * n_bodies + 16)

        @block.tensor
        def _(pe):
            n_bodies = pe.value_load(k.bounds[0:1, 4:5], min_val=1, max_val=BODIES)
            pe.sem_inc(s_c, 2)
            with pe.Fori(0, n_bodies) as b:
                for n in range(BODY):
                    j = n % HALF
                    h = n // HALF
                    if j == 0:
                        pe.wait_ge(s_same, 2 * b + h + 1)
                    pe.wait_ge(s_g[j], 16 * (2 * b + h) + 16)
                    pe.wait_ge(s_c, BODY * b + n + 1)
                    nc.tensor.matmul(ps[n % 2][:, 0:D], same[:, j, :], rows[:, j, :], start=True,
                                     stop=True).then_inc(s_ps, 1)

        @block.scalar
        def _(a):
            n_bodies = a.value_load(k.bounds[0:1, 4:5], min_val=1, max_val=BODIES)
            with a.Fori(0, n_bodies) as b:
                for n in range(BODY):
                    r = n % R
                    a.wait_ge(s_ps, BODY * b + n + 1 + HALF)
                    a.wait_ge(s_sc[r], 16 * (BODY // R * b + n // R) + 16)
                    a.copy(summed[:, r, :], ps[n % 2][:, 0:D]).then_inc(s_c, 1)

        @block.vector
        def _(v):
            n_bodies = v.value_load(k.bounds[0:1, 4:5], min_val=1, max_val=BODIES)
            K = 2 * (6 + 2 * HALF + 3)
            with v.Fori(0, n_bodies) as b:
                o = Order(v, s_v, K * b)
                for h in range(2):
                    v.wait_ge(s_meta[h], 32 * b + 32)
                    src, dst = k.meta[h][:, 0:HALF], k.meta[h][:, HALF:2 * HALF]
                    o(v.tensor_scalar(k.beyond[h][:, :], dst, float(N_HYPER), None, ALU.is_lt))
                    o(v.tensor_scalar(k.gidx[h][:, :], dst, float(N_HYPER - 1), None, ALU.min))
                    o(v.tensor_scalar(k.w_row[h][:, :], k.digits[h][:, 0:HALF], 0.0, None, ALU.is_lt))
                    o(v.tensor_scalar(k.w_act[h][:, :], k.digits[h][:, 0:HALF], float(WIN), None, ALU.is_ge))
                    o.wait()
                    v.sem_inc(s_ix, 1)
                    o(v.tensor_tensor(k.w_row[h][:, :], k.w_row[h][:, :], k.w_act[h][:, :], ALU.max))
                    o.wait()
                    o(v.tensor_tensor(k.beyond[h][:, :], k.beyond[h][:, :], k.w_row[h][:, :], ALU.mult))
                    v.wait_ge(s_row[h], 16 * b + 16)
                    v.wait_ge(s_ps, BODY * b + HALF * h + HALF)
                    for j in range(HALF):
                        o(v.tensor_scalar(same[:, j, :], src_row[h][:, j, :], src[:, j:j + 1], None, ALU.is_equal))
                    for j in range(HALF):
                        o.wait(o.base + o.n - HALF + 1)
                        o(v.tensor_tensor_reduce(waste[:, j, :], same[:, j, :], k.before[:, :], 1.0, 0.0, ALU.mult,
                                                 ALU.add, earlier[:, h, j:j + 1]))
                    o.wait()
                    v.tensor_tensor(same[:, :, :], same[:, :, :],
                                    k.beyond[h][:, :].unsqueeze(2).to_broadcast([P, HALF, P]),
                                    ALU.mult).then_inc(s_same, 1)
                    o(v.tensor_scalar(earlier[:, h, :], earlier[:, h, :], 1.0, None, ALU.min))
                    o(v.tensor_scalar(away[:, h, :], src, -1.0, k.junk[:, 0:1], ALU.mult, ALU.add))
                    o.wait()
                    o(v.tensor_tensor(away[:, h, :], away[:, h, :], earlier[:, h, :], ALU.mult))
                    o.wait()
                    v.tensor_tensor(k.target[h][:, :], away[:, h, :], src, ALU.add).then_inc(s_to, 1)
                assert o.n == K, (o.n, K)


def output_rows(nc, k):
    s_ld = [k.sem(f"out_loaded{h}") for h in range(2)]
    s_c = k.sem("out_constants")
    s_v = k.sem("out_vector_order")
    s_s = k.sem("out_summed")
    s_o = k.sem("out_ready")
    s_st = [k.sem(f"out_stored{h}") for h in range(2)]
    R = SCATTER_TABLES
    W = NG * D

    def grp(i):
        return k.U[:, i * W:(i + 1) * W].rearrange("p (t d) -> p t d", d=D)

    x1 = [grp(0), grp(1)]
    acc = [[grp(2 + R * h + r) for r in range(R)] for h in range(2)]
    g_last = k.U[:, (2 + 2 * R) * W:(2 + 2 * R) * W + D]
    x1_v = k.x1_tab.rearrange("(g t p) d -> g p t d", p=P, t=NG)
    acc_v = [k.acc[r][0:NP, :].rearrange("(g t p) d -> g p t d", p=P, t=NG) for r in range(R)]

    with nc.Block() as block:

        @block.sync
        def _(sp):
            sp.dma_start(g_last, k.g_tab[N_HYPER - 1:N_HYPER, :].partition_broadcast(P)
                         .rearrange("p a d -> p (a d)")).then_inc(s_c, 16)

            def load(g, h):
                sp.dma_start(x1[h], x1_v[ds(g, 1)].rearrange("o p t d -> (o p) t d")).then_inc(s_ld[h], 16)
                for r in range(R):
                    sp.dma_start(acc[h][r], acc_v[r][ds(g, 1)].rearrange("o p t d -> (o p) t d")).then_inc(s_ld[h], 16)

            def store(g, h):
                sp.wait_ge(s_o, g + 1)
                sp.dma_start(k.out[ds(g * NG * P, NG * P), :].rearrange("(t p) d -> p t d", p=P),
                             x1[h]).then_inc(s_st[h], 16)

            for h in range(2):
                load(h, h)
            with sp.Fori(0, NGROUPS // 2 - 1) as b:
                for h in range(2):
                    store(2 * b + h, h)
                    sp.wait_ge(s_st[h], 16 * b + 16)
                    load(2 * b + 2 + h, h)
            store(NGROUPS - 2, 0)
            g = NGROUPS - 1
            whole = (N_NODES - g * NG * P) // P
            rest = N_NODES - g * NG * P - whole * P
            sp.wait_ge(s_o, g + 1)
            sp.dma_start(k.out[g * NG * P:g * NG * P + whole * P, :].rearrange("(t p) d -> p t d", p=P),
                         x1[1][:, 0:whole, :]).then_inc(s_st[1], 16)
            sp.dma_start(k.out[N_NODES - rest:N_NODES, :], x1[1][0:rest, whole, :]).then_inc(s_st[1], 16)
            sp.wait_ge(s_st[0], 16 * (NGROUPS // 2))
            sp.wait_ge(s_st[1], 16 * (NGROUPS // 2) + 16)

        @block.gpsimd
        def _(gp):
            with gp.Fori(0, NGROUPS // 2) as b:
                for h in range(2):
                    gp.wait_ge(s_ld[h], 16 * (1 + R) * (b + 1))
                    gp.tensor_tensor(x1[h], x1[h], k.lb[:, :].unsqueeze(1).to_broadcast([P, NG, D]),
                                     ALU.add).then_inc(s_s, 1)

        @block.vector
        def _(v):
            K = 2 * (R - 1 + NG)
            v.wait_ge(s_c, 16)
            with v.Fori(0, NGROUPS // 2) as b:
                o = Order(v, s_v, K * b)
                for h in range(2):
                    g = 2 * b + h
                    v.wait_ge(s_ld[h], 16 * (1 + R) * (b + 1))
                    for r in range(1, R):
                        o(v.tensor_tensor(acc[h][0], acc[h][0], acc[h][r], ALU.add))
                        o.wait()
                    for t in range(NG):
                        o(v.scalar_tensor_tensor(acc[h][0][:, t, :], g_last, k.beyond_count[:, ds(NG * g + t, 1)],
                                                 acc[h][0][:, t, :], ALU.mult, ALU.add))
                    v.wait_ge(s_s, g + 1)
                    o.wait()
                    for t in range(NG):
                        last = v.scalar_tensor_tensor(x1[h][:, t, :], acc[h][0][:, t, :], k.dvr[:, ds(NG * g + t, 1)],
                                                      x1[h][:, t, :], ALU.mult, ALU.add)
                    last.then_inc(s_o, 1)
                assert o.n == K, (o.n, K)




PHASES = (setup_phase, node_tables, edge_messages, far_messages, far_degrees, hyper_degrees, node_update,
          hyperedge_sums, far_hyperedges, hyperedge_rows, scatter_rows, far_scatter, output_rows)


def message_passing(nc, k):
    for phase in PHASES:
        taken = []

        def sem(name):
            taken.append(nc.alloc_semaphore(name=name))
            return taken[-1]

        k.sem = sem
        phase(nc, k)
        nc.clear_and_free_semaphores(taken)
        nc.all_engine_barrier()


def program(nc, dram):
    with ExitStack() as ctx:
        k = Places(dram)

        def sb(name, shape, dt=F32):
            return ctx.enter_context(nc.sbuf_tensor(name, shape, dt))

        def pair(name, shape, dt=F32, n=2):
            return [sb(f"{name}{i}", shape, dt) for i in range(n)]

        k.s_apart = ctx.enter_context(nc.semaphore('waits_taken_apart'))
        k.U = sb("sums", [P, 3 * UCOLS])
        k.stage = sb("stage", [P, 6 * NG * D + 6 * P])
        k.firsts = sb("window_starts", [P, PAIRS + BODY // 2], I32)
        k.bounds = sb("loop_bounds", [1, 5], I32)
        both = sb("table_weights_and_bias", [P, 2 * (HID + D)])
        k.w0, k.bias0 = both[:, 0:HID + D], both[:, HID + D:2 * (HID + D)]
        k.scratch = both[:, 0:GROUP * HID // 2].bitcast(BF16).rearrange("p (j d) -> p j d", d=HID)
        k.w1b = sb("edge_weights", [DE, HID])
        k.g1, k.be1 = sb("g1", [P, HID]), sb("be1", [P, HID])
        k.gu, k.beu = sb("gu", [P, D]), sb("beu", [P, D])
        k.w2u, k.b2u = sb("w2u", [P, 2 * D]), sb("b2u", [1, D])
        k.lw, k.lb = sb("lw", [P, D]), sb("lb", [P, D])
        k.ident, k.before, k.ones = sb("identity", [P, P]), sb("before", [P, P]), sb("ones", [P, P])
        k.iota, k.iotab = sb("iota", [P, P]), sb("iota_bf16", [P, P], BF16)
        k.zerob = sb("zeros_bf16", [P, P], BF16)
        k.junk = sb("spare_rows", [P, 1])
        k.neghalf = sb("minus_half", [P, NT])
        k.meta = pair("indices", [P, 2 * HALF], I32)
        k.eaA = pair("edge_features_a", [DE * len(EA_A), HALF * P], BF16)
        k.eaB = pair("edge_features_b", [DE * len(EA_B), HALF * P], BF16)
        k.wA, k.wB = (sb(f"edge_weights_{n}", [DE * len(e), HID], BF16) for n, e in (("a", EA_A), ("b", EA_B)))
        k.local, k.beyond = pair("local", [P, HALF]), pair("beyond", [P, HALF])
        k.bits, k.digits = pair("bits", [P, 2 * HALF], I32), pair("digits", [P, 3 * HALF])
        k.src_lo, k.src_hi = ([d[:, i * HALF:(i + 1) * HALF] for d in k.digits] for i in range(2))
        k.gidx, k.target = pair("hyper_index", [P, HALF], I32), pair("target", [P, HALF], I32)
        k.w_row, k.w_act = pair("w_row", [P, HALF]), pair("w_act", [P, HALF])
        k.outside = pair("outside", [P, HALF])
        k.oh = pair("window_mask", [P, HALF, WIN])
        k.lo, k.hi = pair("low_mask", [P, HALF, P], BF16), pair("high_mask", [P, HALF, NT], BF16)
        k.ones_bf = sb("ones_bf16", [P, P], BF16)
        k.ssq, k.var, k.rstd = pair("ssq", [P, HALF]), pair("var", [P, HALF]), pair("rstd", [P, HALF])
        k.beyond_count, k.dvr = sb("beyond_count", [P, NT]), sb("dvr", [P, NT])
        k.w_last, k.w_pt, k.w_de = sb("w_last", [P, 1]), sb("w_pt", [P, HT]), sb("w_de", [P, HT])
        k.nst = [both[:, i * 6 * NG:(i + 1) * 6 * NG].rearrange("p (t s) -> p t s", s=6) for i in range(2)]
        k.nmv = [both[:, (12 + 4 * i) * NG:(16 + 4 * i) * NG].rearrange("p (t s) -> p t s", s=2) for i in range(2)]
        k.nvar, k.nrs = ([both[:, (20 + 4 * n + 2 * i) * NG:(22 + 4 * n + 2 * i) * NG] for i in range(2)]
                         for n in range(2))
        k.mask_lo = [k.stage[:, i * P:(i + 1) * P] for i in range(2)]
        k.mask_hi = [k.stage[:, (2 + i) * P:(3 + i) * P] for i in range(2)]
        k.ut = [k.stage[:, 6 * NG * D + 3 * P * i:6 * NG * D + 3 * P * (i + 1)].rearrange("p (c n) -> p c n", c=3)
                for i in range(2)]

        def pb(name, cols):
            return ctx.enter_context(nc.psum_tensor(name, [P, cols], F32))

        k.psH = [pb("ps_tiles0", GROUP * HID), pb("ps_tiles1", GROUP * HID)]
        k.psA, k.psB, k.psC = pb("ps_a", 512), pb("ps_b", 512), pb("ps_c", 512)
        message_passing(nc, k)


def kernel(**inputs):
    import numpy as np
    import concourse.bacc as bacc
    from concourse.bass_utils import run_bass_kernel_spmd

    def padded(a, n, fill):
        a = np.asarray(a)
        return np.concatenate([a, np.full((n - a.shape[0],) + a.shape[1:], fill, a.dtype)])

    slots = (TILES + BODY) * P
    src = padded(inputs["src"], slots, N_NODES).reshape(-1, HALF, P)
    dst = padded(inputs["dst"], slots, FAR).reshape(-1, HALF, P)
    first = padded(np.asarray(inputs["dst"])[::2 * P], PAIRS + BODY // 2, N_NODES)
    ea = padded(inputs["edge_attr_32"], PAIRS * 2 * P, 0).reshape(PAIRS, 2 * P, DE)
    w = padded(inputs["L1_gnn_hyperedge_weight"], HP, 0)
    arrays = {
        "x": padded(inputs["x"], NP, 0),
        "meta_d": np.concatenate([src.transpose(0, 2, 1), dst.transpose(0, 2, 1)], axis=2),
        "src_d": src,
        "src_pt": src.reshape(-1, P)[:TILES].T,
        "src_tiles": src.reshape(-1, P, 1), "dst_tiles": dst.reshape(-1, P, 1),
        "dst_pt": dst.reshape(-1, P)[:TILES].T,
        "pair_first": first,
        "ea_d": ea.transpose(0, 2, 1),
        "W1": inputs["L0_gnn_W1"], "b1": inputs["L0_gnn_b1"], "g1_d": inputs["L0_gnn_g1"],
        "be1_d": inputs["L0_gnn_be1"], "W2T": np.asarray(inputs["L0_gnn_W2"]).T, "b2": inputs["L0_gnn_b2"],
        "Wu": inputs["L0_gnn_Wu"], "bu": inputs["L0_gnn_bu"], "gu_d": inputs["L0_gnn_gu"],
        "beu_d": inputs["L0_gnn_beu"], "w_d": w.reshape(HP, 1), "w_flat": w, "w_pt_d": w.reshape(HT, P).T,
        "LWT": np.asarray(inputs["L1_gnn_W"]).T, "lb_d": inputs["L1_gnn_b"],
    }
    arrays = {n: np.ascontiguousarray(a) for n, a in arrays.items()}
    nc = bacc.Bacc("TRN2", target_bir_lowering=False, num_devices=1)
    dram = {n: nc.dram_tensor(n, a.shape, mybir.dt.from_np(a.dtype), kind="ExternalInput").ap()
            for n, a in arrays.items()}
    for name, cols in (("p_tab", HID), ("hwu_tab", D), ("xh_tab", D), ("x1_tab", D), ("xp_tab", D)):
        dram[name] = nc.dram_tensor(name, (NP, cols), F32).ap()
    dram["ea_parts"] = [nc.dram_tensor(f"ea_part{n}", (PAIRS, DE, 2 * P), BF16).ap() for n in range(3)]
    dram["digit_tab"] = nc.dram_tensor("digit_tab", (P, 2 * BODIES + 2, 3 * HALF), F32).ap()
    dram["g_tab"] = nc.dram_tensor("g_tab", (HP, D), F32).ap()
    dram["acc"] = [nc.dram_tensor(f"acc{r}", (NP + P, D), F32).ap() for r in range(SCATTER_TABLES)]
    dram["out"] = nc.dram_tensor("out", (N_NODES, D), F32, kind="ExternalOutput").ap()
    program(nc, dram)
    return run_bass_kernel_spmd(nc, [arrays], core_ids=[0]).results[0]["out"]
```
